# Optimizing a Trainium2 kernel written in Bass

```python
import numpy as np
import jax
import jax.numpy as jnp

def _softmax(x, axis=-1):
    return jax.nn.softmax(x, axis=axis)

def _gelu(x):
    return jax.nn.gelu(x, approximate=True)

def _silu(x):
    return jax.nn.silu(x)

def _sigmoid(x):
    return jax.nn.sigmoid(x)

def _layernorm(x, axis=-1, eps=1e-05):
    m = jnp.mean(x, axis=axis, keepdims=True)
    v = jnp.var(x, axis=axis, keepdims=True)
    return (x - m) / jnp.sqrt(v + eps)

def _scatter_add(tgt, idx, src, axis=0):
    return tgt.at[idx].add(src)

def _segment_sum(src, seg, n):
    return jax.ops.segment_sum(src, seg, n)
kernel_name = 'mk_adaln_d1_jaxref_r8_97f226'

def setup_inputs(seed: int=0):
    np.random.seed(seed)
    _w = jnp.asarray

    def _L0_attn_setup():
        import jax, jax.numpy as jnp
        import numpy as np
        LR = 0.001

        def _mlp(params, h):
            W1, b1, W2, b2 = params
            return jax.nn.silu(h @ W1 + b1) @ W2 + b2
        key = jax.random.key(seed)
        ks = jax.random.split(key, 6)
        B, S, D = (8, 256, 128)
        sc = 1.0 / np.sqrt(D)
        x = jax.random.normal(ks[0], (B, S, D), dtype=jnp.float32)
        W_Q = jax.random.normal(ks[1], (D, D), dtype=jnp.float32) * sc
        W_KV = jax.random.normal(ks[2], (D, 2 * D), dtype=jnp.float32) * sc
        W1 = jax.random.normal(ks[3], (D, D), dtype=jnp.float32) * sc
        b1 = jnp.zeros((D,), dtype=jnp.float32)
        W2 = jax.random.normal(ks[4], (D, D), dtype=jnp.float32) * sc
        b2 = jnp.zeros((D,), dtype=jnp.float32)
        return {'x': x, 'W_Q': W_Q, 'W_KV': W_KV, 'W1': W1, 'b1': b1, 'W2': W2, 'b2': b2}
    _L0_attn_in = _L0_attn_setup()

    def _L0_ffn_setup():
        import jax, jax.numpy as jnp
        import numpy as np
        import math
        D_MODEL, D_FF, N_EXPERTS, TOP_K, N_SHARED = (128, 512, 8, 2, 1)
        B, T = (4, 128)
        SCALE = 1.0 / math.sqrt(N_SHARED + TOP_K / N_EXPERTS)
        key = jax.random.key(seed)
        ks = jax.random.split(key, 10)
        s1 = 1.0 / math.sqrt(D_MODEL)
        s2 = 1.0 / math.sqrt(D_FF)
        return {'x': jax.random.normal(ks[0], (B, T, D_MODEL), dtype=jnp.float32), 'w_router': jax.random.normal(ks[1], (N_EXPERTS, D_MODEL), dtype=jnp.float32) * s1, 'W1': jax.random.normal(ks[2], (N_EXPERTS, D_FF, D_MODEL), dtype=jnp.float32) * s1, 'b1': jax.random.normal(ks[3], (N_EXPERTS, D_FF), dtype=jnp.float32) * 0.02, 'W2': jax.random.normal(ks[4], (N_EXPERTS, D_MODEL, D_FF), dtype=jnp.float32) * s2, 'b2': jax.random.normal(ks[5], (N_EXPERTS, D_MODEL), dtype=jnp.float32) * 0.02, 'Ws1': jax.random.normal(ks[6], (D_FF, D_MODEL), dtype=jnp.float32) * s1, 'bs1': jax.random.normal(ks[7], (D_FF,), dtype=jnp.float32) * 0.02, 'Ws2': jax.random.normal(ks[8], (D_MODEL, D_FF), dtype=jnp.float32) * s2, 'bs2': jax.random.normal(ks[9], (D_MODEL,), dtype=jnp.float32) * 0.02}
    _L0_ffn_in = _L0_ffn_setup()
    _L0_c = _w((lambda *s: np.random.randn(*s).astype(np.float32) * 0.05)(4, 128))
    _L0_wmod = _w((lambda *s: np.random.randn(*s).astype(np.float32) * 0.05)(128, 6 * 128) * 128 ** (-0.5))
    _d = {'L0_attn_x': _L0_attn_in['x'], 'L0_attn_W_Q': _L0_attn_in['W_Q'], 'L0_attn_W_KV': _L0_attn_in['W_KV'], 'L0_attn_W1': _L0_attn_in['W1'], 'L0_attn_b1': _L0_attn_in['b1'], 'L0_attn_W2': _L0_attn_in['W2'], 'L0_attn_b2': _L0_attn_in['b2'], 'L0_ffn_w_router': _L0_ffn_in['w_router'], 'L0_ffn_W1': _L0_ffn_in['W1'], 'L0_ffn_b1': _L0_ffn_in['b1'], 'L0_ffn_W2': _L0_ffn_in['W2'], 'L0_ffn_b2': _L0_ffn_in['b2'], 'L0_ffn_Ws1': _L0_ffn_in['Ws1'], 'L0_ffn_bs1': _L0_ffn_in['bs1'], 'L0_ffn_Ws2': _L0_ffn_in['Ws2'], 'L0_ffn_bs2': _L0_ffn_in['bs2'], 'L0_c': _L0_c, 'L0_wmod': _L0_wmod}
    _x0 = _d['L0_attn_x']
    _d['L0_attn_x'] = jax.random.normal(jax.random.fold_in(jax.random.key(seed), 1), (4, 1024, 128), dtype=_x0.dtype)
    del _x0
    return _d

def reference(L0_attn_x, L0_attn_W_Q, L0_attn_W_KV, L0_attn_W1, L0_attn_b1, L0_attn_W2, L0_attn_b2, L0_ffn_w_router, L0_ffn_W1, L0_ffn_b1, L0_ffn_W2, L0_ffn_b2, L0_ffn_Ws1, L0_ffn_bs1, L0_ffn_Ws2, L0_ffn_bs2, L0_c, L0_wmod):

    def _L0_attn_ref(x, W_Q, W_KV, W1, b1, W2, b2):
        import jax, jax.numpy as jnp
        import numpy as np
        LR = 0.001

        def _mlp(params, h):
            W1, b1, W2, b2 = params
            return jax.nn.silu(h @ W1 + b1) @ W2 + b2
        kv = x @ W_KV
        k, v = jnp.split(kv, 2, axis=-1)
        k = jnp.swapaxes(k, 0, 1)
        v = jnp.swapaxes(v, 0, 1)

        def loss_fn(params, k_t, v_t):
            return jnp.mean((_mlp(params, k_t) - v_t) ** 2)

        def step(params, kvt):
            k_t, v_t = kvt
            g = jax.grad(loss_fn)(params, k_t, v_t)
            new_params = tuple((p - LR * gp for p, gp in zip(params, g)))
            return (new_params, None)
        params, _ = jax.lax.scan(step, (W1, b1, W2, b2), (k, v))
        q = x @ W_Q
        return _mlp(params, q)

    def _L0_ffn_ref(x, w_router, W1, b1, W2, b2, Ws1, bs1, Ws2, bs2):
        import jax, jax.numpy as jnp
        import numpy as np
        import math
        D_MODEL, D_FF, N_EXPERTS, TOP_K, N_SHARED = (128, 512, 8, 2, 1)
        B, T = (4, 128)
        SCALE = 1.0 / math.sqrt(N_SHARED + TOP_K / N_EXPERTS)
        logits = jnp.einsum('btd,ed->bte', x, w_router)
        probs = jax.nn.softmax(logits, axis=-1)
        vals, idx = jax.lax.top_k(probs, TOP_K)
        gates = jnp.sum(jax.nn.one_hot(idx, N_EXPERTS, dtype=x.dtype) * vals[..., None], axis=-2)
        hs = jax.nn.gelu(jnp.einsum('btd,fd->btf', x, Ws1) + bs1)
        acc = jnp.einsum('btf,df->btd', hs, Ws2) + bs2
        h = jax.nn.gelu(jnp.einsum('btd,efd->btef', x, W1) + b1)
        y = jnp.einsum('btef,edf->bted', h, W2) + b2
        acc = acc + jnp.einsum('bted,bte->btd', y, gates)
        return SCALE * acc
    x = L0_attn_x
    mod = (_silu(L0_c) @ L0_wmod).reshape(L0_c.shape[0], 6, 1, -1)
    sa, ca, ga, sb, cb, gb = (mod[:, 0], mod[:, 1], mod[:, 2], mod[:, 3], mod[:, 4], mod[:, 5])
    ga = (2 * (ga >= 0) - 1) * jnp.maximum(jnp.abs(ga), 0.25)
    gb = (2 * (gb >= 0) - 1) * jnp.maximum(jnp.abs(gb), 0.25)
    h = _layernorm(x, axis=-1) * (1 + ca) + sa
    x = x + ga * _L0_attn_ref(h, L0_attn_W_Q, L0_attn_W_KV, L0_attn_W1, L0_attn_b1, L0_attn_W2, L0_attn_b2)
    h = _layernorm(x, axis=-1) * (1 + cb) + sb
    x = x + gb * _L0_ffn_ref(h, L0_ffn_w_router, L0_ffn_W1, L0_ffn_b1, L0_ffn_W2, L0_ffn_b2, L0_ffn_Ws1, L0_ffn_bs1, L0_ffn_Ws2, L0_ffn_bs2)
    return x

_drawn_inputs = setup_inputs


def setup_inputs(seed=0):
    import zlib

    import numpy as np

    out = dict(_drawn_inputs(seed))
    spreads = {'L0_attn_b1': (0.0, 0.558), 'L0_attn_b2': (0.0, 0.332)}
    factors = {'L0_attn_W_KV': 8.0,
     'L0_ffn_b1': 42.401,
     'L0_ffn_b2': 28.111,
     'L0_ffn_bs1': 8.0,
     'L0_ffn_bs2': 8.0}
    for name, (base, spread) in spreads.items():
        noise = np.random.default_rng([zlib.crc32(name.encode()), seed]).standard_normal(out[name].shape)
        drawn = base * np.exp(spread * noise) if base else spread * noise
        out[name] = jnp.asarray(drawn.astype(out[name].dtype))
    for name, factor in factors.items():
        out[name] = (out[name] * factor).astype(out[name].dtype)
    return out
```

```python
from contextlib import ExitStack

import concourse.bass as bass
from concourse import mybir

ACT = mybir.ActivationFunctionType
ALU = mybir.AluOpType
F32 = mybir.dt.float32
BF16 = mybir.dt.bfloat16
I32 = mybir.dt.int32
AX_X = mybir.AxisListType.X

P = 128
B, S, D = 4, 1024, 128
STEPS = P // B
CH = S // STEPS
E, F = 8, 512
FT = F // P
GRP = 4
NG = CH // GRP
TOK = GRP * P
LR = 0.001
KAPPA = LR * 2.0 / (B * D)
SCALE = (1 + 2 / E) ** -0.5
EPS = 1e-5
N_IT = 7
N_LO = 3
TOL = 2.0 ** -12
PREP1, PREP2 = 3, 4


def program(nc, x, w_q, w_kv, w1, b1, w2, b2, w_router, e_w1, e_b1, e_w2, e_b2,
            s_w1, s_b1, s_w2, s_b2, cond, w_mod, ident_in, before_in, out):
    with ExitStack() as ctx:
        ctx.enter_context(nc.allow_non_contiguous_dma(reason="small transposed operands"))

        def sb(name, shape, dt=F32):
            return ctx.enter_context(nc.sbuf_tensor(name, shape, dt))

        def sem(name):
            return ctx.enter_context(nc.semaphore(name))

        bank = [ctx.enter_context(nc.psum_tensor(f"bank{i}", [P, 512], F32)) for i in range(8)]
        bankb = [t[:, :].bitcast(BF16) for t in bank]

        xr = sb("xr", [P, CH, D])
        hT = sb("hT", [P, CH + 1, P])
        stats = sb("stats", [P, CH, 6])
        mean = sb("mean", [P, CH])
        var = sb("var", [P, CH])
        rstd = sb("rstd", [P, CH])
        tmp = sb("tmp", [P, CH])
        mod = sb("mod", [P, 6, D])
        condT = sb("condT", [P, B])
        scT = sb("scT", [P, B])
        scB = sb("scB", [P, B, STEPS])
        wmod = sb("wmod", [P, 6 * D])
        ident = sb("ident", [P, P])
        identb = sb("identb", [P, P], BF16)
        before = sb("before", [P, P])
        mk = sb("mk", [P, P])
        mkh = sb("mkh", [P, P])
        ones = sb("ones", [P, P])
        minus = sb("minus", [P, P])
        hstage = sb("hstage", [P, 2, GRP, D])

        wq = sb("wq", [P, D])
        wkv = sb("wkv", [P, 2 * D])
        W1 = sb("W1", [P, D])
        W2 = sb("W2", [P, D])
        W2T = sb("W2T", [P, D])
        W2b = sb("W2b", [P, D], BF16)
        W2Tb = sb("W2Tb", [P, D], BF16)
        b1c = sb("b1c", [P, 1])
        b1h = sb("b1h", [P, 1])
        b2c = sb("b2c", [P, 1])

        block = lambda: nc.Block()

        s_small = sem("s_small")
        s_x = sem("s_x")
        with block() as blk:
            sc_ready = sem("sc_ready")
            mod_ready = sem("mod_ready")
            w2t_ready = sem("w2t_ready")
            setup_done = sem("setup_done")
            mod_copied = sem("mod_copied")

            @blk.sync
            def _(sp):
                for b in range(B):
                    sp.dma_start(xr[b * STEPS:(b + 1) * STEPS, :, :],
                                 x[b].rearrange("(c t) d -> t c d", t=STEPS)).then_inc(s_x, 16)

            @blk.gpsimd
            def _(pool):
                nc.gpsimd.memset(ones[:, :], 1.0)
                nc.gpsimd.memset(minus[:, :], -1.0)
                nc.gpsimd.memset(hT[:, CH, :], 0.0)

            @blk.scalar
            def _(act):
                for dst, src in ((condT[:, :], cond.rearrange("b d -> d b")), (wmod[:, :], w_mod),
                                 (ident[:, :], ident_in), (before[:, :], before_in),
                                 (wq[:, :], w_q), (wkv[:, :], w_kv), (W1[:, :], w1), (W2[:, :], w2),
                                 (b1c[:, :], b1.rearrange("(d o) -> d o", o=1)),
                                 (b2c[:, :], b2.rearrange("(d o) -> d o", o=1))):
                    act.dma_start(dst, src).then_inc(s_small, 16)
                act.wait_ge(s_small, 160)
                nc.scalar.activation(scT[:, :], condT[:, :], ACT.Silu).then_inc(sc_ready, 1)
                act.wait_ge(sc_ready, 1)
                nc.scalar.copy(scB[:, :, :], scT[:, :].unsqueeze(2).broadcast_to([P, B, STEPS])).then_inc(sc_ready, 1)

            @blk.tensor
            def _(pe):
                pe.wait_ge(sc_ready, 2)
                lhs = scB[:, :, :].rearrange("p b t -> p (b t)")
                for n in range(2):
                    pe.matmul(bank[n][:, 0:384], lhs, wmod[:, n * 384:(n + 1) * 384],
                              start=True, stop=True).then_inc(mod_ready, 1)
                pe.transpose(bank[2][:, 0:P], W2[:, :], ident[:, :]).then_inc(w2t_ready, 1)

            @blk.vector
            def _(dve):
                dve.wait_ge(s_x, 16 * B)
                with dve.Fori(0, CH) as c:
                    dve.bn_stats(stats[:, c, :], xr[:, c, :])
                dve.wait_ge(s_small, 160)
                dve.tensor_copy(identb[:, :], ident[:, :])
                dve.tensor_scalar(mk[:, :], before[:, :], -KAPPA, None, ALU.mult)
                dve.tensor_scalar(mkh[:, :], before[:, :], -KAPPA / 2, None, ALU.mult)
                dve.tensor_scalar(b1h[:, :], b1c[:, :], 0.5, None, ALU.mult)
                dve.wait_ge(mod_ready, 2)
                flat = mod[:, :, :].rearrange("p m d -> p (m d)")
                for n in range(2):
                    dve.tensor_copy(flat[:, n * 384:(n + 1) * 384], bank[n][:, 0:384]).then_inc(mod_copied, 1)
                dve.wait_ge(w2t_ready, 1)
                dve.tensor_copy(W2T[:, :], bank[2][:, 0:P]).then_inc(mod_copied, 1)
                dve.wait_ge(mod_copied, 3)
                dve.tensor_copy(W2b[:, :], W2[:, :])
                dve.tensor_copy(W2Tb[:, :], W2T[:, :])
                for n in (1, 4):
                    dve.tensor_scalar(mod[:, n, :], mod[:, n, :], 1.0, None, ALU.add).then_inc(mod_copied, 1)
                k = 5
                for n in (2, 5):
                    dve.tensor_scalar(hstage[:, 0, 0, :], mod[:, n, :], 0.0, 2.0, ALU.is_ge, ALU.mult).then_inc(mod_copied, 1)
                    dve.scalar_tensor_tensor(out=hstage[:, 0, 1, :], in0=mod[:, n, :], scalar=-1.0, in1=mod[:, n, :],
                                             op0=ALU.mult, op1=ALU.max).then_inc(mod_copied, 1)
                    k += 2
                    dve.wait_ge(mod_copied, k)
                    dve.tensor_scalar(hstage[:, 0, 1, :], hstage[:, 0, 1, :], 0.25, None, ALU.max).then_inc(mod_copied, 1)
                    k += 1
                    dve.wait_ge(mod_copied, k)
                    dve.scalar_tensor_tensor(out=mod[:, n, :], in0=hstage[:, 0, 0, :], scalar=-1.0,
                                             in1=hstage[:, 0, 1, :], op0=ALU.add, op1=ALU.mult).then_inc(mod_copied, 1)
                    k += 1
                    dve.wait_ge(mod_copied, k)

        def layer_norm(tag, scale_n, shift_n, router=None):
            with block() as blk:
                stat = sem(f"{tag}_stat")
                var_ready = sem(f"{tag}_var")
                std_ready = sem(f"{tag}_std")
                norm_ready = sem(f"{tag}_norm")
                h_ready = sem(f"{tag}_h")
                hmul = sem(f"{tag}_hmul")
                tr_ready = sem(f"{tag}_tr")
                copied = sem(f"{tag}_copied")
                if router:
                    lg_ready = sem("lg_ready")
                    lg_copied = sem("lg_copied")
                    lr_ready = sem("lr_ready")
                    lr_copied = sem("lr_copied")
                    wrT, lgT, logits = router

                @blk.vector
                def _(dve):
                    n = [0]

                    def link(ins):
                        ins.then_inc(stat, 1)
                        n[0] += 1
                        dve.wait_ge(stat, n[0])

                    me, mo = stats[:, :, 1], stats[:, :, 4]
                    link(dve.tensor_tensor(mean[:, :], me, mo, ALU.add))
                    link(dve.tensor_scalar(mean[:, :], mean[:, :], 0.5, None, ALU.mult))
                    link(dve.tensor_tensor(tmp[:, :], me, mo, ALU.subtract))
                    link(dve.tensor_tensor(tmp[:, :], tmp[:, :], tmp[:, :], ALU.mult))
                    link(dve.tensor_tensor(var[:, :], stats[:, :, 2], stats[:, :, 5], ALU.add))
                    link(dve.tensor_scalar(var[:, :], var[:, :], 1.0 / D, EPS, ALU.mult, ALU.add))
                    dve.scalar_tensor_tensor(out=var[:, :], in0=tmp[:, :], scalar=0.25, in1=var[:, :],
                                             op0=ALU.mult, op1=ALU.add).then_inc(var_ready, 1)
                    dve.wait_ge(std_ready, 1)
                    link(dve.reciprocal(rstd[:, :], tmp[:, :]))
                    link(dve.tensor_tensor(tmp[:, :], rstd[:, :], rstd[:, :], ALU.mult))
                    link(dve.tensor_tensor(tmp[:, :], tmp[:, :], var[:, :], ALU.mult))
                    link(dve.tensor_scalar(tmp[:, :], tmp[:, :], -0.5, 1.5, ALU.mult, ALU.add))
                    link(dve.tensor_tensor(rstd[:, :], rstd[:, :], tmp[:, :], ALU.mult))
                    with dve.Fori(0, NG // 2) as pair:
                        g = pair * 2
                        for k in range(2):
                            dve.wait_ge(tr_ready, g + k + 1)
                            for j in range(GRP):
                                c = (g + k) * GRP + j
                                dve.tensor_scalar(hstage[:, k, j, :], xr[:, c, :], mean[:, bass.ts(c, 1)], rstd[:, bass.ts(c, 1)],
                                                  ALU.subtract, ALU.mult).then_inc(norm_ready, 1)

                @blk.gpsimd
                def _(pool):
                    with pool.Fori(0, NG // 2) as pair:
                        g = pair * 2
                        for k in range(2):
                            pool.wait_ge(norm_ready, (g + k + 1) * GRP)
                            sc = mod[:, scale_n, :].unsqueeze(1).broadcast_to([P, GRP, D])
                            sh = mod[:, shift_n, :].unsqueeze(1).broadcast_to([P, GRP, D])
                            pool.tensor_tensor(hstage[:, k, :, :], hstage[:, k, :, :], sc, ALU.mult).then_inc(hmul, 1)
                            pool.wait_ge(hmul, g + k + 1)
                            pool.tensor_tensor(hstage[:, k, :, :], hstage[:, k, :, :], sh, ALU.add).then_inc(h_ready, 1)

                @blk.tensor
                def _(pe):
                    pe.sem_inc(tr_ready, 2)
                    with pe.Fori(0, NG // 2) as pair:
                        g = pair * 2
                        for k in range(2):
                            pe.wait_ge(h_ready, g + k + 1)
                            pe.wait_ge(copied, g + k + 1)
                            for j in range(GRP):
                                t = pe.transpose(bank[k][:, j * P:(j + 1) * P], hstage[:, k, j, :], ident[:, :])
                            t.then_inc(tr_ready, 1)
                            if router:
                                pe.wait_ge(copied, g + k + 3)
                                pe.wait_ge(lg_copied, g + k + 1)
                                pe.matmul(bank[2][0:E, :], wrT[:, :],
                                          hT[:, bass.ts(g + k, GRP), :].rearrange("p c t -> p (c t)"),
                                          start=True, stop=True).then_inc(lg_ready, 1)
                                pe.wait_ge(lg_copied, g + k + 2)
                                pe.wait_ge(lr_copied, g + k + 1)
                                for j in range(GRP):
                                    t = pe.matmul(bank[3][:, j * E:(j + 1) * E], lgT[0:E, j * P:(j + 1) * P],
                                                  ident[0:E, 0:E], start=True, stop=True)
                                t.then_inc(lr_ready, 1)

                @blk.scalar
                def _(act):
                    act.sem_inc(copied, 2)
                    if router:
                        act.sem_inc(lg_copied, 1)
                        act.sem_inc(lr_copied, 1)
                    act.wait_ge(var_ready, 1)
                    nc.scalar.activation(tmp[:, :], var[:, :], ACT.Sqrt).then_inc(std_ready, 1)
                    with act.Fori(0, NG // 2) as pair:
                        g = pair * 2
                        for k in range(2):
                            act.wait_ge(tr_ready, g + k + 3)
                            nc.scalar.copy(hT[:, bass.ts(g + k, GRP), :].rearrange("p c t -> p (c t)"),
                                           bank[k][:, :]).then_inc(copied, 1)
                            if router:
                                act.wait_ge(lg_ready, g + k + 1)
                                nc.scalar.copy(lgT[0:E, :], bank[2][0:E, :]).then_inc(lg_copied, 1)
                                act.wait_ge(lr_ready, g + k + 1)
                                nc.scalar.copy(logits[:, bass.ts(g + k, GRP), :].rearrange("p c e -> p (c e)"),
                                               bank[3][:, 0:GRP * E]).then_inc(lr_copied, 1)

        layer_norm("ln1", 1, 0)

        def lo(i):
            return i < N_LO

        kv = [sb(f"kv{i}", [P, 2 * P]) for i in range(2)]
        krow = [sb(f"krow{i}", [P, P]) for i in range(2)]
        G = [sb(f"G{i}", [P, P]) for i in range(2)]
        Gn = [sb(f"Gn{i}", [P, P]) for i in range(2)]
        Gb = [sb(f"Gb{i}", [P, P], BF16) for i in range(2)]
        Gbn = [sb(f"Gbn{i}", [P, P], BF16) for i in range(2)]
        aT = {l: sb(f"aT{l:d}", [P, P], BF16 if l else F32) for l in (False, True)}
        tT = {l: sb(f"tT{l:d}", [P, P], BF16 if l else F32) for l in (False, True)}
        eT = {l: sb(f"eT{l:d}", [P, P], BF16 if l else F32) for l in (False, True)}
        GaM = {l: sb(f"GaM{l:d}", [P, P], BF16 if l else F32) for l in (False, True)}
        GeM = {l: sb(f"GeM{l:d}", [P, P], BF16 if l else F32) for l in (False, True)}
        arow = {l: [sb(f"arow{l:d}{i}", [P, P], BF16 if l else F32) for i in range(2)] for l in (False, True)}
        erow = {l: [sb(f"erow{l:d}{i}", [P, P], BF16 if l else F32) for i in range(2)] for l in (False, True)}
        g2 = {l: [sb(f"g{l:d}{i}", [P, P], BF16 if l else F32) for i in range(2)] for l in (False, True)}
        u_sb = sb("u_sb", [P, P])
        sp_sb = sb("sp_sb", [P, P])
        chk = sb("chk", [P, 4, P])
        chd = sb("chd", [P, 4, P])
        bZ, bY, bF, bGA, bGE, bTA, bTE, bP = range(8)

        with block() as blk:
            z_ready, aT_ready, tT_ready = sem("z_ready"), sem("aT_ready"), sem("tT_ready")
            gA_ready, GaM_ready, y_ready, eT_ready = sem("gA_ready"), sem("GaM_ready"), sem("y_ready"), sem("eT_ready")
            rows_ready, arow_ready = sem("rows_ready"), sem("arow_ready")
            etr_ready, erow_ready = sem("etr_ready"), sem("erow_ready")
            u_ready, sp_ready = sem("u_ready"), sem("sp_ready")
            f_ready, g_ready, gE_ready, GeM_ready = sem("f_ready"), sem("g_ready"), sem("gE_ready"), sem("GeM_ready")
            kvp_ready, kv_ready = sem("kvp_ready"), sem("kv_ready")
            kg_ready, krow_ready, G_ready, prep_ready = sem("kg_ready"), sem("krow_ready"), sem("G_ready"), sem("prep_ready")
            U1_ready, U2_ready, W1_ready, b1_ready = sem("U1_ready"), sem("U2_ready"), sem("W1_ready"), sem("b1_ready")
            W2_ready, W2_step = sem("W2_ready"), sem("W2_step")
            chk_done, chk_step = sem("chk_done"), sem("chk_step")

            @blk.tensor
            def _(pe):
                def prep1(par, c):
                    rhs = hT[:, c, :]
                    pe.matmul(bank[bP][:, 0:P], wkv[:, 0:D], rhs, start=True, stop=True)
                    pe.matmul(bank[bP][:, P:2 * P], wkv[:, D:2 * D], rhs, start=True, stop=True).then_inc(kvp_ready, 1)

                def prep2(par, c):
                    pe.wait_ge(kv_ready, c + 1)
                    kT = kv[par][:, 0:P]
                    pe.transpose(bank[bP][:, 2 * P:3 * P], kT, ident[:, :])
                    pe.matmul(bank[bP][:, 3 * P:4 * P], kT, kT, start=True, stop=True).then_inc(kg_ready, 1)

                def chunk(par, c):
                    N1 = N_IT - 1
                    pe.wait_ge(prep_ready, c + 1)
                    pe.wait_ge(W1_ready, c + 1)
                    pe.matmul(bank[bZ][:, 0:P], W1[:, :], kv[par][:, 0:P], start=True, stop=False,
                              skip_group_check=True).then_inc(z_ready, 1)
                    for i in range(N_IT):
                        l, lp = lo(i), lo(i - 1)
                        tr = bankb if l else bank
                        idn = (identb if l else ident)[:, :]
                        pe.wait_ge(aT_ready, c * N_IT + i + 1)
                        if i == 0:
                            pe.wait_ge(W2_ready, c + 1)
                        if i:
                            pe.matmul(bank[bGA][:, 0:P], aT[l][:, :], aT[l][:, :], start=True, stop=True).then_inc(gA_ready, 1)
                        mm = pe.matmul(bank[bY][:, 0:P], (W2b if l else W2)[:, :], aT[l][:, :], start=True, stop=(i == 0),
                                       skip_group_check=True)
                        if i == 0:
                            mm.then_inc(y_ready, 1)
                        pe.wait_ge(tT_ready, c * N_IT + i + 1)
                        pe.transpose(tr[bTA][:, 0:P], aT[l][:, :], idn)
                        pe.transpose(tr[bTA][:, P:2 * P], tT[l][:, :], idn).then_inc(rows_ready, 1)
                        if i:
                            pe.wait_ge(erow_ready, c * N_IT + i)
                            pe.wait_ge(GaM_ready, c * N1 + i)
                            pe.matmul(bank[bY][:, 0:P], erow[l][(i - 1) % 2][:, :], GaM[l][:, :], start=False, stop=True,
                                      skip_group_check=True).then_inc(y_ready, 1)
                            pe.wait_ge(GeM_ready, c * N1 + i)
                            pe.matmul(bank[bF][:, 0:P], GeM[l][:, :], arow[l][(i - 1) % 2][:, :], start=True, stop=False,
                                      skip_group_check=True)
                        if 1 <= i < N1:
                            pe.matmul(bank[bZ][:, 0:P], g2[lp][(i - 1) % 2][:, :], (Gbn if lp else Gn)[par][:, :],
                                      start=False, stop=False, skip_group_check=True)
                        pe.wait_ge(eT_ready, c * N_IT + i + 1)
                        pe.matmul(bank[bF][:, 0:P], eT[l][:, :], (W2Tb if l else W2T)[:, :], start=(i == 0), stop=True,
                                  skip_group_check=True).then_inc(f_ready, 1)
                        if i < N1:
                            pe.matmul(bank[bGE][:, 0:P], eT[l][:, :], eT[l][:, :], start=True, stop=True).then_inc(gE_ready, 1)
                        pe.transpose(tr[bTE][:, 0:P], eT[l][:, :], idn).then_inc(etr_ready, 1)
                        if i == PREP1:
                            prep1(1 - par, c + 1)
                        if i == PREP2:
                            prep2(1 - par, c + 1)
                        if i < N1:
                            pe.wait_ge(g_ready, c * N_IT + i + 1)
                            pe.matmul(bank[bZ][:, 0:P], g2[l][i % 2][:, :], (Gb if l else G)[par][:, :],
                                      start=False, stop=False, skip_group_check=True).then_inc(z_ready, 1)
                    last = N1 % 2
                    gl, al, el = g2[False][last][:, :], arow[False][last][:, :], erow[False][last][:, :]
                    pe.wait_ge(prep_ready, c + 2)
                    pe.wait_ge(g_ready, (c + 1) * N_IT)
                    pe.matmul(bank[bP][:, 0:P], krow[par][:, :], gl, start=True, stop=True)
                    pe.matmul(bank[bP][:, P:P + 1], gl, ones[:, 0:1], start=True, stop=True).then_inc(U1_ready, 1)
                    pe.wait_ge(erow_ready, (c + 1) * N_IT)
                    pe.matmul(bank[bGA][:, 0:P], al, el, start=True, stop=True)
                    pe.matmul(bank[bGA][:, P:2 * P], el, al, start=True, stop=True)
                    pe.matmul(bank[bGA][:, 2 * P:2 * P + 1], el, ones[:, 0:1], start=True, stop=True).then_inc(U2_ready, 1)

                prep1(0, 0)
                prep2(0, 0)
                with pe.Fori(0, CH // 2) as pair:
                    c = pair * 2
                    chunk(0, c)
                    chunk(1, c + 1)

            @blk.scalar
            def _(act):
                def prep1(par, c):
                    act.wait_ge(kvp_ready, c + 1)
                    nc.scalar.copy(kv[par][:, :], bank[bP][:, 0:2 * P]).then_inc(kv_ready, 1)

                def prep2(par, c):
                    act.wait_ge(kg_ready, c + 1)
                    nc.scalar.copy(krow[par][:, :], bank[bP][:, 2 * P:3 * P]).then_inc(krow_ready, 1)

                def chunk(par, c):
                    act.wait_ge(b1_ready, c + 1)
                    for i in range(N_IT):
                        l, ln = lo(i), lo(i + 1)
                        act.wait_ge(z_ready, c * N_IT + i + 1)
                        nc.scalar.activation(aT[l][:, :], bank[bZ][:, 0:P], ACT.Silu, bias=b1c[:, 0:1]).then_inc(aT_ready, 1)
                        nc.scalar.activation(tT[l][:, :], bank[bZ][:, 0:P], ACT.Tanh, bias=b1h[:, 0:1],
                                             scale=0.5).then_inc(tT_ready, 1)
                        if i == N_LO - 1:
                            act.wait_ge(chk_done, c + 1)
                        act.wait_ge(rows_ready, c * N_IT + i + 1)
                        tr = bankb if l else bank
                        nc.scalar.copy(arow[ln][i % 2][:, :], tr[bTA][:, 0:P]).then_inc(arow_ready, 1)
                        act.wait_ge(etr_ready, c * N_IT + i + 1)
                        nc.scalar.copy(erow[ln][i % 2][:, :], tr[bTE][:, 0:P]).then_inc(erow_ready, 1)
                        if i == PREP1:
                            prep1(1 - par, c + 1)
                        if i == PREP2:
                            prep2(1 - par, c + 1)

                nc.scalar.preload_act_table_set("silu_and_others")
                prep1(0, 0)
                prep2(0, 0)
                with act.Fori(0, CH // 2) as pair:
                    c = pair * 2
                    chunk(0, c)
                    chunk(1, c + 1)

            @blk.vector
            def _(dve):
                def prep(par, c):
                    dve.wait_ge(krow_ready, c + 1)
                    dve.scalar_tensor_tensor(out=G[par][:, :], in0=bank[bP][:, 3 * P:4 * P], scalar=1.0, in1=mkh[:, :],
                                             op0=ALU.add, op1=ALU.mult).then_inc(G_ready, 1)

                def chunk(par, c):
                    N1 = N_IT - 1
                    for i in range(N_IT):
                        l, ln = lo(i), lo(i + 1)
                        tr = bankb if l else bank
                        if i:
                            dve.wait_ge(gA_ready, c * N1 + i)
                            dve.scalar_tensor_tensor(out=GaM[l][:, :], in0=bank[bGA][:, 0:P], scalar=1.0, in1=mk[:, :],
                                                     op0=ALU.add, op1=ALU.mult).then_inc(GaM_ready, 1)
                        dve.wait_ge(y_ready, c * N_IT + i + 1)
                        dve.scalar_tensor_tensor(out=eT[l][:, :], in0=bank[bY][:, 0:P], scalar=b2c[:, 0:1],
                                                 in1=kv[par][:, P:2 * P], op0=ALU.add, op1=ALU.subtract).then_inc(eT_ready, 1)
                        dve.wait_ge(arow_ready, c * N_IT + i + 1)
                        ar = arow[ln][i % 2][:, :]
                        dve.scalar_tensor_tensor(out=u_sb[:, :], in0=ar, scalar=-1.0, in1=tr[bTA][:, P:2 * P],
                                                 op0=ALU.add, op1=ALU.mult).then_inc(u_ready, 1)
                        dve.wait_ge(u_ready, c * N_IT + i + 1)
                        dve.scalar_tensor_tensor(out=sp_sb[:, :], in0=ar, scalar=1.0, in1=u_sb[:, :],
                                                 op0=ALU.add, op1=ALU.subtract).then_inc(sp_ready, 1)
                        dve.wait_ge(sp_ready, c * N_IT + i + 1)
                        if i == N_LO:
                            dve.wait_ge(chk_done, c + 1)
                        dve.wait_ge(f_ready, c * N_IT + i + 1)
                        dve.tensor_tensor(g2[l][i % 2][:, :], bank[bF][:, 0:P], sp_sb[:, :], ALU.mult).then_inc(g_ready, 1)
                        if i < N1:
                            dve.wait_ge(gE_ready, c * N1 + i + 1)
                            dve.tensor_tensor(GeM[ln][:, :], bank[bGE][:, 0:P], mk[:, :], ALU.mult).then_inc(GeM_ready, 1)
                        if i == PREP2:
                            prep(1 - par, c + 1)
                    dve.wait_ge(U1_ready, c + 1)
                    upd = lambda w, u, s=-KAPPA: dve.scalar_tensor_tensor(out=w, in0=u, scalar=s, in1=w,
                                                                         op0=ALU.mult, op1=ALU.add)
                    upd(W1[:, :], bank[bP][:, 0:P], -KAPPA / 2).then_inc(W1_ready, 1)
                    upd(b1c[:, :], bank[bP][:, P:P + 1], -KAPPA / 2)
                    upd(b1h[:, :], bank[bP][:, P:P + 1], -KAPPA / 4).then_inc(b1_ready, 1)
                    dve.wait_ge(U2_ready, c + 1)
                    upd(W2[:, :], bank[bGA][:, 0:P]).then_inc(W2_step, 1)
                    upd(W2T[:, :], bank[bGA][:, P:2 * P]).then_inc(W2_step, 1)
                    upd(b2c[:, :], bank[bGA][:, 2 * P:2 * P + 1]).then_inc(W2_step, 1)
                    dve.wait_ge(W2_step, c * 3 + 3)
                    dve.tensor_copy(W2b[:, :], W2[:, :])
                    dve.tensor_copy(W2Tb[:, :], W2T[:, :]).then_inc(W2_ready, 1)

                prep(0, 0)
                for s_first in (W1_ready, b1_ready, W2_ready):
                    dve.sem_inc(s_first, 1)
                with dve.Fori(0, CH // 2) as pair:
                    c = pair * 2
                    chunk(0, c)
                    chunk(1, c + 1)

            @blk.gpsimd
            def _(pool):
                nc.gpsimd.memset(chk[:, :, :], 0.0).then_inc(chk_step, 1)
                pool.wait_ge(chk_step, 1)
                pool.sem_inc(chk_done, 1)

                def prep(par, c):
                    pool.wait_ge(G_ready, c + 1)
                    pool.tensor_tensor(Gn[par][:, :], G[par][:, :], minus[:, :], ALU.mult)
                    pool.tensor_copy(Gb[par][:, :], G[par][:, :])
                    pool.tensor_scalar(Gbn[par][:, :], G[par][:, :], -1.0, None, ALU.mult).then_inc(prep_ready, 1)

                def chunk(par, c):
                    prep(1 - par, c + 1)
                    a, b = (N_IT - 1) % 2, N_IT % 2
                    pool.wait_ge(chk_step, c * 6 + 1)
                    pool.wait_ge(g_ready, (c + 1) * N_IT)
                    pool.tensor_tensor(chd[:, 0, :], g2[False][a][:, :], g2[False][b][:, :], ALU.subtract).then_inc(chk_step, 1)
                    pool.tensor_tensor(chd[:, 1, :], g2[False][a][:, :], g2[False][a][:, :], ALU.mult).then_inc(chk_step, 1)
                    pool.wait_ge(erow_ready, (c + 1) * N_IT)
                    pool.tensor_tensor(chd[:, 2, :], erow[False][a][:, :], erow[False][b][:, :], ALU.subtract).then_inc(chk_step, 1)
                    pool.tensor_tensor(chd[:, 3, :], erow[False][a][:, :], erow[False][a][:, :], ALU.mult).then_inc(chk_done, 1)
                    pool.wait_ge(chk_step, c * 6 + 4)
                    pool.tensor_tensor(chd[:, 0, :], chd[:, 0, :], chd[:, 0, :], ALU.mult).then_inc(chk_step, 1)
                    pool.tensor_tensor(chd[:, 2, :], chd[:, 2, :], chd[:, 2, :], ALU.mult).then_inc(chk_step, 1)
                    pool.wait_ge(chk_step, c * 6 + 6)
                    pool.wait_ge(chk_done, c + 2)
                    flat = chk[:, :, :].rearrange("p a b -> p (a b)")
                    pool.tensor_tensor(flat, flat, chd[:, :, :].rearrange("p a b -> p (a b)"), ALU.add).then_inc(chk_step, 1)

                prep(0, 0)
                with pool.Fori(0, CH // 2) as pair:
                    c = pair * 2
                    chunk(0, c)
                    chunk(1, c + 1)

        sums = sb("sums", [P, 4])
        holds = sb("holds", [P, 4])
        count = sb("count", [1, 1], I32)
        with block() as blk:
            sums_ready, holds_step, total_ready, count_ready = sem("sums_ready"), sem("holds_step"), sem("total_ready"), sem("count_ready")

            @blk.vector
            def _(dve):
                dve.tensor_reduce(sums[:, :], chk[:, :, :], AX_X, ALU.add).then_inc(sums_ready, 1)
                dve.wait_ge(sums_ready, 1)
                for n in range(2):
                    dve.scalar_tensor_tensor(out=holds[:, 2 * n:2 * n + 1], in0=sums[:, 2 * n + 1:2 * n + 2], scalar=TOL * TOL,
                                             in1=sums[:, 2 * n:2 * n + 1], op0=ALU.mult, op1=ALU.is_ge).then_inc(holds_step, 1)
                    dve.tensor_scalar(holds[:, 2 * n + 1:2 * n + 2], sums[:, 2 * n + 1:2 * n + 2], 3e38, None,
                                      ALU.is_le).then_inc(holds_step, 1)
                dve.wait_ge(total_ready, 1)
                dve.tensor_reduce(holds[0:1, 0:1], bank[0][0:1, 0:4], AX_X, ALU.add).then_inc(holds_step, 1)
                dve.wait_ge(holds_step, 5)
                dve.tensor_copy(count[:, :], holds[0:1, 0:1]).then_inc(count_ready, 1)

            @blk.tensor
            def _(pe):
                pe.wait_ge(holds_step, 4)
                pe.matmul(bank[0][0:1, 0:4], ones[:, 0:1], holds[:, :], start=True, stop=True).then_inc(total_ready, 1)

        k4 = sb("k4", [P, 2 * B])
        a4, t4, u4, sp4, e4, g4 = (sb(n, [P, B]) for n in ("a4", "t4", "u4", "sp4", "e4", "g4"))
        gs, es = sb("gs", [P, 1]), sb("es", [P, 1])
        rows4 = sb("rows4", [B, 4, P])
        with block() as blk:
            s_again, w2t_again, w2t_copied = sem("s_again"), sem("w2t_again"), sem("w2t_copied")
            k_step, kc_step, z_step, a_step, t_step = (sem(f"{n}_step") for n in ("k", "kc", "z", "a", "t"))
            y_step, e_step, u_step, sp_step, f_step = (sem(f"{n}_step") for n in ("y", "e", "u", "sp", "f"))
            g_step, r_step, rc_step, U_step, s_step = (sem(f"{n}_step") for n in ("g", "r", "rc", "U", "s"))
            w_step = sem("w_step")

            def holding(eng):
                return eng.value_load(count[0:1, 0:1], min_val=0, max_val=4 * P)

            def steps(eng, body):
                with eng.Fori(0, CH) as c:
                    with eng.Fori(0, STEPS) as j:
                        body(c, j, c * STEPS + j)

            @blk.sync
            def _(sp):
                with sp.If(holding(sp) < 4 * P):
                    for dst, src in ((W1[:, :], w1), (W2[:, :], w2), (b1c[:, :], b1.rearrange("(d o) -> d o", o=1)),
                                     (b2c[:, :], b2.rearrange("(d o) -> d o", o=1))):
                        sp.dma_start(dst, src).then_inc(s_again, 16)

            @blk.tensor
            def _(pe):
                with pe.If(holding(pe) < 4 * P):
                    pe.wait_ge(s_again, 64)
                    pe.transpose(bank[0][:, 0:P], W2[:, :], ident[:, :]).then_inc(w2t_again, 1)

                    def step(c, j, n):
                        h4 = hT[:, c, :].rearrange("p (b t) -> p t b", t=STEPS)[:, j, :]
                        pe.wait_ge(w_step, n * 6 + 6)
                        pe.matmul(bank[0][:, 0:B], wkv[:, 0:D], h4, start=True, stop=True)
                        pe.matmul(bank[0][:, B:2 * B], wkv[:, D:2 * D], h4, start=True, stop=True).then_inc(k_step, 1)
                        pe.wait_ge(kc_step, n + 1)
                        pe.matmul(bank[1][:, 0:B], W1[:, :], k4[:, 0:B], start=True, stop=True).then_inc(z_step, 1)
                        pe.wait_ge(a_step, n + 1)
                        pe.matmul(bank[2][:, 0:B], W2[:, :], a4[:, :], start=True, stop=True).then_inc(y_step, 1)
                        pe.wait_ge(e_step, n + 1)
                        pe.matmul(bank[3][:, 0:B], W2T[:, :], e4[:, :], start=True, stop=True).then_inc(f_step, 1)
                        pe.wait_ge(g_step, n + 1)
                        for m, src in enumerate((k4[:, 0:B], a4[:, :], e4[:, :], g4[:, :])):
                            t = pe.transpose(bank[4][0:B, m * P:(m + 1) * P], src, ident[:, :])
                        t.then_inc(r_step, 1)
                        pe.wait_ge(rc_step, n + 1)
                        kr, ar, er, gr = (rows4[:, m, :] for m in range(4))
                        pe.matmul(bank[5][:, 0:P], kr, gr, start=True, stop=True)
                        pe.matmul(bank[5][:, P:2 * P], ar, er, start=True, stop=True)
                        pe.matmul(bank[5][:, 2 * P:3 * P], er, ar, start=True, stop=True).then_inc(U_step, 1)
                    steps(pe, step)

            @blk.scalar
            def _(act):
                with act.If(holding(act) < 4 * P):
                    def step(c, j, n):
                        act.wait_ge(k_step, n + 1)
                        nc.scalar.copy(k4[:, :], bank[0][:, 0:2 * B]).then_inc(kc_step, 1)
                        act.wait_ge(z_step, n + 1)
                        nc.scalar.activation(a4[:, :], bank[1][:, 0:B], ACT.Silu, bias=b1c[:, 0:1]).then_inc(a_step, 1)
                        nc.scalar.activation(t4[:, :], bank[1][:, 0:B], ACT.Tanh, bias=b1h[:, 0:1],
                                             scale=0.5).then_inc(t_step, 1)
                    steps(act, step)

            @blk.vector
            def _(dve):
                with dve.If(holding(dve) < 4 * P):
                    dve.wait_ge(w2t_again, 1)
                    dve.tensor_copy(W2T[:, :], bank[0][:, 0:P]).then_inc(w2t_copied, 1)
                    dve.tensor_scalar(b1h[:, :], b1c[:, :], 0.5, None, ALU.mult).then_inc(w2t_copied, 1)
                    dve.wait_ge(w2t_copied, 2)
                    dve.sem_inc(w_step, 6)

                    def step(c, j, n):
                        dve.wait_ge(y_step, n + 1)
                        dve.scalar_tensor_tensor(out=e4[:, :], in0=bank[2][:, 0:B], scalar=b2c[:, 0:1], in1=k4[:, B:2 * B],
                                                 op0=ALU.add, op1=ALU.subtract).then_inc(e_step, 1)
                        dve.wait_ge(t_step, n + 1)
                        dve.scalar_tensor_tensor(out=u4[:, :], in0=a4[:, :], scalar=-1.0, in1=t4[:, :],
                                                 op0=ALU.add, op1=ALU.mult).then_inc(u_step, 1)
                        dve.wait_ge(u_step, n + 1)
                        dve.scalar_tensor_tensor(out=sp4[:, :], in0=a4[:, :], scalar=1.0, in1=u4[:, :],
                                                 op0=ALU.add, op1=ALU.subtract).then_inc(sp_step, 1)
                        dve.wait_ge(sp_step, n + 1)
                        dve.wait_ge(f_step, n + 1)
                        dve.tensor_tensor(g4[:, :], bank[3][:, 0:B], sp4[:, :], ALU.mult).then_inc(g_step, 1)
                        dve.wait_ge(r_step, n + 1)
                        dve.tensor_copy(rows4[:, :, :].rearrange("b m d -> b (m d)"), bank[4][0:B, :]).then_inc(rc_step, 1)
                        dve.wait_ge(g_step, n + 1)
                        dve.tensor_reduce(gs[:, :], g4[:, :], AX_X, ALU.add).then_inc(s_step, 1)
                        dve.tensor_reduce(es[:, :], e4[:, :], AX_X, ALU.add).then_inc(s_step, 1)
                        dve.wait_ge(s_step, n * 2 + 2)
                        dve.wait_ge(U_step, n + 1)
                        for w, u, r in ((W1[:, :], bank[5][:, 0:P], -KAPPA / 2), (W2[:, :], bank[5][:, P:2 * P], -KAPPA),
                                        (W2T[:, :], bank[5][:, 2 * P:3 * P], -KAPPA), (b1c[:, :], gs[:, :], -KAPPA / 2),
                                        (b1h[:, :], gs[:, :], -KAPPA / 4), (b2c[:, :], es[:, :], -KAPPA)):
                            dve.scalar_tensor_tensor(out=w, in0=u, scalar=r, in1=w, op0=ALU.mult,
                                                     op1=ALU.add).then_inc(w_step, 1)
                        dve.wait_ge(w_step, n * 6 + 12)
                    steps(dve, step)


        qT = [sb(f"qT{i}", [P, TOK]) for i in range(2)]
        qa = [sb(f"qa{i}", [P, TOK]) for i in range(2)]
        t1 = [sb(f"t1{i}", [P, GRP, D]) for i in range(2)]
        gab = sb("gab", [P, D])
        with block() as blk:
            d_ready, b_ready, gab_ready = sem("d_ready"), sem("b_ready"), sem("gab_ready")
            q_ready, q_copied = sem("q_ready"), sem("q_copied")
            qz_ready, qa_ready = sem("qz_ready"), sem("qa_ready")
            o_ready, o_used, xg_ready, x1_ready = sem("o_ready"), sem("o_used"), sem("xg_ready"), sem("x1_ready")

            @blk.tensor
            def _(pe):
                pe.wait_ge(d_ready, 1)
                pe.matmul(bank[6][:, 0:D], ones[:, :], u_sb[:, :], start=True, stop=True).then_inc(b_ready, 1)
                with pe.Fori(0, NG // 2) as pair:
                    g = pair * 2
                    for k in range(2):
                        pe.wait_ge(q_copied, g + k + 1)
                        pe.matmul(bank[k][:, :], wq[:, :], hT[:, bass.ts(g + k, GRP), :].rearrange("p c t -> p (c t)"),
                                  start=True, stop=True).then_inc(q_ready, 1)
                        pe.wait_ge(q_copied, g + k + 2)
                        pe.wait_ge(qa_ready, g + k + 1)
                        pe.matmul(bank[2 + k][:, :], W1[:, :], qT[k][:, :], start=True, stop=True).then_inc(qz_ready, 1)
                        pe.wait_ge(qa_ready, g + k + 2)
                        pe.wait_ge(o_used, g + k + 1)
                        for j in range(GRP):
                            mm = pe.matmul(bank[4 + k][:, j * P:(j + 1) * P], qa[k][:, j * P:(j + 1) * P], W2[:, :],
                                           start=True, stop=True)
                        mm.then_inc(o_ready, 1)

            @blk.scalar
            def _(act):
                nc.scalar.preload_act_table_set("silu_and_others")
                act.sem_inc(q_copied, 1)
                act.sem_inc(qa_ready, 1)
                with act.Fori(0, NG // 2) as pair:
                    g = pair * 2
                    for k in range(2):
                        act.wait_ge(q_ready, g + k + 1)
                        nc.scalar.copy(qT[k][:, :], bank[k][:, :]).then_inc(q_copied, 1)
                        act.wait_ge(qz_ready, g + k + 1)
                        nc.scalar.activation(qa[k][:, :], bank[2 + k][:, :], ACT.Silu, bias=b1c[:, 0:1]).then_inc(qa_ready, 1)

            @blk.vector
            def _(dve):
                dve.tensor_scalar(u_sb[:, :], ident[:, :], b2c[:, 0:1], None, ALU.mult).then_inc(d_ready, 1)
                dve.sem_inc(o_used, 1)
                dve.wait_ge(b_ready, 1)
                dve.tensor_tensor(gab[:, :], bank[6][:, 0:D], mod[:, 2, :], ALU.mult).then_inc(gab_ready, 1)
                with dve.Fori(0, NG // 2) as pair:
                    g = pair * 2
                    for k in range(2):
                        dve.wait_ge(o_ready, g + k + 1)
                        dve.tensor_tensor(t1[k][:, :, :], bank[4 + k][:, :].rearrange("p (c d) -> p c d", c=GRP),
                                          mod[:, 2, :].unsqueeze(1).broadcast_to([P, GRP, D]), ALU.mult).then_inc(o_used, 1)
                        dve.wait_ge(o_used, g + k + 2)
                        dve.wait_ge(xg_ready, g + k + 1)
                        xs = xr[:, bass.ts(g + k, GRP), :]
                        dve.tensor_tensor(xs, t1[k][:, :, :], xs, ALU.add).then_inc(x1_ready, 1)
                        dve.wait_ge(x1_ready, g + k + 1)
                        for j in range(GRP):
                            c = (g + k) * GRP + j
                            dve.bn_stats(stats[:, c, :], xr[:, c, :])

            @blk.gpsimd
            def _(pool):
                pool.wait_ge(gab_ready, 1)
                with pool.Fori(0, NG) as g:
                    xs = xr[:, bass.ts(g, GRP), :]
                    pool.tensor_tensor(xs, xs, gab[:, :].unsqueeze(1).broadcast_to([P, GRP, D]), ALU.add).then_inc(xg_ready, 1)

        wrT = sb("wrT", [P, E])
        lgT = sb("lgT", [E, TOK])
        logits = sb("logits", [P, CH, E])
        gates = sb("gates", [P, CH, E])
        gtmp = sb("gtmp", [P, CH, E])
        rank = sb("rank", [P, CH, E])
        cmp = sb("cmp", [P, CH, E, E])
        red = sb("red", [P, CH])
        b2blk = sb("b2blk", [GRP * E, GRP, D])
        bs2 = sb("bs2", [P, D])
        w1n = sb("w1n", [P, 2, FT, D])
        w2n = sb("w2n", [P, 2, F])
        w1T = sb("w1T", [P, E + 1, FT, P])
        w2T = sb("w2T", [P, E + 1, FT, D])
        eb1 = sb("eb1", [P, E + 1, FT])
        with block() as blk:
            s_w, s_b = [sem(f"s_w{i}") for i in range(2)], sem("s_b")
            wt_ready, wt_copied, z_b2 = sem("wt_ready"), sem("wt_copied"), sem("z_b2")

            @blk.gpsimd
            def _(pool):
                nc.gpsimd.memset(b2blk[:, :, :], 0.0).then_inc(z_b2, 1)

            @blk.sync
            def _(sp):
                sp.dma_start(wrT[:, :], w_router.rearrange("e d -> d e")).then_inc(s_b, 16)
                for e in range(E + 1):
                    src = e_b1[e] if e < E else s_b1
                    sp.dma_start(eb1[:, e, :], src.rearrange("(n p) -> p n", p=P)).then_inc(s_b, 16)
                sp.dma_start(bs2[:, :], s_b2.rearrange("(o d) -> o d", o=1).broadcast_to([P, D])).then_inc(s_b, 16)
                sp.wait_ge(z_b2, 1)
                for j in range(GRP):
                    sp.dma_start(b2blk[j * E:(j + 1) * E, j, :], e_b2).then_inc(s_b, 16)
                for e in range(E + 1):
                    w1s, w2s = (e_w1[e], e_w2[e]) if e < E else (s_w1, s_w2)
                    if e >= 2:
                        sp.wait_ge(wt_ready, 2 * (e - 1))
                    sp.dma_start(w1n[:, e % 2, :, :], w1s.rearrange("(n p) d -> p n d", p=P)).then_inc(s_w[e % 2], 16)
                    sp.dma_start(w2n[:, e % 2, :], w2s).then_inc(s_w[e % 2], 16)
                sp.wait_ge(s_b, 16 * (E + 7))

            @blk.tensor
            def _(pe):
                for e in range(E + 1):
                    pe.wait_ge(s_w[e % 2], 32 * (e // 2 + 1))
                    for m in range(2):
                        if e:
                            pe.wait_ge(wt_copied, 2 * e - 1 + m)
                        for n in range(FT):
                            src = w2n[:, e % 2, n * P:(n + 1) * P] if m else w1n[:, e % 2, n, :]
                            t = pe.transpose(bank[m][:, n * P:(n + 1) * P], src, ident[:, :])
                        t.then_inc(wt_ready, 1)

            @blk.vector
            def _(dve):
                for e in range(E + 1):
                    for m, dst in enumerate((w1T, w2T)):
                        dve.wait_ge(wt_ready, 2 * e + m + 1)
                        dve.tensor_copy(dst[:, e, :, :].rearrange("p n d -> p (n d)"), bank[m][:, :]).then_inc(wt_copied, 1)

        layer_norm("ln2", 4, 3, router=(wrT, lgT, logits))

        with block() as blk:
            step, ex_ready = sem("gate_step"), sem("ex_ready")

            @blk.scalar
            def _(act):
                act.wait_ge(step, 2)
                nc.scalar.activation(gates[:, :, :], gtmp[:, :, :], ACT.Exp).then_inc(ex_ready, 1)

            @blk.vector
            def _(dve):
                n = [0]

                def link(ins):
                    ins.then_inc(step, 1)
                    n[0] += 1
                    dve.wait_ge(step, n[0])

                bc = lambda t: t.unsqueeze(2).broadcast_to([P, CH, E])
                link(dve.tensor_reduce(red[:, :], logits[:, :, :], AX_X, ALU.max))
                link(dve.tensor_tensor(gtmp[:, :, :], logits[:, :, :], bc(red[:, :]), ALU.subtract))
                mine = logits[:, :, :].unsqueeze(3).broadcast_to([P, CH, E, E])
                other = logits[:, :, :].unsqueeze(2).broadcast_to([P, CH, E, E])
                link(dve.tensor_tensor(cmp[:, :, :, :], other, mine, ALU.is_gt))
                for e in range(1, E):
                    link(dve.tensor_tensor(cmp[:, :, e, 0:e], other[:, :, e, 0:e], mine[:, :, e, 0:e], ALU.is_ge))
                link(dve.tensor_reduce(rank[:, :, :], cmp[:, :, :, :], AX_X, ALU.add))
                dve.wait_ge(ex_ready, 1)
                link(dve.tensor_reduce(red[:, :], gates[:, :, :], AX_X, ALU.add))
                link(dve.reciprocal(red[:, :], red[:, :]))
                link(dve.tensor_tensor(gates[:, :, :], gates[:, :, :], bc(red[:, :]), ALU.mult))
                link(dve.scalar_tensor_tensor(out=gates[:, :, :], in0=rank[:, :, :], scalar=1.5, in1=gates[:, :, :],
                                              op0=ALU.is_lt, op1=ALU.mult))
                link(dve.tensor_scalar(mod[:, 5, :], mod[:, 5, :], SCALE, None, ALU.mult))

        hh = [sb(f"hh{i}", [P, FT, TOK]) for i in range(2)]
        acc = [sb(f"acc{i}", [P, GRP, D]) for i in range(2)]
        gst = sb("gst", [P, GRP, E])
        gT = sb("gT", [GRP * E, P])
        N_E = E + 1
        with block() as blk:
            gst_ready, gt_ready, gT_ready, bias_ready = sem("gst_ready"), sem("gt_ready"), sem("gT_ready"), sem("bias_ready")
            u_rdy, h_rdy = sem("up_ready"), sem("hid_ready")
            y_rdy, y_used = sem("down_ready"), sem("down_used")
            acc_step, fin_step, fin_ready = sem("acc_step"), sem("fin_step"), sem("fin_ready")
            s_out = sem("s_out")
            HB, YB = (0, 1, 2, 3), (4, 5)
            out_v = [out[b].rearrange("(c t) d -> t c d", t=STEPS) for b in range(B)]

            @blk.tensor
            def _(pe):
                def group(g, par):
                    hg = hT[:, bass.ts(g, GRP), :].rearrange("p c t -> p (c t)")

                    def up(e):
                        for n in range(FT):
                            if e:
                                pe.wait_ge(h_rdy, (g * N_E + e - 1) * FT + n + 1)
                            pe.matmul(bank[HB[n]][:, :], w1T[:, e, n, :], hg, start=True, stop=True).then_inc(u_rdy, 1)

                    def down(e):
                        pe.wait_ge(h_rdy, (g * N_E + e + 1) * FT)
                        pe.wait_ge(y_used, g * N_E + max(e - 1, 0) + 1)
                        for j in range(GRP):
                            for n in range(FT):
                                mm = pe.matmul(bank[YB[e % 2]][:, j * P:(j + 1) * P], hh[e % 2][:, n, j * P:(j + 1) * P],
                                               w2T[:, e, n, :], start=(n == 0), stop=(n == FT - 1))
                        mm.then_inc(y_rdy, 1)

                    pe.wait_ge(gst_ready, g + 1)
                    pe.transpose(bank[6][0:GRP * E, 0:P], gst[:, :, :].rearrange("p c e -> p (c e)"), ident[:, :]).then_inc(gt_ready, 1)
                    return up, down

                def body(g):
                    up, down = group(g, 0)
                    up(0)
                    pe.wait_ge(gT_ready, g + 2)
                    pe.matmul(bank[7][:, :], gT[:, :], b2blk[:, :, :].rearrange("p c d -> p (c d)"),
                              start=True, stop=True).then_inc(bias_ready, 1)
                    for e in range(1, N_E):
                        up(e)
                        down(e - 1)
                    down(N_E - 1)

                pe.sem_inc(y_rdy, 1)
                with pe.Fori(0, NG) as g:
                    body(g)

            @blk.scalar
            def _(act):
                nc.scalar.preload_act_table_set("gelu_apprx_tanh_and_others")
                act.sem_inc(gT_ready, 1)
                with act.Fori(0, NG) as g:
                    act.wait_ge(gt_ready, g + 1)
                    nc.scalar.copy(gT[:, :], bank[6][0:GRP * E, 0:P]).then_inc(gT_ready, 1)
                    for e in range(N_E):
                        act.wait_ge(y_rdy, g * N_E + max(e - 1, 0) + 1)
                        for n in range(FT):
                            act.wait_ge(u_rdy, (g * N_E + e) * FT + n + 1)
                            nc.scalar.activation(hh[e % 2][:, n, :], bank[HB[n]][:, :], ACT.Gelu_apprx_tanh,
                                                 bias=eb1[:, e, n:n + 1]).then_inc(h_rdy, 1)

            @blk.vector
            def _(dve):
                dve.sem_inc(y_used, 1)
                with dve.Fori(0, NG) as g:
                    dve.wait_ge(gT_ready, g + 1)
                    dve.tensor_copy(gst[:, :, :], gates[:, bass.ts(g, GRP), :]).then_inc(gst_ready, 1)
                    dve.wait_ge(bias_ready, g + 1)
                    dve.tensor_tensor(acc[0][:, :, :], bank[7][:, :].rearrange("p (c d) -> p c d", c=GRP),
                                      bs2[:, :].unsqueeze(1).broadcast_to([P, GRP, D]), ALU.add).then_inc(acc_step, 1)
                    for e in range(N_E):
                        dve.wait_ge(acc_step, g * (N_E + 1) + e + 1)
                        dve.wait_ge(y_rdy, g * N_E + e + 2)
                        src, dst = acc[e % 2], acc[1 - e % 2]
                        if e == N_E - 1:
                            dve.tensor_tensor(dst[:, :, :], bank[YB[e % 2]][:, :].rearrange("p (c d) -> p c d", c=GRP),
                                              src[:, :, :], ALU.add).then_inc(y_used, 1)
                            break
                        for j in range(GRP):
                            ins = dve.scalar_tensor_tensor(
                                out=dst[:, j, :], in0=bank[YB[e % 2]][:, j * P:(j + 1) * P],
                                scalar=gates[:, g * GRP + j, e:e + 1], in1=src[:, j, :], op0=ALU.mult, op1=ALU.add)
                            if j == 0:
                                ins.then_inc(acc_step, 1)
                        ins.then_inc(y_used, 1)
                        dve.wait_ge(y_used, g * N_E + e + 2)
                    dve.wait_ge(y_used, g * N_E + N_E + 1)
                    a, b = acc[1 - (N_E - 1) % 2], acc[(N_E - 1) % 2]
                    dve.tensor_tensor(b[:, :, :], a[:, :, :], mod[:, 5, :].unsqueeze(1).broadcast_to([P, GRP, D]),
                                      ALU.mult).then_inc(acc_step, 1)
                    dve.wait_ge(acc_step, g * (N_E + 1) + N_E + 1)
                    xs = xr[:, bass.ts(g, GRP), :]
                    dve.tensor_tensor(xs, b[:, :, :], xs, ALU.add).then_inc(fin_ready, 1)

            @blk.sync
            def _(sp):
                with sp.Fori(0, NG) as g:
                    sp.wait_ge(fin_ready, g + 1)
                    for b in range(B):
                        sp.dma_start(out_v[b][:, bass.ts(g, GRP), :],
                                     xr[b * STEPS:(b + 1) * STEPS, bass.ts(g, GRP), :]).then_inc(s_out, 16)
                sp.wait_ge(s_out, 16 * B * NG)


_INS = ['L0_attn_x', 'L0_attn_W_Q', 'L0_attn_W_KV', 'L0_attn_W1', 'L0_attn_b1', 'L0_attn_W2', 'L0_attn_b2',
        'L0_ffn_w_router', 'L0_ffn_W1', 'L0_ffn_b1', 'L0_ffn_W2', 'L0_ffn_b2', 'L0_ffn_Ws1', 'L0_ffn_bs1',
        'L0_ffn_Ws2', 'L0_ffn_bs2', 'L0_c', 'L0_wmod']


def kernel(**inputs):
    import numpy as _np
    import concourse.bacc as _bacc
    from concourse import mybir as _mybir
    from concourse.bass_utils import run_bass_kernel_spmd as _run

    nc = _bacc.Bacc("TRN2", target_bir_lowering=False, num_devices=1)
    arrays, args = {}, []
    step = _np.arange(P) % STEPS
    given = {name: _np.ascontiguousarray(inputs[name]) for name in _INS}
    given["ident"] = _np.eye(P, dtype=_np.float32)
    given["before"] = (step[:, None] < step[None, :]).astype(_np.float32)
    for name, a in given.items():
        arrays[f"in_{name}_dram"] = a
        args.append(nc.dram_tensor(f"in_{name}_dram", a.shape, _mybir.dt.from_np(a.dtype), kind="ExternalInput").ap())
    out = nc.dram_tensor("out_0_dram", (B, S, D), F32, kind="ExternalOutput").ap()
    program(nc, *args, out)
    r = _run(nc, [arrays], core_ids=[0])
    return r.results[0]["out_0_dram"]
```

```python
from contextlib import ExitStack

import concourse.bass as bass
from concourse import mybir

ACT = mybir.ActivationFunctionType
ALU = mybir.AluOpType
F32 = mybir.dt.float32
BF16 = mybir.dt.bfloat16
I32 = mybir.dt.int32
AX_X = mybir.AxisListType.X

P = 128
B, S, D = 4, 1024, 128
STEPS = P // B
CH = S // STEPS
E, F = 8, 512
FT = F // P
GRP = 4
NG = CH // GRP
TOK = GRP * P
LR = 0.001
KAPPA = LR * 2.0 / (B * D)
SCALE = (1 + 2 / E) ** -0.5
EPS = 1e-5
N_H = 3
TOL = 2.0 ** -11


def program(nc, x, w_q, w_kv, w1, b1, w2, b2, w_router, e_w1, e_b1, e_w2, e_b2,
            s_w1, s_b1, s_w2, s_b2, cond, w_mod, ident_in, before_in, out):
    with ExitStack() as ctx:
        ctx.enter_context(nc.allow_non_contiguous_dma(reason="small transposed operands"))

        def sb(name, shape, dt=F32):
            return ctx.enter_context(nc.sbuf_tensor(name, shape, dt))

        def sem(name):
            return ctx.enter_context(nc.semaphore(name))

        bank = [ctx.enter_context(nc.psum_tensor(f"bank{i}", [P, 512], F32)) for i in range(8)]
        bankb = [t[:, :].bitcast(BF16) for t in bank]

        xr = sb("xr", [P, CH, D])
        hT = sb("hT", [P, CH + 2, P])
        stats = sb("stats", [P, CH, 6])
        mean = sb("mean", [P, CH])
        var = sb("var", [P, CH])
        rstd = sb("rstd", [P, CH])
        tmp = sb("tmp", [P, CH])
        mod = sb("mod", [P, 6, D])
        condT = sb("condT", [P, B])
        scT = sb("scT", [P, B])
        scB = sb("scB", [P, B, STEPS])
        wmod = sb("wmod", [P, 6 * D])
        ident = sb("ident", [P, P])
        identb = sb("identb", [P, P], BF16)
        before = sb("before", [P, P])
        mk = sb("mk", [P, P])
        mkh = sb("mkh", [P, P])
        ones = sb("ones", [P, P])
        onesb = sb("onesb", [P, 1], BF16)
        hstage = sb("hstage", [P, 2, GRP, D])

        wq = sb("wq", [P, D])
        wkv = sb("wkv", [P, 2 * D])
        W1 = sb("W1", [P, D])
        W2 = sb("W2", [P, D])
        W2T = sb("W2T", [P, D])
        b1c = sb("b1c", [P, 1])
        b1h = sb("b1h", [P, 1])
        b2c = sb("b2c", [P, 1])

        block = lambda: nc.Block()

        s_small = sem("s_small")
        s_x = sem("s_x")
        with block() as blk:
            sc_ready = sem("sc_ready")
            mod_ready = sem("mod_ready")
            w2t_ready = sem("w2t_ready")
            setup_done = sem("setup_done")
            mod_copied = sem("mod_copied")

            @blk.sync
            def _(sp):
                for b in range(B):
                    sp.dma_start(xr[b * STEPS:(b + 1) * STEPS, :, :],
                                 x[b].rearrange("(c t) d -> t c d", t=STEPS)).then_inc(s_x, 16)

            @blk.gpsimd
            def _(pool):
                nc.gpsimd.memset(ones[:, :], 1.0)
                nc.gpsimd.memset(onesb[:, :], 1.0)
                nc.gpsimd.memset(hT[:, CH:CH + 2, :], 0.0)

            @blk.scalar
            def _(act):
                for dst, src in ((condT[:, :], cond.rearrange("b d -> d b")), (wmod[:, :], w_mod),
                                 (ident[:, :], ident_in), (before[:, :], before_in),
                                 (wq[:, :], w_q), (wkv[:, :], w_kv), (W1[:, :], w1), (W2[:, :], w2),
                                 (b1c[:, :], b1.rearrange("(d o) -> d o", o=1)),
                                 (b2c[:, :], b2.rearrange("(d o) -> d o", o=1))):
                    act.dma_start(dst, src).then_inc(s_small, 16)
                act.wait_ge(s_small, 160)
                nc.scalar.activation(scT[:, :], condT[:, :], ACT.Silu).then_inc(sc_ready, 1)
                act.wait_ge(sc_ready, 1)
                nc.scalar.copy(scB[:, :, :], scT[:, :].unsqueeze(2).broadcast_to([P, B, STEPS])).then_inc(sc_ready, 1)

            @blk.tensor
            def _(pe):
                pe.wait_ge(sc_ready, 2)
                lhs = scB[:, :, :].rearrange("p b t -> p (b t)")
                for n in range(2):
                    pe.matmul(bank[n][:, 0:384], lhs, wmod[:, n * 384:(n + 1) * 384],
                              start=True, stop=True).then_inc(mod_ready, 1)
                pe.transpose(bank[2][:, 0:P], W2[:, :], ident[:, :]).then_inc(w2t_ready, 1)

            @blk.vector
            def _(dve):
                dve.wait_ge(s_x, 16 * B)
                with dve.Fori(0, CH) as c:
                    dve.bn_stats(stats[:, c, :], xr[:, c, :])
                dve.wait_ge(s_small, 160)
                dve.tensor_copy(identb[:, :], ident[:, :])
                dve.tensor_scalar(mk[:, :], before[:, :], -KAPPA, None, ALU.mult)
                dve.tensor_scalar(mkh[:, :], before[:, :], -KAPPA / 2, None, ALU.mult)
                dve.tensor_scalar(b1h[:, :], b1c[:, :], 0.5, None, ALU.mult)
                dve.wait_ge(mod_ready, 2)
                flat = mod[:, :, :].rearrange("p m d -> p (m d)")
                for n in range(2):
                    dve.tensor_copy(flat[:, n * 384:(n + 1) * 384], bank[n][:, 0:384]).then_inc(mod_copied, 1)
                dve.wait_ge(w2t_ready, 1)
                dve.tensor_copy(W2T[:, :], bank[2][:, 0:P]).then_inc(mod_copied, 1)
                dve.wait_ge(mod_copied, 3)
                for n in (1, 4):
                    dve.tensor_scalar(mod[:, n, :], mod[:, n, :], 1.0, None, ALU.add).then_inc(mod_copied, 1)
                k = 5
                for n in (2, 5):
                    dve.tensor_scalar(hstage[:, 0, 0, :], mod[:, n, :], 0.0, 2.0, ALU.is_ge, ALU.mult).then_inc(mod_copied, 1)
                    dve.scalar_tensor_tensor(out=hstage[:, 0, 1, :], in0=mod[:, n, :], scalar=-1.0, in1=mod[:, n, :],
                                             op0=ALU.mult, op1=ALU.max).then_inc(mod_copied, 1)
                    k += 2
                    dve.wait_ge(mod_copied, k)
                    dve.tensor_scalar(hstage[:, 0, 1, :], hstage[:, 0, 1, :], 0.25, None, ALU.max).then_inc(mod_copied, 1)
                    k += 1
                    dve.wait_ge(mod_copied, k)
                    dve.scalar_tensor_tensor(out=mod[:, n, :], in0=hstage[:, 0, 0, :], scalar=-1.0,
                                             in1=hstage[:, 0, 1, :], op0=ALU.add, op1=ALU.mult).then_inc(mod_copied, 1)
                    k += 1
                    dve.wait_ge(mod_copied, k)

        def layer_norm(tag, scale_n, shift_n, router=None):
            with block() as blk:
                stat = sem(f"{tag}_stat")
                var_ready = sem(f"{tag}_var")
                std_ready = sem(f"{tag}_std")
                norm_ready = sem(f"{tag}_norm")
                h_ready = sem(f"{tag}_h")
                hmul = sem(f"{tag}_hmul")
                tr_ready = sem(f"{tag}_tr")
                copied = sem(f"{tag}_copied")
                if router:
                    lg_ready = sem("lg_ready")
                    lg_copied = sem("lg_copied")
                    lr_ready = sem("lr_ready")
                    lr_copied = sem("lr_copied")
                    wrT, lgT, logits = router

                @blk.vector
                def _(dve):
                    n = [0]

                    def link(ins):
                        ins.then_inc(stat, 1)
                        n[0] += 1
                        dve.wait_ge(stat, n[0])

                    me, mo = stats[:, :, 1], stats[:, :, 4]
                    link(dve.tensor_tensor(mean[:, :], me, mo, ALU.add))
                    link(dve.tensor_scalar(mean[:, :], mean[:, :], 0.5, None, ALU.mult))
                    link(dve.tensor_tensor(tmp[:, :], me, mo, ALU.subtract))
                    link(dve.tensor_tensor(tmp[:, :], tmp[:, :], tmp[:, :], ALU.mult))
                    link(dve.tensor_tensor(var[:, :], stats[:, :, 2], stats[:, :, 5], ALU.add))
                    link(dve.tensor_scalar(var[:, :], var[:, :], 1.0 / D, EPS, ALU.mult, ALU.add))
                    dve.scalar_tensor_tensor(out=var[:, :], in0=tmp[:, :], scalar=0.25, in1=var[:, :],
                                             op0=ALU.mult, op1=ALU.add).then_inc(var_ready, 1)
                    dve.wait_ge(std_ready, 1)
                    link(dve.reciprocal(rstd[:, :], tmp[:, :]))
                    link(dve.tensor_tensor(tmp[:, :], rstd[:, :], rstd[:, :], ALU.mult))
                    link(dve.tensor_tensor(tmp[:, :], tmp[:, :], var[:, :], ALU.mult))
                    link(dve.tensor_scalar(tmp[:, :], tmp[:, :], -0.5, 1.5, ALU.mult, ALU.add))
                    link(dve.tensor_tensor(rstd[:, :], rstd[:, :], tmp[:, :], ALU.mult))
                    with dve.Fori(0, NG // 2) as pair:
                        g = pair * 2
                        for k in range(2):
                            dve.wait_ge(tr_ready, g + k + 1)
                            for j in range(GRP):
                                c = (g + k) * GRP + j
                                dve.tensor_scalar(hstage[:, k, j, :], xr[:, c, :], mean[:, bass.ts(c, 1)], rstd[:, bass.ts(c, 1)],
                                                  ALU.subtract, ALU.mult).then_inc(norm_ready, 1)

                @blk.gpsimd
                def _(pool):
                    with pool.Fori(0, NG // 2) as pair:
                        g = pair * 2
                        for k in range(2):
                            pool.wait_ge(norm_ready, (g + k + 1) * GRP)
                            sc = mod[:, scale_n, :].unsqueeze(1).broadcast_to([P, GRP, D])
                            sh = mod[:, shift_n, :].unsqueeze(1).broadcast_to([P, GRP, D])
                            pool.tensor_tensor(hstage[:, k, :, :], hstage[:, k, :, :], sc, ALU.mult).then_inc(hmul, 1)
                            pool.wait_ge(hmul, g + k + 1)
                            pool.tensor_tensor(hstage[:, k, :, :], hstage[:, k, :, :], sh, ALU.add).then_inc(h_ready, 1)

                @blk.tensor
                def _(pe):
                    pe.sem_inc(tr_ready, 2)
                    with pe.Fori(0, NG // 2) as pair:
                        g = pair * 2
                        for k in range(2):
                            pe.wait_ge(h_ready, g + k + 1)
                            pe.wait_ge(copied, g + k + 1)
                            for j in range(GRP):
                                t = pe.transpose(bank[k][:, j * P:(j + 1) * P], hstage[:, k, j, :], ident[:, :])
                            t.then_inc(tr_ready, 1)
                            if router:
                                pe.wait_ge(copied, g + k + 3)
                                pe.wait_ge(lg_copied, g + k + 1)
                                pe.matmul(bank[2][0:E, :], wrT[:, :],
                                          hT[:, bass.ts(g + k, GRP), :].rearrange("p c t -> p (c t)"),
                                          start=True, stop=True).then_inc(lg_ready, 1)
                                pe.wait_ge(lg_copied, g + k + 2)
                                pe.wait_ge(lr_copied, g + k + 1)
                                for j in range(GRP):
                                    t = pe.matmul(bank[3][:, j * E:(j + 1) * E], lgT[0:E, j * P:(j + 1) * P],
                                                  ident[0:E, 0:E], start=True, stop=True)
                                t.then_inc(lr_ready, 1)

                @blk.scalar
                def _(act):
                    act.sem_inc(copied, 2)
                    if router:
                        act.sem_inc(lg_copied, 1)
                        act.sem_inc(lr_copied, 1)
                    act.wait_ge(var_ready, 1)
                    nc.scalar.activation(tmp[:, :], var[:, :], ACT.Sqrt).then_inc(std_ready, 1)
                    with act.Fori(0, NG // 2) as pair:
                        g = pair * 2
                        for k in range(2):
                            act.wait_ge(tr_ready, g + k + 3)
                            nc.scalar.copy(hT[:, bass.ts(g + k, GRP), :].rearrange("p c t -> p (c t)"),
                                           bank[k][:, :]).then_inc(copied, 1)
                            if router:
                                act.wait_ge(lg_ready, g + k + 1)
                                nc.scalar.copy(lgT[0:E, :], bank[2][0:E, :]).then_inc(lg_copied, 1)
                                act.wait_ge(lr_ready, g + k + 1)
                                nc.scalar.copy(logits[:, bass.ts(g + k, GRP), :].rearrange("p c e -> p (c e)"),
                                               bank[3][:, 0:GRP * E]).then_inc(lr_copied, 1)

        layer_norm("ln1", 1, 0)

        RING = 4
        kv = [sb(f"kv{i}", [P, 2 * P]) for i in range(RING)]
        krow = [sb(f"krow{i}", [P, P]) for i in range(RING)]
        G = [sb(f"G{i}", [P, P]) for i in range(RING)]
        kTb, krowb, Gb = ([sb(f"{n}{i}", [P, P], BF16) for i in range(RING)] for n in ("kTb", "krowb", "Gb"))
        aH, tH, eH, GaH, GeH, arowH, uH, spH = (sb(n, [P, P]) for n in ("aH", "tH", "eH", "GaH", "GeH", "arowH", "uH", "spH"))
        erowH, gH = ([sb(f"{n}{i}", [P, P]) for i in range(2)] for n in ("erowH", "gH"))
        aL, tL, eL, GaL, GeL, arowL, erowLb, arowLb = (
            sb(n, [P, P], BF16) for n in ("aL", "tL", "eL", "GaL", "GeL", "arowL", "erowLb", "arowLb"))
        uL, spL = sb("uL", [P, P]), sb("spL", [P, P])
        erowL = [sb(f"erowL{i}", [P, P], BF16) for i in range(2)]
        gL = [sb(f"gL{i}", [P, P], BF16) for i in range(2)]
        arowX, erowX, GeX = (sb(n, [P, P]) for n in ("arowX", "erowX", "GeX"))
        W1L, W2L, W2TL = (sb(n, [P, P], BF16) for n in ("W1L", "W2L", "W2TL"))
        b1L, b1hL, b2L = (sb(n, [P, 1]) for n in ("b1L", "b1hL", "b2L"))
        chk = sb("chk", [P, 4, P])
        chd = sb("chd", [P, 4, P])
        HZ, HY, HF, HG, LA, LB, LC, LD = (bank[i] for i in range(8))
        LAb, LBb = bankb[4], bankb[5]

        with block() as blk:
            h_z, h_a, h_t, h_gram, h_GaM, h_y, h_e, h_tr, h_arow, h_u, h_sp, h_f, h_g, h_etr, h_erow = (
                sem(f"h_{n}") for n in "z a t gram GaM y e tr arow u sp f g etr erow".split())
            h_gE, h_GeM = sem("h_gE"), sem("h_GeM")
            h_U1, h_W1, h_U2 = sem("h_U1"), sem("h_W1"), sem("h_U2")
            h_b1, h_W2 = sem("h_b1"), sem("h_W2")
            l_z, l_a, l_t, l_gram, l_GaM, l_ya, l_ea, l_T, l_arow, l_u, l_sp, l_yb, l_eb, l_f, l_g, l_gE, l_GeM, l_cast = (
                sem(f"l_{n}") for n in "z a t gram GaM ya ea T arow u sp yb eb f g gE GeM cast".split())
            l_etr, l_erow = sem("l_etr"), sem("l_erow")
            l_U1, l_W1, l_U2 = sem("l_U1"), sem("l_W1"), sem("l_U2")
            l_b1, l_W2 = sem("l_b1"), sem("l_W2")
            q_kv, q_kvc, q_kg, q_krow, q_G, q_cast = (sem(f"q_{n}") for n in "kv kvc kg krow G cast".split())
            chk_done, chk_step = sem("chk_done"), sem("chk_step")

            @blk.tensor
            def _(pe):
                def mm(dst, lhs, rhs, start, stop):
                    return pe.matmul(dst, lhs, rhs, start=start, stop=stop, skip_group_check=True)

                def q_proj(q):
                    mm(LD[:, 0:P], wkv[:, 0:D], hT[:, q, :], True, True)
                    mm(LD[:, P:2 * P], wkv[:, D:2 * D], hT[:, q, :], True, True).then_inc(q_kv, 1)

                def q_gram(r):
                    pe.transpose(LD[:, 2 * P:3 * P], kv[r][:, 0:P], ident[:, :])
                    mm(LD[:, 3 * P:4 * P], kv[r][:, 0:P], kv[r][:, 0:P], True, True).then_inc(q_kg, 1)

                def l_upd1(m, r):
                    pe.wait_ge(l_g, 2 * m)
                    mm(LD[:, 0:P], krowb[(r - 1) % RING][:, :], gL[1][:, :], True, True)
                    mm(LD[:, P:P + 1], gL[1][:, :], onesb[:, :], True, True).then_inc(l_U1, 1)

                def l_upd2(m):
                    pe.wait_ge(l_cast, 2 * m)
                    pe.wait_ge(l_u, 2 * m)
                    mm(LB[:, 0:P], arowLb[:, :], erowLb[:, :], True, True)
                    mm(LB[:, P:2 * P], erowLb[:, :], arowLb[:, :], True, True)
                    mm(LB[:, 2 * P:2 * P + 1], erowLb[:, :], onesb[:, :], True, True).then_inc(l_U2, 1)

                def l_z0(m, r, first=False):
                    pe.wait_ge(l_W1, m + 1)
                    pe.wait_ge(q_cast, m + 1)
                    if not first:
                        pe.wait_ge(l_erow, 4 * m)
                    mm(LA[:, 0:P], W1L[:, :], kTb[r][:, :], True, True).then_inc(l_z, 1)

                def l_z1(m, r):
                    pe.wait_ge(l_erow, 4 * m + 2)
                    mm(LA[:, 0:P], W1L[:, :], kTb[r][:, :], True, False)
                    pe.wait_ge(l_g, 2 * m + 1)
                    mm(LA[:, 0:P], gL[0][:, :], Gb[r][:, :], False, True).then_inc(l_z, 1)

                def l_gram_(m, j):
                    pe.wait_ge(l_a, 2 * m + j + 1)
                    if j == 0:
                        pe.wait_ge(l_W2, 3 * m + 3)
                    else:
                        pe.wait_ge(l_u, 2 * m + 1)
                    mm(LB[:, 0:P], aL[:, :], aL[:, :], True, True).then_inc(l_gram, 1)

                def l_y0(m, first=False):
                    if not first:
                        pe.wait_ge(l_GeM, 2 * m)
                    mm(LC[:, 0:P], W2L[:, :], aL[:, :], True, True).then_inc(l_ya, 1)

                def l_y1(m):
                    pe.wait_ge(l_GeM, 2 * m + 1)
                    mm(LC[:, 0:P], W2L[:, :], aL[:, :], True, False)
                    pe.wait_ge(l_GaM, 2 * m + 2)
                    mm(LC[:, 0:P], erowL[1][:, :], GaL[:, :], False, True).then_inc(l_ya, 1)

                def l_rows(m, j):
                    pe.wait_ge(l_t, 2 * m + j + 1)
                    pe.wait_ge(l_GaM, 2 * m + j + 1)
                    pe.transpose(LBb[:, 0:P], aL[:, :], identb[:, :])
                    pe.transpose(LBb[:, P:2 * P], tL[:, :], identb[:, :]).then_inc(l_T, 1)

                def l_etr_a(m, j):
                    pe.wait_ge(l_ea, 2 * m + j + 1)
                    pe.transpose(LAb[:, 0:P], eL[:, :], identb[:, :]).then_inc(l_etr, 1)

                def l_y_again(m, j):
                    mm(LC[:, 0:P], W2L[:, :], aL[:, :], True, False)
                    pe.wait_ge(l_erow, 4 * m + 2 * j + 1)
                    mm(LC[:, 0:P], erowL[0][:, :], GaL[:, :], False, True).then_inc(l_yb, 1)

                def l_fc(m):
                    pe.wait_ge(q_G, m + 2)
                    pe.wait_ge(l_arow, 2 * m + 1)
                    mm(LD[:, 0:P], GeL[:, :], arowL[:, :], True, False)

                def l_fb(m, j):
                    pe.wait_ge(l_eb, 2 * m + j + 1)
                    if j == 0:
                        pe.wait_ge(q_kvc, m + 2)
                    mm(LD[:, 0:P], eL[:, :], W2TL[:, :], j == 0, True).then_inc(l_f, 1)

                def l_etr_b():
                    pe.transpose(LAb[:, 0:P], eL[:, :], identb[:, :]).then_inc(l_etr, 1)

                def l_ee():
                    mm(LC[:, 0:P], eL[:, :], eL[:, :], True, True).then_inc(l_gE, 1)

                def h_z0(c, r):
                    pe.wait_ge(h_W1, c + 1)
                    pe.wait_ge(q_cast, c + 1)
                    mm(HZ[:, 0:P], W1[:, :], kv[r][:, 0:P], True, False)
                    pe.wait_ge(l_g, 2 * c + 2)
                    mm(HZ[:, 0:P], gL[1][:, :], Gb[r][:, :], False, True).then_inc(h_z, 1)

                def h_zb(c, r, i):
                    pe.wait_ge(h_t, N_H * c + i)
                    mm(HZ[:, 0:P], W1[:, :], kv[r][:, 0:P], True, False)

                def h_zg(c, r, i):
                    pe.wait_ge(h_g, N_H * c + i)
                    mm(HZ[:, 0:P], gH[(i - 1) % 2][:, :], G[r][:, :], False, True).then_inc(h_z, 1)

                def h_fc(c, i):
                    if i == 0:
                        pe.wait_ge(h_b1, 2 * c + 2)
                        pe.wait_ge(l_GeM, 2 * c + 2)
                        pe.wait_ge(l_arow, 2 * c + 2)
                        mm(HF[:, 0:P], GeX[:, :], arowX[:, :], True, False)
                    else:
                        pe.wait_ge(h_g, N_H * c + i)
                        pe.wait_ge(h_GeM, (N_H - 1) * c + i)
                        pe.wait_ge(h_arow, N_H * c + i)
                        mm(HF[:, 0:P], GeH[:, :], arowH[:, :], True, False)

                def h_gram_(c, i):
                    pe.wait_ge(h_a, N_H * c + i + 1)
                    if i == 0:
                        pe.wait_ge(h_W2, 3 * c + 3)
                    else:
                        pe.wait_ge(h_erow, N_H * c + i)
                    mm(HG[:, 0:P], aH[:, :], aH[:, :], True, True).then_inc(h_gram, 1)

                def h_yb(c, i):
                    if i:
                        pe.wait_ge(h_GeM, (N_H - 1) * c + i)
                    mm(HY[:, 0:P], W2[:, :], aH[:, :], True, False)

                def h_yc(c, i):
                    pe.wait_ge(h_GaM, N_H * c + i + 1)
                    if i == 0:
                        pe.wait_ge(l_erow, 4 * c + 4)
                    mm(HY[:, 0:P], (erowH[(i - 1) % 2] if i else erowX)[:, :], GaH[:, :], False, True).then_inc(h_y, 1)

                def h_rows(c, i):
                    pe.wait_ge(h_t, N_H * c + i + 1)
                    pe.transpose(HG[:, 0:P], aH[:, :], ident[:, :])
                    pe.transpose(HG[:, P:2 * P], tH[:, :], ident[:, :]).then_inc(h_tr, 1)

                def h_fb(c, i):
                    pe.wait_ge(h_e, N_H * c + i + 1)
                    mm(HF[:, 0:P], eH[:, :], W2T[:, :], False, True).then_inc(h_f, 1)

                def h_ee():
                    mm(HY[:, 0:P], eH[:, :], eH[:, :], True, True).then_inc(h_gE, 1)

                def h_etr_(c, i):
                    pe.wait_ge(h_u, N_H * c + i + 1)
                    pe.transpose(HG[:, 0:P], eH[:, :], ident[:, :]).then_inc(h_etr, 1)

                def h_upd1(c, r):
                    pe.wait_ge(h_g, N_H * c + N_H)
                    mm(HF[:, 0:P], krow[r][:, :], gH[0][:, :], True, True)
                    mm(HF[:, P:P + 1], gH[0][:, :], ones[:, 0:1], True, True).then_inc(h_U1, 1)

                def h_upd2(c):
                    pe.wait_ge(h_arow, N_H * c + N_H)
                    pe.wait_ge(h_erow, N_H * c + N_H)
                    mm(HG[:, 0:P], arowH[:, :], erowH[0][:, :], True, True)
                    mm(HG[:, P:2 * P], erowH[0][:, :], arowH[:, :], True, True)
                    mm(HG[:, 2 * P:2 * P + 1], erowH[0][:, :], ones[:, 0:1], True, True).then_inc(h_U2, 1)

                q_proj(0)
                pe.wait_ge(q_kvc, 1)
                q_gram(0)
                pe.wait_ge(q_G, 1)
                q_proj(1)
                pe.wait_ge(q_kvc, 2)
                q_gram(1)
                l_z0(0, 0, first=True)
                l_gram_(0, 0)
                l_y0(0, first=True)
                l_rows(0, 0)
                l_etr_a(0, 0)
                l_y_again(0, 0)
                pe.wait_ge(q_G, 2)
                l_fb(0, 0)
                l_etr_b()
                l_ee()
                l_z1(0, 0)
                l_gram_(0, 1)
                l_y1(0)
                l_rows(0, 1)
                l_etr_a(0, 1)
                l_fc(0)
                l_y_again(0, 1)
                l_fb(0, 1)
                l_etr_b()
                l_ee()

                with pe.Fori(0, CH // RING) as ring:
                    for r in range(RING):
                        c = ring * RING + r
                        m, s = c + 1, (r + 1) % RING
                        l_upd1(m, s)
                        h_z0(c, r)
                        h_fc(c, 0)
                        l_upd2(m)
                        l_z0(m, s)
                        pe.wait_ge(l_b1, 2 * m + 2)
                        q_proj(c + 2)
                        h_gram_(c, 0)
                        h_yb(c, 0)
                        h_zb(c, r, 1)
                        l_gram_(m, 0)
                        l_y0(m)
                        h_yc(c, 0)
                        h_rows(c, 0)
                        l_rows(m, 0)
                        l_etr_a(m, 0)
                        h_fb(c, 0)
                        h_ee()
                        l_y_again(m, 0)
                        h_etr_(c, 0)
                        h_zg(c, r, 1)
                        h_fc(c, 1)
                        l_fb(m, 0)
                        l_etr_b()
                        l_ee()
                        h_gram_(c, 1)
                        h_yb(c, 1)
                        h_zb(c, r, 2)
                        l_z1(m, s)
                        h_yc(c, 1)
                        h_rows(c, 1)
                        q_gram((r + 2) % RING)
                        l_gram_(m, 1)
                        h_fb(c, 1)
                        h_ee()
                        h_etr_(c, 1)
                        l_y1(m)
                        l_rows(m, 1)
                        h_zg(c, r, 2)
                        h_fc(c, 2)
                        l_etr_a(m, 1)
                        l_fc(m)
                        h_gram_(c, 2)
                        h_yb(c, 2)
                        l_y_again(m, 1)
                        h_yc(c, 2)
                        h_rows(c, 2)
                        l_fb(m, 1)
                        l_etr_b()
                        l_ee()
                        h_fb(c, 2)
                        h_etr_(c, 2)
                        h_upd1(c, r)
                        h_upd2(c)

            @blk.scalar
            def _(act):
                def q_copy(q, r):
                    act.wait_ge(q_kv, q + 1)
                    nc.scalar.copy(kv[r][:, :], LD[:, 0:2 * P]).then_inc(q_kvc, 1)

                def q_rows(q, r):
                    act.wait_ge(q_kg, q + 1)
                    nc.scalar.copy(krow[r][:, :], LD[:, 2 * P:3 * P]).then_inc(q_krow, 1)

                def l_at(m, j):
                    if j == 0:
                        act.wait_ge(l_b1, 2 * m + 2)
                    act.wait_ge(l_z, 2 * m + j + 1)
                    nc.scalar.activation(aL[:, :], LA[:, 0:P], ACT.Silu, bias=b1L[:, 0:1]).then_inc(l_a, 1)
                    nc.scalar.activation(tL[:, :], LA[:, 0:P], ACT.Tanh, bias=b1hL[:, 0:1], scale=0.5).then_inc(l_t, 1)

                def l_arow_(m, j, first=False):
                    if j == 1 and not first:
                        act.wait_ge(l_cast, 2 * m)
                    act.wait_ge(l_T, 2 * m + j + 1)
                    nc.scalar.copy((arowX if j else arowL)[:, :], LBb[:, 0:P]).then_inc(l_arow, 1)

                def l_erow_(m, n, first=False):
                    if n == 3 and not first:
                        act.wait_ge(l_cast, 2 * m)
                    act.wait_ge(l_etr, 4 * m + n + 1)
                    nc.scalar.copy((erowX if n == 3 else erowL[n % 2])[:, :], LAb[:, 0:P]).then_inc(l_erow, 1)

                def h_at(c, i):
                    if i == 0:
                        act.wait_ge(h_b1, 2 * c + 2)
                    act.wait_ge(h_z, N_H * c + i + 1)
                    nc.scalar.activation(aH[:, :], HZ[:, 0:P], ACT.Silu, bias=b1c[:, 0:1]).then_inc(h_a, 1)
                    nc.scalar.activation(tH[:, :], HZ[:, 0:P], ACT.Tanh, bias=b1h[:, 0:1], scale=0.5).then_inc(h_t, 1)

                def h_arow_(c, i):
                    act.wait_ge(h_tr, N_H * c + i + 1)
                    nc.scalar.copy(arowH[:, :], HG[:, 0:P]).then_inc(h_arow, 1)

                def h_erow_(c, i):
                    if i == 0:
                        act.wait_ge(chk_done, c + 1)
                    act.wait_ge(h_etr, N_H * c + i + 1)
                    nc.scalar.copy(erowH[i % 2][:, :], HG[:, 0:P]).then_inc(h_erow, 1)

                nc.scalar.preload_act_table_set("silu_and_others")
                q_copy(0, 0)
                q_rows(0, 0)
                q_copy(1, 1)
                q_rows(1, 1)
                l_at(0, 0)
                l_arow_(0, 0, first=True)
                l_erow_(0, 0, first=True)
                l_erow_(0, 1, first=True)
                l_at(0, 1)
                l_arow_(0, 1, first=True)
                l_erow_(0, 2, first=True)
                l_erow_(0, 3, first=True)
                with act.Fori(0, CH // RING) as ring:
                    for r in range(RING):
                        c = ring * RING + r
                        m, t = c + 1, (r + 2) % RING
                        h_at(c, 0)
                        l_at(m, 0)
                        q_copy(c + 2, t)
                        h_arow_(c, 0)
                        l_arow_(m, 0)
                        l_erow_(m, 0)
                        h_erow_(c, 0)
                        h_at(c, 1)
                        l_erow_(m, 1)
                        l_at(m, 1)
                        h_arow_(c, 1)
                        q_rows(c + 2, t)
                        h_erow_(c, 1)
                        l_arow_(m, 1)
                        h_at(c, 2)
                        l_erow_(m, 2)
                        h_arow_(c, 2)
                        l_erow_(m, 3)
                        h_erow_(c, 2)

            @blk.vector
            def _(dve):
                def stt(dst, a, s, b, o0, o1):
                    return dve.scalar_tensor_tensor(out=dst, in0=a, scalar=s, in1=b, op0=o0, op1=o1)

                def q_G_(q, r):
                    dve.wait_ge(q_krow, q + 1)
                    stt(G[r][:, :], LD[:, 3 * P:4 * P], 1.0, mkh[:, :], ALU.add, ALU.mult).then_inc(q_G, 1)

                def l_new1(m):
                    dve.wait_ge(l_U1, m)
                    dve.wait_ge(h_W1, m)
                    dve.wait_ge(h_b1, 2 * m)
                    stt(W1L[:, :], LD[:, 0:P], -KAPPA / 2, W1[:, :], ALU.mult, ALU.add).then_inc(l_W1, 1)
                    stt(b1L[:, :], LD[:, P:P + 1], -KAPPA / 2, b1c[:, :], ALU.mult, ALU.add).then_inc(l_b1, 1)
                    stt(b1hL[:, :], LD[:, P:P + 1], -KAPPA / 4, b1h[:, :], ALU.mult, ALU.add).then_inc(l_b1, 1)

                def l_new2(m):
                    dve.wait_ge(l_U2, m)
                    dve.wait_ge(h_W2, 3 * m)
                    stt(W2L[:, :], LB[:, 0:P], -KAPPA, W2[:, :], ALU.mult, ALU.add).then_inc(l_W2, 1)
                    stt(W2TL[:, :], LB[:, P:2 * P], -KAPPA, W2T[:, :], ALU.mult, ALU.add).then_inc(l_W2, 1)
                    stt(b2L[:, :], LB[:, 2 * P:2 * P + 1], -KAPPA, b2c[:, :], ALU.mult, ALU.add).then_inc(l_W2, 1)

                def l_Ga(m, j):
                    dve.wait_ge(l_gram, 2 * m + j + 1)
                    stt(GaL[:, :], LB[:, 0:P], 1.0, mk[:, :], ALU.add, ALU.mult).then_inc(l_GaM, 1)

                def l_e1(m, r, j):
                    if j == 0:
                        dve.wait_ge(l_W2, 3 * m + 3)
                    dve.wait_ge(l_ya, 2 * m + j + 1)
                    stt(eL[:, :], LC[:, 0:P], b2L[:, 0:1], kv[r][:, P:2 * P], ALU.add, ALU.subtract).then_inc(l_ea, 1)

                def l_e2(m, r, j):
                    dve.wait_ge(l_yb, 2 * m + j + 1)
                    stt(eL[:, :], LC[:, 0:P], b2L[:, 0:1], kv[r][:, P:2 * P], ALU.add, ALU.subtract).then_inc(l_eb, 1)

                def l_u_(m, j):
                    dve.wait_ge(l_arow, 2 * m + j + 1)
                    stt(uL[:, :], (arowX if j else arowL)[:, :], -1.0, LBb[:, P:2 * P], ALU.add, ALU.mult).then_inc(l_u, 1)

                def l_sp_(m, j):
                    dve.wait_ge(l_u, 2 * m + j + 1)
                    stt(spL[:, :], (arowX if j else arowL)[:, :], 1.0, uL[:, :], ALU.add, ALU.subtract).then_inc(l_sp, 1)

                def l_g_(m, j):
                    dve.wait_ge(l_sp, 2 * m + j + 1)
                    dve.wait_ge(l_f, 2 * m + j + 1)
                    dve.tensor_tensor(gL[j][:, :], LD[:, 0:P], spL[:, :], ALU.mult).then_inc(l_g, 1)

                def l_Ge(m, j):
                    dve.wait_ge(l_gE, 2 * m + j + 1)
                    dve.tensor_tensor((GeX if j else GeL)[:, :], LC[:, 0:P], mk[:, :], ALU.mult).then_inc(l_GeM, 1)

                def h_Ga(c, i):
                    dve.wait_ge(h_gram, N_H * c + i + 1)
                    stt(GaH[:, :], HG[:, 0:P], 1.0, mk[:, :], ALU.add, ALU.mult).then_inc(h_GaM, 1)

                def h_e_(c, r, i):
                    dve.wait_ge(h_y, N_H * c + i + 1)
                    stt(eH[:, :], HY[:, 0:P], b2c[:, 0:1], kv[r][:, P:2 * P], ALU.add, ALU.subtract).then_inc(h_e, 1)

                def h_u_(c, i):
                    dve.wait_ge(h_arow, N_H * c + i + 1)
                    stt(uH[:, :], arowH[:, :], -1.0, HG[:, P:2 * P], ALU.add, ALU.mult).then_inc(h_u, 1)

                def h_sp_(c, i):
                    dve.wait_ge(h_u, N_H * c + i + 1)
                    stt(spH[:, :], arowH[:, :], 1.0, uH[:, :], ALU.add, ALU.subtract).then_inc(h_sp, 1)

                def h_Ge(c, i):
                    dve.wait_ge(h_gE, (N_H - 1) * c + i + 1)
                    dve.tensor_tensor(GeH[:, :], HY[:, 0:P], mk[:, :], ALU.mult).then_inc(h_GeM, 1)

                def h_g_(c, i):
                    if i == 0:
                        dve.wait_ge(chk_done, c + 1)
                    dve.wait_ge(h_sp, N_H * c + i + 1)
                    dve.wait_ge(h_f, N_H * c + i + 1)
                    dve.tensor_tensor(gH[i % 2][:, :], HF[:, 0:P], spH[:, :], ALU.mult).then_inc(h_g, 1)

                def h_new1(c):
                    dve.wait_ge(h_U1, c + 1)
                    for w, u, s, done in ((W1[:, :], HF[:, 0:P], -KAPPA / 2, h_W1), (b1c[:, :], HF[:, P:P + 1], -KAPPA / 2, h_b1),
                                          (b1h[:, :], HF[:, P:P + 1], -KAPPA / 4, h_b1)):
                        stt(w, u, s, w, ALU.mult, ALU.add).then_inc(done, 1)

                def h_new2(c):
                    dve.wait_ge(h_U2, c + 1)
                    for w, u in ((W2[:, :], HG[:, 0:P]), (W2T[:, :], HG[:, P:2 * P]), (b2c[:, :], HG[:, 2 * P:2 * P + 1])):
                        stt(w, u, -KAPPA, w, ALU.mult, ALU.add).then_inc(h_W2, 1)

                dve.tensor_copy(W1L[:, :], W1[:, :]).then_inc(l_W1, 1)
                for dst, src in ((b1L, b1c), (b1hL, b1h)):
                    dve.tensor_copy(dst[:, :], src[:, :]).then_inc(l_b1, 1)
                for dst, src in ((W2L, W2), (W2TL, W2T), (b2L, b2c)):
                    dve.tensor_copy(dst[:, :], src[:, :]).then_inc(l_W2, 1)
                dve.sem_inc(h_W1, 1)
                dve.sem_inc(h_b1, 2)
                dve.sem_inc(h_W2, 3)
                q_G_(0, 0)
                q_G_(1, 1)
                for j in range(2):
                    l_Ga(0, j)
                    l_e1(0, 0, j)
                    l_u_(0, j)
                    l_sp_(0, j)
                    l_e2(0, 0, j)
                    l_g_(0, j)
                    l_Ge(0, j)
                with dve.Fori(0, CH // RING) as ring:
                    for r in range(RING):
                        c = ring * RING + r
                        m, s = c + 1, (r + 1) % RING
                        l_new1(m)
                        l_new2(m)
                        h_Ga(c, 0)
                        l_Ga(m, 0)
                        l_e1(m, s, 0)
                        h_e_(c, r, 0)
                        h_u_(c, 0)
                        l_u_(m, 0)
                        h_sp_(c, 0)
                        h_Ge(c, 0)
                        h_g_(c, 0)
                        l_e2(m, s, 0)
                        l_sp_(m, 0)
                        l_g_(m, 0)
                        l_Ge(m, 0)
                        h_Ga(c, 1)
                        h_e_(c, r, 1)
                        h_u_(c, 1)
                        l_Ga(m, 1)
                        h_sp_(c, 1)
                        h_Ge(c, 1)
                        h_g_(c, 1)
                        l_e1(m, s, 1)
                        q_G_(c + 2, (r + 2) % RING)
                        l_u_(m, 1)
                        l_sp_(m, 1)
                        h_Ga(c, 2)
                        l_e2(m, s, 1)
                        h_e_(c, r, 2)
                        l_g_(m, 1)
                        l_Ge(m, 1)
                        h_u_(c, 2)
                        h_sp_(c, 2)
                        h_g_(c, 2)
                        h_new1(c)
                        h_new2(c)

            @blk.gpsimd
            def _(pool):
                def q_cast_(q, r):
                    pool.wait_ge(q_G, q + 1)
                    pool.tensor_tensor(kTb[r][:, :], kv[r][:, 0:P], ones[:, :], ALU.mult)
                    pool.tensor_tensor(Gb[r][:, :], G[r][:, :], ones[:, :], ALU.mult)
                    pool.tensor_tensor(krowb[r][:, :], krow[r][:, :], ones[:, :], ALU.mult).then_inc(q_cast, 1)

                def l_cast_(m):
                    pool.wait_ge(l_arow, 2 * m + 2)
                    pool.tensor_tensor(arowLb[:, :], arowX[:, :], ones[:, :], ALU.mult).then_inc(l_cast, 1)
                    pool.wait_ge(l_erow, 4 * m + 4)
                    pool.tensor_tensor(erowLb[:, :], erowX[:, :], ones[:, :], ALU.mult).then_inc(l_cast, 1)

                def check(c):
                    pool.wait_ge(chk_step, c * 6 + 1)
                    pool.wait_ge(h_g, N_H * c + N_H)
                    pool.tensor_tensor(chd[:, 0, :], gH[0][:, :], gH[1][:, :], ALU.subtract).then_inc(chk_step, 1)
                    pool.tensor_tensor(chd[:, 1, :], gH[0][:, :], gH[0][:, :], ALU.mult).then_inc(chk_step, 1)
                    pool.wait_ge(h_erow, N_H * c + N_H)
                    pool.tensor_tensor(chd[:, 2, :], erowH[0][:, :], erowH[1][:, :], ALU.subtract).then_inc(chk_step, 1)
                    pool.tensor_tensor(chd[:, 3, :], erowH[0][:, :], erowH[0][:, :], ALU.mult).then_inc(chk_done, 1)
                    pool.wait_ge(chk_step, c * 6 + 4)
                    pool.tensor_tensor(chd[:, 0, :], chd[:, 0, :], chd[:, 0, :], ALU.mult).then_inc(chk_step, 1)
                    pool.tensor_tensor(chd[:, 2, :], chd[:, 2, :], chd[:, 2, :], ALU.mult).then_inc(chk_step, 1)
                    pool.wait_ge(chk_step, c * 6 + 6)
                    pool.wait_ge(chk_done, c + 2)
                    flat = chk[:, :, :].rearrange("p a b -> p (a b)")
                    pool.tensor_tensor(flat, flat, chd[:, :, :].rearrange("p a b -> p (a b)"), ALU.add).then_inc(chk_step, 1)

                nc.gpsimd.memset(chk[:, :, :], 0.0).then_inc(chk_step, 1)
                pool.wait_ge(chk_step, 1)
                pool.sem_inc(chk_done, 1)
                q_cast_(0, 0)
                q_cast_(1, 1)
                l_cast_(0)
                with pool.Fori(0, CH // RING) as ring:
                    for r in range(RING):
                        c = ring * RING + r
                        q_cast_(c + 2, (r + 2) % RING)
                        l_cast_(c + 1)
                        check(c)

        sums = sb("sums", [P, 4])
        holds = sb("holds", [P, 4])
        count = sb("count", [1, 1], I32)
        with block() as blk:
            sums_ready, holds_step, total_ready, count_ready = sem("sums_ready"), sem("holds_step"), sem("total_ready"), sem("count_ready")

            @blk.vector
            def _(dve):
                dve.tensor_reduce(sums[:, :], chk[:, :, :], AX_X, ALU.add).then_inc(sums_ready, 1)
                dve.wait_ge(sums_ready, 1)
                for n in range(2):
                    dve.scalar_tensor_tensor(out=holds[:, 2 * n:2 * n + 1], in0=sums[:, 2 * n + 1:2 * n + 2], scalar=TOL * TOL,
                                             in1=sums[:, 2 * n:2 * n + 1], op0=ALU.mult, op1=ALU.is_ge).then_inc(holds_step, 1)
                    dve.tensor_scalar(holds[:, 2 * n + 1:2 * n + 2], sums[:, 2 * n + 1:2 * n + 2], 3e38, None,
                                      ALU.is_le).then_inc(holds_step, 1)
                dve.wait_ge(total_ready, 1)
                dve.tensor_reduce(holds[0:1, 0:1], bank[0][0:1, 0:4], AX_X, ALU.add).then_inc(holds_step, 1)
                dve.wait_ge(holds_step, 5)
                dve.tensor_copy(count[:, :], holds[0:1, 0:1]).then_inc(count_ready, 1)

            @blk.tensor
            def _(pe):
                pe.wait_ge(holds_step, 4)
                pe.matmul(bank[0][0:1, 0:4], ones[:, 0:1], holds[:, :], start=True, stop=True).then_inc(total_ready, 1)

        k4 = sb("k4", [P, 2 * B])
        a4, t4, u4, sp4, e4, g4 = (sb(n, [P, B]) for n in ("a4", "t4", "u4", "sp4", "e4", "g4"))
        gs, es = sb("gs", [P, 1]), sb("es", [P, 1])
        rows4 = sb("rows4", [B, 4, P])
        with block() as blk:
            s_again, w2t_again, w2t_copied = sem("s_again"), sem("w2t_again"), sem("w2t_copied")
            k_step, kc_step, z_step, a_step, t_step = (sem(f"{n}_step") for n in ("k", "kc", "z", "a", "t"))
            y_step, e_step, u_step, sp_step, f_step = (sem(f"{n}_step") for n in ("y", "e", "u", "sp", "f"))
            g_step, r_step, rc_step, U_step, s_step = (sem(f"{n}_step") for n in ("g", "r", "rc", "U", "s"))
            w_step = sem("w_step")

            def holding(eng):
                return eng.value_load(count[0:1, 0:1], min_val=0, max_val=4 * P)

            def steps(eng, body):
                with eng.Fori(0, CH) as c:
                    with eng.Fori(0, STEPS) as j:
                        body(c, j, c * STEPS + j)

            @blk.sync
            def _(sp):
                with sp.If(holding(sp) < 4 * P):
                    for dst, src in ((W1[:, :], w1), (W2[:, :], w2), (b1c[:, :], b1.rearrange("(d o) -> d o", o=1)),
                                     (b2c[:, :], b2.rearrange("(d o) -> d o", o=1))):
                        sp.dma_start(dst, src).then_inc(s_again, 16)

            @blk.tensor
            def _(pe):
                with pe.If(holding(pe) < 4 * P):
                    pe.wait_ge(s_again, 64)
                    pe.transpose(bank[0][:, 0:P], W2[:, :], ident[:, :]).then_inc(w2t_again, 1)

                    def step(c, j, n):
                        h4 = hT[:, c, :].rearrange("p (b t) -> p t b", t=STEPS)[:, j, :]
                        pe.wait_ge(w_step, n * 6 + 6)
                        pe.matmul(bank[0][:, 0:B], wkv[:, 0:D], h4, start=True, stop=True)
                        pe.matmul(bank[0][:, B:2 * B], wkv[:, D:2 * D], h4, start=True, stop=True).then_inc(k_step, 1)
                        pe.wait_ge(kc_step, n + 1)
                        pe.matmul(bank[1][:, 0:B], W1[:, :], k4[:, 0:B], start=True, stop=True).then_inc(z_step, 1)
                        pe.wait_ge(a_step, n + 1)
                        pe.matmul(bank[2][:, 0:B], W2[:, :], a4[:, :], start=True, stop=True).then_inc(y_step, 1)
                        pe.wait_ge(e_step, n + 1)
                        pe.matmul(bank[3][:, 0:B], W2T[:, :], e4[:, :], start=True, stop=True).then_inc(f_step, 1)
                        pe.wait_ge(g_step, n + 1)
                        for m, src in enumerate((k4[:, 0:B], a4[:, :], e4[:, :], g4[:, :])):
                            t = pe.transpose(bank[4][0:B, m * P:(m + 1) * P], src, ident[:, :])
                        t.then_inc(r_step, 1)
                        pe.wait_ge(rc_step, n + 1)
                        kr, ar, er, gr = (rows4[:, m, :] for m in range(4))
                        pe.matmul(bank[5][:, 0:P], kr, gr, start=True, stop=True)
                        pe.matmul(bank[5][:, P:2 * P], ar, er, start=True, stop=True)
                        pe.matmul(bank[5][:, 2 * P:3 * P], er, ar, start=True, stop=True).then_inc(U_step, 1)
                    steps(pe, step)

            @blk.scalar
            def _(act):
                with act.If(holding(act) < 4 * P):
                    def step(c, j, n):
                        act.wait_ge(k_step, n + 1)
                        nc.scalar.copy(k4[:, :], bank[0][:, 0:2 * B]).then_inc(kc_step, 1)
                        act.wait_ge(z_step, n + 1)
                        nc.scalar.activation(a4[:, :], bank[1][:, 0:B], ACT.Silu, bias=b1c[:, 0:1]).then_inc(a_step, 1)
                        nc.scalar.activation(t4[:, :], bank[1][:, 0:B], ACT.Tanh, bias=b1h[:, 0:1],
                                             scale=0.5).then_inc(t_step, 1)
                    steps(act, step)

            @blk.vector
            def _(dve):
                with dve.If(holding(dve) < 4 * P):
                    dve.wait_ge(w2t_again, 1)
                    dve.tensor_copy(W2T[:, :], bank[0][:, 0:P]).then_inc(w2t_copied, 1)
                    dve.tensor_scalar(b1h[:, :], b1c[:, :], 0.5, None, ALU.mult).then_inc(w2t_copied, 1)
                    dve.wait_ge(w2t_copied, 2)
                    dve.sem_inc(w_step, 6)

                    def step(c, j, n):
                        dve.wait_ge(y_step, n + 1)
                        dve.scalar_tensor_tensor(out=e4[:, :], in0=bank[2][:, 0:B], scalar=b2c[:, 0:1], in1=k4[:, B:2 * B],
                                                 op0=ALU.add, op1=ALU.subtract).then_inc(e_step, 1)
                        dve.wait_ge(t_step, n + 1)
                        dve.scalar_tensor_tensor(out=u4[:, :], in0=a4[:, :], scalar=-1.0, in1=t4[:, :],
                                                 op0=ALU.add, op1=ALU.mult).then_inc(u_step, 1)
                        dve.wait_ge(u_step, n + 1)
                        dve.scalar_tensor_tensor(out=sp4[:, :], in0=a4[:, :], scalar=1.0, in1=u4[:, :],
                                                 op0=ALU.add, op1=ALU.subtract).then_inc(sp_step, 1)
                        dve.wait_ge(sp_step, n + 1)
                        dve.wait_ge(f_step, n + 1)
                        dve.tensor_tensor(g4[:, :], bank[3][:, 0:B], sp4[:, :], ALU.mult).then_inc(g_step, 1)
                        dve.wait_ge(r_step, n + 1)
                        dve.tensor_copy(rows4[:, :, :].rearrange("b m d -> b (m d)"), bank[4][0:B, :]).then_inc(rc_step, 1)
                        dve.wait_ge(g_step, n + 1)
                        dve.tensor_reduce(gs[:, :], g4[:, :], AX_X, ALU.add).then_inc(s_step, 1)
                        dve.tensor_reduce(es[:, :], e4[:, :], AX_X, ALU.add).then_inc(s_step, 1)
                        dve.wait_ge(s_step, n * 2 + 2)
                        dve.wait_ge(U_step, n + 1)
                        for w, u, r in ((W1[:, :], bank[5][:, 0:P], -KAPPA / 2), (W2[:, :], bank[5][:, P:2 * P], -KAPPA),
                                        (W2T[:, :], bank[5][:, 2 * P:3 * P], -KAPPA), (b1c[:, :], gs[:, :], -KAPPA / 2),
                                        (b1h[:, :], gs[:, :], -KAPPA / 4), (b2c[:, :], es[:, :], -KAPPA)):
                            dve.scalar_tensor_tensor(out=w, in0=u, scalar=r, in1=w, op0=ALU.mult,
                                                     op1=ALU.add).then_inc(w_step, 1)
                        dve.wait_ge(w_step, n * 6 + 12)
                    steps(dve, step)


        qT = [sb(f"qT{i}", [P, TOK]) for i in range(2)]
        qa = [sb(f"qa{i}", [P, TOK]) for i in range(2)]
        t1 = [sb(f"t1{i}", [P, GRP, D]) for i in range(2)]
        gab = sb("gab", [P, D])
        with block() as blk:
            d_ready, b_ready, gab_ready = sem("d_ready"), sem("b_ready"), sem("gab_ready")
            q_ready, q_copied = sem("q_ready"), sem("q_copied")
            qz_ready, qa_ready = sem("qz_ready"), sem("qa_ready")
            o_ready, o_used, xg_ready, x1_ready = sem("o_ready"), sem("o_used"), sem("xg_ready"), sem("x1_ready")

            @blk.tensor
            def _(pe):
                pe.wait_ge(d_ready, 1)
                pe.matmul(bank[6][:, 0:D], ones[:, :], uH[:, :], start=True, stop=True).then_inc(b_ready, 1)
                with pe.Fori(0, NG // 2) as pair:
                    g = pair * 2
                    for k in range(2):
                        pe.wait_ge(q_copied, g + k + 1)
                        pe.matmul(bank[k][:, :], wq[:, :], hT[:, bass.ts(g + k, GRP), :].rearrange("p c t -> p (c t)"),
                                  start=True, stop=True).then_inc(q_ready, 1)
                        pe.wait_ge(q_copied, g + k + 2)
                        pe.wait_ge(qa_ready, g + k + 1)
                        pe.matmul(bank[2 + k][:, :], W1[:, :], qT[k][:, :], start=True, stop=True).then_inc(qz_ready, 1)
                        pe.wait_ge(qa_ready, g + k + 2)
                        pe.wait_ge(o_used, g + k + 1)
                        for j in range(GRP):
                            mm = pe.matmul(bank[4 + k][:, j * P:(j + 1) * P], qa[k][:, j * P:(j + 1) * P], W2[:, :],
                                           start=True, stop=True)
                        mm.then_inc(o_ready, 1)

            @blk.scalar
            def _(act):
                nc.scalar.preload_act_table_set("silu_and_others")
                act.sem_inc(q_copied, 1)
                act.sem_inc(qa_ready, 1)
                with act.Fori(0, NG // 2) as pair:
                    g = pair * 2
                    for k in range(2):
                        act.wait_ge(q_ready, g + k + 1)
                        nc.scalar.copy(qT[k][:, :], bank[k][:, :]).then_inc(q_copied, 1)
                        act.wait_ge(qz_ready, g + k + 1)
                        nc.scalar.activation(qa[k][:, :], bank[2 + k][:, :], ACT.Silu, bias=b1c[:, 0:1]).then_inc(qa_ready, 1)

            @blk.vector
            def _(dve):
                dve.tensor_scalar(uH[:, :], ident[:, :], b2c[:, 0:1], None, ALU.mult).then_inc(d_ready, 1)
                dve.sem_inc(o_used, 1)
                dve.wait_ge(b_ready, 1)
                dve.tensor_tensor(gab[:, :], bank[6][:, 0:D], mod[:, 2, :], ALU.mult).then_inc(gab_ready, 1)
                with dve.Fori(0, NG // 2) as pair:
                    g = pair * 2
                    for k in range(2):
                        dve.wait_ge(o_ready, g + k + 1)
                        dve.tensor_tensor(t1[k][:, :, :], bank[4 + k][:, :].rearrange("p (c d) -> p c d", c=GRP),
                                          mod[:, 2, :].unsqueeze(1).broadcast_to([P, GRP, D]), ALU.mult).then_inc(o_used, 1)
                        dve.wait_ge(o_used, g + k + 2)
                        dve.wait_ge(xg_ready, g + k + 1)
                        xs = xr[:, bass.ts(g + k, GRP), :]
                        dve.tensor_tensor(xs, t1[k][:, :, :], xs, ALU.add).then_inc(x1_ready, 1)
                        dve.wait_ge(x1_ready, g + k + 1)
                        for j in range(GRP):
                            c = (g + k) * GRP + j
                            dve.bn_stats(stats[:, c, :], xr[:, c, :])

            @blk.gpsimd
            def _(pool):
                pool.wait_ge(gab_ready, 1)
                with pool.Fori(0, NG) as g:
                    xs = xr[:, bass.ts(g, GRP), :]
                    pool.tensor_tensor(xs, xs, gab[:, :].unsqueeze(1).broadcast_to([P, GRP, D]), ALU.add).then_inc(xg_ready, 1)

        wrT = sb("wrT", [P, E])
        lgT = sb("lgT", [E, TOK])
        logits = sb("logits", [P, CH, E])
        gates = sb("gates", [P, CH, E])
        gtmp = sb("gtmp", [P, CH, E])
        rank = sb("rank", [P, CH, E])
        cmp = sb("cmp", [P, CH, E, E])
        red = sb("red", [P, CH])
        b2blk = sb("b2blk", [GRP * E, GRP, D])
        bs2 = sb("bs2", [P, D])
        w1n = sb("w1n", [P, 2, FT, D])
        w2n = sb("w2n", [P, 2, F])
        w1T = sb("w1T", [P, E + 1, FT, P])
        w2T = sb("w2T", [P, E + 1, FT, D])
        eb1 = sb("eb1", [P, E + 1, FT])
        with block() as blk:
            s_w, s_b = [sem(f"s_w{i}") for i in range(2)], sem("s_b")
            wt_ready, wt_copied, z_b2 = sem("wt_ready"), sem("wt_copied"), sem("z_b2")

            @blk.gpsimd
            def _(pool):
                nc.gpsimd.memset(b2blk[:, :, :], 0.0).then_inc(z_b2, 1)

            @blk.sync
            def _(sp):
                sp.dma_start(wrT[:, :], w_router.rearrange("e d -> d e")).then_inc(s_b, 16)
                for e in range(E + 1):
                    src = e_b1[e] if e < E else s_b1
                    sp.dma_start(eb1[:, e, :], src.rearrange("(n p) -> p n", p=P)).then_inc(s_b, 16)
                sp.dma_start(bs2[:, :], s_b2.rearrange("(o d) -> o d", o=1).broadcast_to([P, D])).then_inc(s_b, 16)
                sp.wait_ge(z_b2, 1)
                for j in range(GRP):
                    sp.dma_start(b2blk[j * E:(j + 1) * E, j, :], e_b2).then_inc(s_b, 16)
                for e in range(E + 1):
                    w1s, w2s = (e_w1[e], e_w2[e]) if e < E else (s_w1, s_w2)
                    if e >= 2:
                        sp.wait_ge(wt_ready, 2 * (e - 1))
                    sp.dma_start(w1n[:, e % 2, :, :], w1s.rearrange("(n p) d -> p n d", p=P)).then_inc(s_w[e % 2], 16)
                    sp.dma_start(w2n[:, e % 2, :], w2s).then_inc(s_w[e % 2], 16)
                sp.wait_ge(s_b, 16 * (E + 7))

            @blk.tensor
            def _(pe):
                for e in range(E + 1):
                    pe.wait_ge(s_w[e % 2], 32 * (e // 2 + 1))
                    for m in range(2):
                        if e:
                            pe.wait_ge(wt_copied, 2 * e - 1 + m)
                        for n in range(FT):
                            src = w2n[:, e % 2, n * P:(n + 1) * P] if m else w1n[:, e % 2, n, :]
                            t = pe.transpose(bank[m][:, n * P:(n + 1) * P], src, ident[:, :])
                        t.then_inc(wt_ready, 1)

            @blk.vector
            def _(dve):
                for e in range(E + 1):
                    for m, dst in enumerate((w1T, w2T)):
                        dve.wait_ge(wt_ready, 2 * e + m + 1)
                        dve.tensor_copy(dst[:, e, :, :].rearrange("p n d -> p (n d)"), bank[m][:, :]).then_inc(wt_copied, 1)

        layer_norm("ln2", 4, 3, router=(wrT, lgT, logits))

        with block() as blk:
            step, ex_ready = sem("gate_step"), sem("ex_ready")

            @blk.scalar
            def _(act):
                act.wait_ge(step, 2)
                nc.scalar.activation(gates[:, :, :], gtmp[:, :, :], ACT.Exp).then_inc(ex_ready, 1)

            @blk.vector
            def _(dve):
                n = [0]

                def link(ins):
                    ins.then_inc(step, 1)
                    n[0] += 1
                    dve.wait_ge(step, n[0])

                bc = lambda t: t.unsqueeze(2).broadcast_to([P, CH, E])
                link(dve.tensor_reduce(red[:, :], logits[:, :, :], AX_X, ALU.max))
                link(dve.tensor_tensor(gtmp[:, :, :], logits[:, :, :], bc(red[:, :]), ALU.subtract))
                mine = logits[:, :, :].unsqueeze(3).broadcast_to([P, CH, E, E])
                other = logits[:, :, :].unsqueeze(2).broadcast_to([P, CH, E, E])
                link(dve.tensor_tensor(cmp[:, :, :, :], other, mine, ALU.is_gt))
                for e in range(1, E):
                    link(dve.tensor_tensor(cmp[:, :, e, 0:e], other[:, :, e, 0:e], mine[:, :, e, 0:e], ALU.is_ge))
                link(dve.tensor_reduce(rank[:, :, :], cmp[:, :, :, :], AX_X, ALU.add))
                dve.wait_ge(ex_ready, 1)
                link(dve.tensor_reduce(red[:, :], gates[:, :, :], AX_X, ALU.add))
                link(dve.reciprocal(red[:, :], red[:, :]))
                link(dve.tensor_tensor(gates[:, :, :], gates[:, :, :], bc(red[:, :]), ALU.mult))
                link(dve.scalar_tensor_tensor(out=gates[:, :, :], in0=rank[:, :, :], scalar=1.5, in1=gates[:, :, :],
                                              op0=ALU.is_lt, op1=ALU.mult))
                link(dve.tensor_scalar(mod[:, 5, :], mod[:, 5, :], SCALE, None, ALU.mult))

        hh = [sb(f"hh{i}", [P, FT, TOK]) for i in range(2)]
        acc = [sb(f"acc{i}", [P, GRP, D]) for i in range(2)]
        gst = sb("gst", [P, GRP, E])
        gT = sb("gT", [GRP * E, P])
        N_E = E + 1
        with block() as blk:
            gst_ready, gt_ready, gT_ready, bias_ready = sem("gst_ready"), sem("gt_ready"), sem("gT_ready"), sem("bias_ready")
            u_rdy, h_rdy = sem("up_ready"), sem("hid_ready")
            y_rdy, y_used = sem("down_ready"), sem("down_used")
            acc_step, fin_step, fin_ready = sem("acc_step"), sem("fin_step"), sem("fin_ready")
            s_out = sem("s_out")
            HB, YB = (0, 1, 2, 3), (4, 5)
            out_v = [out[b].rearrange("(c t) d -> t c d", t=STEPS) for b in range(B)]

            @blk.tensor
            def _(pe):
                def group(g, par):
                    hg = hT[:, bass.ts(g, GRP), :].rearrange("p c t -> p (c t)")

                    def up(e):
                        for n in range(FT):
                            if e:
                                pe.wait_ge(h_rdy, (g * N_E + e - 1) * FT + n + 1)
                            pe.matmul(bank[HB[n]][:, :], w1T[:, e, n, :], hg, start=True, stop=True).then_inc(u_rdy, 1)

                    def down(e):
                        pe.wait_ge(h_rdy, (g * N_E + e + 1) * FT)
                        pe.wait_ge(y_used, g * N_E + max(e - 1, 0) + 1)
                        for j in range(GRP):
                            for n in range(FT):
                                mm = pe.matmul(bank[YB[e % 2]][:, j * P:(j + 1) * P], hh[e % 2][:, n, j * P:(j + 1) * P],
                                               w2T[:, e, n, :], start=(n == 0), stop=(n == FT - 1))
                        mm.then_inc(y_rdy, 1)

                    pe.wait_ge(gst_ready, g + 1)
                    pe.transpose(bank[6][0:GRP * E, 0:P], gst[:, :, :].rearrange("p c e -> p (c e)"), ident[:, :]).then_inc(gt_ready, 1)
                    return up, down

                def body(g):
                    up, down = group(g, 0)
                    up(0)
                    pe.wait_ge(gT_ready, g + 2)
                    pe.matmul(bank[7][:, :], gT[:, :], b2blk[:, :, :].rearrange("p c d -> p (c d)"),
                              start=True, stop=True).then_inc(bias_ready, 1)
                    for e in range(1, N_E):
                        up(e)
                        down(e - 1)
                    down(N_E - 1)

                pe.sem_inc(y_rdy, 1)
                with pe.Fori(0, NG) as g:
                    body(g)

            @blk.scalar
            def _(act):
                nc.scalar.preload_act_table_set("gelu_apprx_tanh_and_others")
                act.sem_inc(gT_ready, 1)
                with act.Fori(0, NG) as g:
                    act.wait_ge(gt_ready, g + 1)
                    nc.scalar.copy(gT[:, :], bank[6][0:GRP * E, 0:P]).then_inc(gT_ready, 1)
                    for e in range(N_E):
                        act.wait_ge(y_rdy, g * N_E + max(e - 1, 0) + 1)
                        for n in range(FT):
                            act.wait_ge(u_rdy, (g * N_E + e) * FT + n + 1)
                            nc.scalar.activation(hh[e % 2][:, n, :], bank[HB[n]][:, :], ACT.Gelu_apprx_tanh,
                                                 bias=eb1[:, e, n:n + 1]).then_inc(h_rdy, 1)

            @blk.vector
            def _(dve):
                dve.sem_inc(y_used, 1)
                with dve.Fori(0, NG) as g:
                    dve.wait_ge(gT_ready, g + 1)
                    dve.tensor_copy(gst[:, :, :], gates[:, bass.ts(g, GRP), :]).then_inc(gst_ready, 1)
                    dve.wait_ge(bias_ready, g + 1)
                    dve.tensor_tensor(acc[0][:, :, :], bank[7][:, :].rearrange("p (c d) -> p c d", c=GRP),
                                      bs2[:, :].unsqueeze(1).broadcast_to([P, GRP, D]), ALU.add).then_inc(acc_step, 1)
                    for e in range(N_E):
                        dve.wait_ge(acc_step, g * (N_E + 1) + e + 1)
                        dve.wait_ge(y_rdy, g * N_E + e + 2)
                        src, dst = acc[e % 2], acc[1 - e % 2]
                        if e == N_E - 1:
                            dve.tensor_tensor(dst[:, :, :], bank[YB[e % 2]][:, :].rearrange("p (c d) -> p c d", c=GRP),
                                              src[:, :, :], ALU.add).then_inc(y_used, 1)
                            break
                        for j in range(GRP):
                            ins = dve.scalar_tensor_tensor(
                                out=dst[:, j, :], in0=bank[YB[e % 2]][:, j * P:(j + 1) * P],
                                scalar=gates[:, g * GRP + j, e:e + 1], in1=src[:, j, :], op0=ALU.mult, op1=ALU.add)
                            if j == 0:
                                ins.then_inc(acc_step, 1)
                        ins.then_inc(y_used, 1)
                        dve.wait_ge(y_used, g * N_E + e + 2)
                    dve.wait_ge(y_used, g * N_E + N_E + 1)
                    a, b = acc[1 - (N_E - 1) % 2], acc[(N_E - 1) % 2]
                    dve.tensor_tensor(b[:, :, :], a[:, :, :], mod[:, 5, :].unsqueeze(1).broadcast_to([P, GRP, D]),
                                      ALU.mult).then_inc(acc_step, 1)
                    dve.wait_ge(acc_step, g * (N_E + 1) + N_E + 1)
                    xs = xr[:, bass.ts(g, GRP), :]
                    dve.tensor_tensor(xs, b[:, :, :], xs, ALU.add).then_inc(fin_ready, 1)

            @blk.sync
            def _(sp):
                with sp.Fori(0, NG) as g:
                    sp.wait_ge(fin_ready, g + 1)
                    for b in range(B):
                        sp.dma_start(out_v[b][:, bass.ts(g, GRP), :],
                                     xr[b * STEPS:(b + 1) * STEPS, bass.ts(g, GRP), :]).then_inc(s_out, 16)
                sp.wait_ge(s_out, 16 * B * NG)


_INS = ['L0_attn_x', 'L0_attn_W_Q', 'L0_attn_W_KV', 'L0_attn_W1', 'L0_attn_b1', 'L0_attn_W2', 'L0_attn_b2',
        'L0_ffn_w_router', 'L0_ffn_W1', 'L0_ffn_b1', 'L0_ffn_W2', 'L0_ffn_b2', 'L0_ffn_Ws1', 'L0_ffn_bs1',
        'L0_ffn_Ws2', 'L0_ffn_bs2', 'L0_c', 'L0_wmod']


def kernel(**inputs):
    import numpy as _np
    import concourse.bacc as _bacc
    from concourse import mybir as _mybir
    from concourse.bass_utils import run_bass_kernel_spmd as _run

    nc = _bacc.Bacc("TRN2", target_bir_lowering=False, num_devices=1)
    arrays, args = {}, []
    step = _np.arange(P) % STEPS
    given = {name: _np.ascontiguousarray(inputs[name]) for name in _INS}
    given["ident"] = _np.eye(P, dtype=_np.float32)
    given["before"] = (step[:, None] < step[None, :]).astype(_np.float32)
    for name, a in given.items():
        arrays[f"in_{name}_dram"] = a
        args.append(nc.dram_tensor(f"in_{name}_dram", a.shape, _mybir.dt.from_np(a.dtype), kind="ExternalInput").ap())
    out = nc.dram_tensor("out_0_dram", (B, S, D), F32, kind="ExternalOutput").ap()
    program(nc, *args, out)
    r = _run(nc, [arrays], core_ids=[0])
    return r.results[0]["out_0_dram"]
```

```python
from contextlib import ExitStack

import concourse.bass as bass
from concourse import mybir

ACT = mybir.ActivationFunctionType
ALU = mybir.AluOpType
F32 = mybir.dt.float32
BF16 = mybir.dt.bfloat16
F32R = mybir.dt.float32r
I32 = mybir.dt.int32
AX_X = mybir.AxisListType.X

P = 128
B, S, D = 4, 1024, 128
STEPS = P // B
CH = S // STEPS
E, F = 8, 512
FT = F // P
GRP = 4
NG = CH // GRP
TOK = GRP * P
LR = 0.001
KAPPA = LR * 2.0 / (B * D)
SCALE = (1 + 2 / E) ** -0.5
EPS = 1e-5
N_H = 3
TOL = 2.0 ** -10


def program(nc, x, w_q, w_kv, w1, b1, w2, b2, w_router, e_w1, e_b1, e_w2, e_b2,
            s_w1, s_b1, s_w2, s_b2, cond, w_mod, ident_in, before_in, out):
    with ExitStack() as ctx:
        ctx.enter_context(nc.allow_non_contiguous_dma(reason="small transposed operands"))

        def sb(name, shape, dt=F32):
            return ctx.enter_context(nc.sbuf_tensor(name, shape, dt))

        def sem(name):
            return ctx.enter_context(nc.semaphore(name))

        bank = [ctx.enter_context(nc.psum_tensor(f"bank{i}", [P, 512], F32)) for i in range(8)]
        bankb = [t[:, :].bitcast(BF16) for t in bank]

        xr = sb("xr", [P, CH, D])
        hT = sb("hT", [P, CH + 2, P])
        stats = sb("stats", [P, CH, 6])
        mean = sb("mean", [P, CH])
        var = sb("var", [P, CH])
        rstd = sb("rstd", [P, CH])
        tmp = sb("tmp", [P, CH])
        gate = sb("gate", [P, 2, D])
        gtm = sb("gtm", [P, 2, 2, D])
        modT = sb("modT", [P, 4, B])
        condT = sb("condT", [P, B])
        scT = sb("scT", [P, B])
        scB = sb("scB", [P, B, STEPS])
        wmod = sb("wmod", [P, 6 * D])
        ident = sb("ident", [P, P])
        identb = sb("identb", [P, P], BF16)
        before = sb("before", [P, P])
        mk = sb("mk", [P, P])
        mkh = sb("mkh", [P, P])
        ones = sb("ones", [P, P])
        onesb = sb("onesb", [P, 1], BF16)
        hstage = sb("hstage", [P, 2, GRP, D])

        wq = sb("wq", [P, D])
        wqT = sb("wqT", [P, D])
        wkv = sb("wkv", [P, 2 * D])
        W1 = sb("W1", [P, D])
        W2 = sb("W2", [P, D])
        W2T = sb("W2T", [P, D])
        b1c = sb("b1c", [P, 1])
        b1h = sb("b1h", [P, 1])
        b2c = sb("b2c", [P, 1])

        wrT = sb("wrT", [P, E])
        logits = sb("logits", [P, CH, E])
        gates = sb("gates", [P, CH, E])
        gparts = sb("gparts", [P, CH, 3 * E], BF16)
        sel = sb("sel", [3 * E, E, P], BF16)
        selc = sb("selc", [3 * E, E])
        b2T = sb("b2T", [P, E])
        bs2T = sb("bs2T", [P, 1])
        eb1 = sb("eb1", [P, E + 1, FT])
        w1H, w1L, w2H, w2L = (sb(n, [P, E + 1, FT, P], F32R) for n in ("w1H", "w1L", "w2H", "w2L"))

        block = lambda: nc.Block()

        def phase(stack):
            return lambda name, shape, dt=F32: stack.enter_context(nc.sbuf_tensor(name, shape, dt))

        class LayerNorm:

            def __init__(self, tag, shift):
                self.shift = shift
                self.stat = sem(f"{tag}_stat")
                self.var_ready = sem(f"{tag}_var")
                self.std_ready = sem(f"{tag}_std")
                self.norm = sem(f"{tag}_norm")
                self.tr = sem(f"{tag}_tr")
                self.copied = sem(f"{tag}_copied")

            def vector_stats(self, dve):
                n = [0]

                def link(ins):
                    ins.then_inc(self.stat, 1)
                    n[0] += 1
                    dve.wait_ge(self.stat, n[0])

                me, mo = stats[:, :, 1], stats[:, :, 4]
                link(dve.tensor_tensor(mean[:, :], me, mo, ALU.add))
                link(dve.tensor_scalar(mean[:, :], mean[:, :], 0.5, None, ALU.mult))
                link(dve.tensor_tensor(tmp[:, :], me, mo, ALU.subtract))
                link(dve.tensor_tensor(tmp[:, :], tmp[:, :], tmp[:, :], ALU.mult))
                link(dve.tensor_tensor(var[:, :], stats[:, :, 2], stats[:, :, 5], ALU.add))
                link(dve.tensor_scalar(var[:, :], var[:, :], 1.0 / D, EPS, ALU.mult, ALU.add))
                dve.scalar_tensor_tensor(out=var[:, :], in0=tmp[:, :], scalar=0.25, in1=var[:, :],
                                         op0=ALU.mult, op1=ALU.add).then_inc(self.var_ready, 1)
                self.n = n[0]

            def vector(self, dve):
                n = [self.n]

                def link(ins):
                    ins.then_inc(self.stat, 1)
                    n[0] += 1
                    dve.wait_ge(self.stat, n[0])

                dve.wait_ge(self.std_ready, 1)
                link(dve.reciprocal(rstd[:, :], tmp[:, :]))
                link(dve.tensor_tensor(tmp[:, :], rstd[:, :], rstd[:, :], ALU.mult))
                link(dve.tensor_tensor(tmp[:, :], tmp[:, :], var[:, :], ALU.mult))
                link(dve.tensor_scalar(tmp[:, :], tmp[:, :], -0.5, 1.5, ALU.mult, ALU.add))
                link(dve.tensor_tensor(rstd[:, :], rstd[:, :], tmp[:, :], ALU.mult))
                with dve.Fori(0, NG // 2) as pair:
                    g = pair * 2
                    for k in range(2):
                        dve.wait_ge(self.tr, g + k + 1)
                        for j in range(GRP):
                            c = (g + k) * GRP + j
                            dve.tensor_scalar(hstage[:, k, j, :], xr[:, c, :], mean[:, bass.ts(c, 1)], rstd[:, bass.ts(c, 1)],
                                              ALU.subtract, ALU.mult).then_inc(self.norm, 1)

            def transpose(self, pe, g, k):
                pe.wait_ge(self.norm, (g + k + 1) * GRP)
                pe.wait_ge(self.copied, g + k + 1)
                for j in range(GRP):
                    t = pe.transpose(bank[k][:, j * P:(j + 1) * P], hstage[:, k, j, :], ident[:, :])
                t.then_inc(self.tr, 1)

            def scalar(self, act):
                act.sem_inc(self.copied, 2)
                act.wait_ge(self.var_ready, 1)
                nc.scalar.activation(tmp[:, :], var[:, :], ACT.Sqrt).then_inc(self.std_ready, 1)
                nc.scalar.preload_act_table_set("silu_and_others")
                act.wait_ge(modT_ready, 2)
                with act.Fori(0, NG // 2) as pair:
                    g = pair * 2
                    for k in range(2):
                        act.wait_ge(self.tr, g + k + 3)
                        src = bank[k][:, :].rearrange("p (c t) -> p c t", c=GRP)
                        for b in range(B):
                            rows = slice(b * STEPS, (b + 1) * STEPS)
                            cp = nc.scalar.activation(hT[:, bass.ts(g + k, GRP), rows], src[:, :, rows], ACT.Identity,
                                                      bias=modT[:, self.shift, b:b + 1], scale=modT[:, self.shift + 1, b:b + 1])
                        cp.then_inc(self.copied, 1)

        modT_ready = sem("modT_ready")
        with ExitStack() as stack, block() as blk:
            psb = phase(stack)
            N_W = 6
            w1n = psb("w1n", [P, N_W, FT, D])
            w2n = psb("w2n", [P, N_W, F])
            s_small, s_x, s_b = sem("s_small"), [sem(f"s_x{i}") for i in range(2)], sem("s_b")
            s_w = [sem(f"s_w{i}") for i in range(N_W)]
            bn_ready = sem("bn_ready")
            sc_ready, mod_ready, set_ready, gate_done = sem("sc_ready"), sem("mod_ready"), sem("set_ready"), sem("gate_done")
            wt_ready, w_hi, wt_copied = sem("wt_ready"), sem("w_hi"), sem("wt_copied")
            ln1 = LayerNorm("ln1", 0)
            WB = (4, 5, 6, 7)

            @blk.sync
            def _(sp):
                for half in range(2):
                    cs = slice(half * CH // 2, (half + 1) * CH // 2)
                    for b in range(B):
                        sp.dma_start(xr[b * STEPS:(b + 1) * STEPS, cs, :],
                                     x[b].rearrange("(c t) d -> t c d", t=STEPS)[:, cs, :]).then_inc(s_x[half], 16)
                for e in range(E + 1):
                    w1s, w2s = (e_w1[e], e_w2[e]) if e < E else (s_w1, s_w2)
                    if e >= N_W:
                        sp.wait_ge(wt_ready, 2 * (e - N_W + 1))
                    sp.dma_start(w1n[:, e % N_W, :, :], w1s.rearrange("(n p) d -> p n d", p=P)).then_inc(s_w[e % N_W], 16)
                    sp.dma_start(w2n[:, e % N_W, :], w2s).then_inc(s_w[e % N_W], 16)
                sp.dma_start(wrT[:, :], w_router.rearrange("e d -> d e")).then_inc(s_b, 16)
                for e in range(E + 1):
                    src = e_b1[e] if e < E else s_b1
                    sp.dma_start(eb1[:, e, :], src.rearrange("(n p) -> p n", p=P)).then_inc(s_b, 16)
                sp.dma_start(bs2T[:, :], s_b2.rearrange("(d o) -> d o", o=1)).then_inc(s_b, 16)
                sp.dma_start(b2T[:, :], e_b2.rearrange("e d -> d e")).then_inc(s_b, 16)
                sp.wait_ge(s_b, 16 * (E + 4))

            @blk.gpsimd
            def _(pool):
                nc.gpsimd.memset(ones[:, :], 1.0)
                nc.gpsimd.memset(onesb[:, :], 1.0)
                nc.gpsimd.memset(hT[:, CH:CH + 2, :], 0.0)

            @blk.scalar
            def _(act):
                for dst, src in ((condT[:, :], cond.rearrange("b d -> d b")), (wmod[:, :], w_mod),
                                 (ident[:, :], ident_in), (before[:, :], before_in),
                                 (wq[:, :], w_q), (wkv[:, :], w_kv), (W1[:, :], w1), (W2[:, :], w2),
                                 (b1c[:, :], b1.rearrange("(d o) -> d o", o=1)),
                                 (b2c[:, :], b2.rearrange("(d o) -> d o", o=1))):
                    act.dma_start(dst, src).then_inc(s_small, 16)
                act.wait_ge(s_small, 160)
                nc.scalar.activation(scT[:, :], condT[:, :], ACT.Silu).then_inc(sc_ready, 1)
                act.wait_ge(sc_ready, 1)
                nc.scalar.copy(scB[:, :, :], scT[:, :].unsqueeze(2).broadcast_to([P, B, STEPS])).then_inc(sc_ready, 1)
                ln1.scalar(act)
                for e in range(E + 1):
                    for m, hi in enumerate((w1H, w2H)):
                        act.wait_ge(wt_ready, 2 * e + m + 1)
                        nc.scalar.copy(hi[:, e, :, :].rearrange("p n d -> p (n d)"),
                                       bank[WB[2 * (e % 2) + m]][:, :]).then_inc(w_hi, 1)

            @blk.tensor
            def _(pe):
                pe.wait_ge(sc_ready, 2)
                for i, n in enumerate((0, 1, 3, 4)):
                    mm = pe.matmul(bank[3][:, i * B:(i + 1) * B], wmod[:, n * D:(n + 1) * D], scT[:, :], start=True, stop=True)
                mm.then_inc(mod_ready, 1)
                lhs = scB[:, :, :].rearrange("p b t -> p (b t)")
                for i, n in enumerate((2, 5)):
                    pe.matmul(bank[2][:, i * D:(i + 1) * D], lhs, wmod[:, n * D:(n + 1) * D], start=True, stop=True)
                pe.transpose(bank[2][:, 2 * P:3 * P], W2[:, :], ident[:, :])
                pe.transpose(bank[2][:, 3 * P:4 * P], wq[:, :], ident[:, :]).then_inc(mod_ready, 1)
                pe.sem_inc(ln1.tr, 2)
                with pe.Fori(0, NG // 2) as pair:
                    for k in range(2):
                        ln1.transpose(pe, pair * 2, k)
                for e in range(E + 1):
                    pe.wait_ge(s_w[e % N_W], 32 * (e // N_W + 1))
                    for m in range(2):
                        if e >= 2:
                            pe.wait_ge(wt_copied, 2 * e - 3 + m)
                        for n in range(FT):
                            src = w2n[:, e % N_W, n * P:(n + 1) * P] if m else w1n[:, e % N_W, n, :]
                            t = pe.transpose(bank[WB[2 * (e % 2) + m]][:, n * P:(n + 1) * P], src, ident[:, :])
                        t.then_inc(wt_ready, 1)

            @blk.vector
            def _(dve):
                for half in range(2):
                    dve.wait_ge(s_x[half], 16 * B)
                    with dve.Fori(half * NG // 2, (half + 1) * NG // 2) as g:
                        for j in range(GRP):
                            c = g * GRP + j
                            dve.bn_stats(stats[:, c, :], xr[:, c, :]).then_inc(bn_ready, 1)
                dve.wait_ge(bn_ready, CH)
                ln1.vector_stats(dve)
                dve.wait_ge(mod_ready, 1)
                dve.tensor_copy(modT[:, :, :].rearrange("p m b -> p (m b)"), bank[3][:, 0:4 * B]).then_inc(set_ready, 1)
                dve.wait_ge(set_ready, 1)
                for n in (1, 3):
                    dve.tensor_scalar(modT[:, n, :], modT[:, n, :], 1.0, None, ALU.add).then_inc(modT_ready, 1)
                ln1.vector(dve)
                dve.tensor_copy(identb[:, :], ident[:, :])
                dve.tensor_reduce(selc[:, :], ident[0:3 * E, 0:3 * E].rearrange("k (m e) -> k e m", m=3),
                                  AX_X, ALU.add).then_inc(set_ready, 1)
                dve.wait_ge(set_ready, 2)
                dve.tensor_copy(sel[:, :, :], selc[:, :].unsqueeze(2).broadcast_to([3 * E, E, P]))
                dve.tensor_scalar(mk[:, :], before[:, :], -KAPPA, None, ALU.mult)
                dve.tensor_scalar(mkh[:, :], before[:, :], -KAPPA / 2, None, ALU.mult)
                dve.tensor_scalar(b1h[:, :], b1c[:, :], 0.5, None, ALU.mult)
                dve.wait_ge(mod_ready, 2)
                dve.tensor_copy(gate[:, :, :].rearrange("p m d -> p (m d)"), bank[2][:, 0:2 * D]).then_inc(gate_done, 1)
                dve.tensor_copy(W2T[:, :], bank[2][:, 2 * P:3 * P])
                dve.tensor_copy(wqT[:, :], bank[2][:, 3 * P:4 * P])
                dve.wait_ge(gate_done, 1)
                dve.tensor_scalar(gtm[:, 0, :, :], gate[:, :, :], 0.0, 2.0, ALU.is_ge, ALU.mult).then_inc(gate_done, 1)
                dve.scalar_tensor_tensor(out=gtm[:, 1, :, :], in0=gate[:, :, :], scalar=-1.0, in1=gate[:, :, :],
                                         op0=ALU.mult, op1=ALU.max).then_inc(gate_done, 1)
                dve.wait_ge(gate_done, 3)
                dve.tensor_scalar(gtm[:, 1, :, :], gtm[:, 1, :, :], 0.25, None, ALU.max).then_inc(gate_done, 1)
                dve.wait_ge(gate_done, 4)
                dve.scalar_tensor_tensor(out=gate[:, :, :], in0=gtm[:, 0, :, :], scalar=-1.0,
                                         in1=gtm[:, 1, :, :], op0=ALU.add, op1=ALU.mult).then_inc(gate_done, 1)
                dve.wait_ge(gate_done, 5)
                dve.tensor_scalar(gate[:, 1, :], gate[:, 1, :], SCALE, None, ALU.mult)
                for e in range(E + 1):
                    for m, (hi, lo) in enumerate(((w1H, w1L), (w2H, w2L))):
                        dve.wait_ge(w_hi, 2 * e + m + 1)
                        dve.tensor_tensor(lo[:, e, :, :].rearrange("p n d -> p (n d)"), bank[WB[2 * (e % 2) + m]][:, :],
                                          hi[:, e, :, :].rearrange("p n d -> p (n d)").bitcast(F32), ALU.subtract).then_inc(wt_copied, 1)

        scan_stack = ExitStack()
        psb = phase(scan_stack)
        RING = 4
        kv = [psb(f"kv{i}", [P, 2 * P]) for i in range(RING)]
        krow = [psb(f"krow{i}", [P, P]) for i in range(RING)]
        G = [psb(f"G{i}", [P, P]) for i in range(RING)]
        kTb, krowb, Gb = ([psb(f"{n}{i}", [P, P], BF16) for i in range(RING)] for n in ("kTb", "krowb", "Gb"))
        aH, tH, eH, GaH, GeH, uH, spH = (psb(n, [P, P]) for n in ("aH", "tH", "eH", "GaH", "GeH", "uH", "spH"))
        erowH, gH = ([psb(f"{n}{i}", [P, P]) for i in range(2)] for n in ("erowH", "gH"))
        arowH = [psb(f"arowH{i}", [P, P + 1]) for i in range(2)]
        aL, tL, eL = (psb(n, [P, P], BF16) for n in ("aL", "tL", "eL"))
        uL, spL = psb("uL", [P, P]), psb("spL", [P, P])
        GaL, GeL, gL = ([psb(f"{n}{i}", [P, P], BF16) for i in range(2)] for n in ("GaL", "GeL", "gL"))
        arowL = [psb(f"arowL{i}", [P, P + 1], BF16) for i in range(2)]
        erowL = [psb(f"erowL{i}", [P, P], BF16) for i in range(3)]
        W1L, W2L, W2TL = (psb(n, [P, P], BF16) for n in ("W1L", "W2L", "W2TL"))
        b1L, b1hL, b2L = (psb(n, [P, 1]) for n in ("b1L", "b1hL", "b2L"))
        chk = psb("chk", [P, 4, P])
        chd = psb("chd", [P, 4, P])
        HZ, HY, HF, HG, LA, LB, LC, LD = (bank[i] for i in range(8))
        LAb, LBb = bankb[4], bankb[5]

        with block() as blk:
            h_z, h_a, h_t, h_y, h_e, h_Ta, h_Tt, h_arow, h_u, h_sp, h_f, h_g, h_etr, h_erow = (
                sem(f"h_{n}") for n in "z a t y e Ta Tt arow u sp f g etr erow".split())
            h_gram, h_GaM, h_GeM = sem("h_gram"), sem("h_GaM"), sem("h_GeM")
            h_U1, h_U1b, h_W1, h_U2 = (sem(f"h_{n}") for n in "U1 U1b W1 U2".split())
            h_b1, h_W2 = sem("h_b1"), sem("h_W2")
            l_z, l_a, l_t, l_gram, l_GaM, l_ya, l_ea, l_T, l_arow, l_u, l_sp, l_yb, l_eb, l_f, l_g, l_gE, l_GeM = (
                sem(f"l_{n}") for n in "z a t gram GaM ya ea T arow u sp yb eb f g gE GeM".split())
            l_etr, l_erow = sem("l_etr"), sem("l_erow")
            l_U1, l_W1, l_U2 = sem("l_U1"), sem("l_W1"), sem("l_U2")
            l_b1, l_W2 = sem("l_b1"), sem("l_W2")
            q_kv, q_kvc, q_kg, q_krow, q_G, q_cast = (sem(f"q_{n}") for n in "kv kvc kg krow G cast".split())
            chk_done, chk_step = sem("chk_done"), sem("chk_step")

            @blk.tensor
            def _(pe):
                def mm(dst, lhs, rhs, start, stop):
                    return pe.matmul(dst, lhs, rhs, start=start, stop=stop, skip_group_check=True)

                def q_proj(q):
                    mm(LD[:, 0:P], wkv[:, 0:D], hT[:, q, :], True, True)
                    mm(LD[:, P:2 * P], wkv[:, D:2 * D], hT[:, q, :], True, True).then_inc(q_kv, 1)

                def q_gram(r):
                    pe.transpose(LD[:, 2 * P:3 * P], kv[r][:, 0:P], ident[:, :])
                    mm(LD[:, 3 * P:4 * P], kv[r][:, 0:P], kv[r][:, 0:P], True, True).then_inc(q_kg, 1)

                def l_upd1(m, r):
                    pe.wait_ge(l_g, 2 * m)
                    mm(LD[:, 0:P], krowb[(r - 1) % RING][:, :], gL[1][:, :], True, True)
                    mm(LD[:, P:P + 1], gL[1][:, :], onesb[:, :], True, True).then_inc(l_U1, 1)

                def l_upd2(m):
                    pe.wait_ge(l_arow, 2 * m)
                    pe.wait_ge(l_erow, 4 * m)
                    pe.wait_ge(l_u, 2 * m)
                    mm(LB[:, 0:P], arowL[1][:, 0:P], erowL[2][:, :], True, True)
                    mm(LB[:, P:2 * P + 1], erowL[2][:, :], arowL[1][:, :], True, True).then_inc(l_U2, 1)

                def l_z0(m, r, first=False):
                    pe.wait_ge(l_W1, m + 1)
                    pe.wait_ge(q_cast, m + 1)
                    if not first:
                        pe.wait_ge(l_erow, 4 * m)
                    mm(LA[:, 0:P], W1L[:, :], kTb[r][:, :], True, True).then_inc(l_z, 1)

                def l_z1(m, r):
                    pe.wait_ge(l_erow, 4 * m + 2)
                    mm(LA[:, 0:P], W1L[:, :], kTb[r][:, :], True, False)
                    pe.wait_ge(l_g, 2 * m + 1)
                    mm(LA[:, 0:P], gL[0][:, :], Gb[r][:, :], False, True).then_inc(l_z, 1)

                def l_gram_(m, j):
                    pe.wait_ge(l_a, 2 * m + j + 1)
                    if j == 0:
                        pe.wait_ge(l_W2, 3 * m + 3)
                    else:
                        pe.wait_ge(l_u, 2 * m + 1)
                    mm(LB[:, 0:P], aL[:, :], aL[:, :], True, True).then_inc(l_gram, 1)

                def l_y0(m, first=False):
                    pe.wait_ge(l_a, 2 * m + 1)
                    pe.wait_ge(l_W2, 3 * m + 3)
                    if not first:
                        pe.wait_ge(l_GeM, 2 * m)
                    mm(LC[:, 0:P], W2L[:, :], aL[:, :], True, True).then_inc(l_ya, 1)

                def l_y1(m):
                    pe.wait_ge(l_a, 2 * m + 2)
                    pe.wait_ge(l_GeM, 2 * m + 1)
                    mm(LC[:, 0:P], W2L[:, :], aL[:, :], True, False)
                    pe.wait_ge(l_GaM, 2 * m + 2)
                    pe.wait_ge(l_erow, 4 * m + 2)
                    mm(LC[:, 0:P], erowL[1][:, :], GaL[1][:, :], False, True).then_inc(l_ya, 1)

                def l_rows(m, j):
                    pe.wait_ge(l_t, 2 * m + j + 1)
                    pe.wait_ge(l_GaM, 2 * m + j + 1)
                    pe.transpose(LBb[:, 0:P], aL[:, :], identb[:, :])
                    pe.transpose(LBb[:, P:2 * P], tL[:, :], identb[:, :]).then_inc(l_T, 1)

                def l_etr_a(m, j):
                    pe.wait_ge(l_ea, 2 * m + j + 1)
                    pe.wait_ge(l_t, 2 * m + j + 1)
                    pe.transpose(LAb[:, 0:P], eL[:, :], identb[:, :]).then_inc(l_etr, 1)

                def l_y_again(m, j):
                    mm(LC[:, 0:P], W2L[:, :], aL[:, :], True, False)
                    pe.wait_ge(l_erow, 4 * m + 2 * j + 1)
                    pe.wait_ge(l_GaM, 2 * m + j + 1)
                    mm(LC[:, 0:P], erowL[0][:, :], GaL[j][:, :], False, True).then_inc(l_yb, 1)

                def l_fc(m):
                    pe.wait_ge(q_G, m + 2)
                    pe.wait_ge(l_arow, 2 * m + 1)
                    pe.wait_ge(l_GeM, 2 * m + 1)
                    mm(LD[:, 0:P], GeL[0][:, :], arowL[0][:, 0:P], True, False)

                def l_fb(m, j):
                    pe.wait_ge(l_eb, 2 * m + j + 1)
                    if j == 0:
                        pe.wait_ge(q_kvc, m + 2)
                    mm(LD[:, 0:P], eL[:, :], W2TL[:, :], j == 0, True).then_inc(l_f, 1)

                def l_etr_b(m, j):
                    pe.wait_ge(l_eb, 2 * m + j + 1)
                    pe.transpose(LAb[:, 0:P], eL[:, :], identb[:, :]).then_inc(l_etr, 1)

                def l_ee(m, j):
                    pe.wait_ge(l_eb, 2 * m + j + 1)
                    mm(LC[:, 0:P], eL[:, :], eL[:, :], True, True).then_inc(l_gE, 1)

                def h_z0(c, r):
                    pe.wait_ge(q_cast, c + 1)
                    pe.wait_ge(l_g, 2 * c + 2)
                    mm(HZ[:, 0:P], gL[1][:, :], Gb[r][:, :], True, False)
                    pe.wait_ge(h_W1, c + 1)
                    mm(HZ[:, 0:P], W1[:, :], kv[r][:, 0:P], False, True).then_inc(h_z, 1)

                def h_zb(c, r, i):
                    pe.wait_ge(h_u, N_H * c + i)
                    mm(HZ[:, 0:P], W1[:, :], kv[r][:, 0:P], True, False)

                def h_zg(c, r, i):
                    pe.wait_ge(h_g, N_H * c + i)
                    mm(HZ[:, 0:P], gH[(i - 1) % 2][:, :], G[r][:, :], False, True).then_inc(h_z, 1)

                def h_yc(c, i):
                    if i == 0:
                        pe.wait_ge(h_b1, 2 * c + 2)
                        pe.wait_ge(l_GaM, 2 * c + 2)
                        pe.wait_ge(l_erow, 4 * c + 4)
                        mm(HY[:, 0:P], erowL[2][:, :], GaL[1][:, :], True, False)
                    else:
                        pe.wait_ge(h_GaM, (N_H - 1) * c + i)
                        pe.wait_ge(h_GeM, (N_H - 1) * c + i)
                        pe.wait_ge(h_erow, N_H * c + i)
                        mm(HY[:, 0:P], erowH[(i - 1) % 2][:, :], GaH[:, :], True, False)

                def h_yb(c, i):
                    pe.wait_ge(h_a, N_H * c + i + 1)
                    if i == 0:
                        pe.wait_ge(h_W2, 3 * c + 3)
                    mm(HY[:, 0:P], W2[:, :], aH[:, :], False, True).then_inc(h_y, 1)

                def h_Ta_(c, i):
                    pe.wait_ge(h_a, N_H * c + i + 1)
                    if i == 0:
                        pe.wait_ge(h_W2, 3 * c + 3)
                    else:
                        pe.wait_ge(h_erow, N_H * c + i)
                    pe.transpose(HG[:, 0:P], aH[:, :], ident[:, :]).then_inc(h_Ta, 1)

                def h_Tt_(c, i):
                    pe.wait_ge(h_t, N_H * c + i + 1)
                    pe.transpose(HZ[:, P:2 * P], tH[:, :], ident[:, :]).then_inc(h_Tt, 1)

                def h_fc(c, i):
                    if i == 0:
                        pe.wait_ge(h_W1, c + 1)
                        pe.wait_ge(l_GeM, 2 * c + 2)
                        pe.wait_ge(l_arow, 2 * c + 2)
                        mm(HF[:, 0:P], GeL[1][:, :], arowL[1][:, 0:P], True, False)
                    else:
                        pe.wait_ge(h_g, N_H * c + i)
                        pe.wait_ge(h_GeM, (N_H - 1) * c + i)
                        pe.wait_ge(h_arow, N_H * c + i)
                        mm(HF[:, 0:P], GeH[:, :], arowH[(i - 1) % 2][:, 0:P], True, False)

                def h_fb(c, i):
                    pe.wait_ge(h_e, N_H * c + i + 1)
                    mm(HF[:, 0:P], eH[:, :], W2T[:, :], False, True).then_inc(h_f, 1)

                def h_grams(c, i):
                    pe.wait_ge(h_e, N_H * c + i + 1)
                    mm(HY[:, 0:P], aH[:, :], aH[:, :], True, True)
                    mm(HY[:, P:2 * P], eH[:, :], eH[:, :], True, True).then_inc(h_gram, 1)

                def h_etr_(c, i):
                    pe.wait_ge(h_e, N_H * c + i + 1)
                    pe.wait_ge(h_arow, N_H * c + i + 1)
                    pe.transpose(HG[:, 0:P], eH[:, :], ident[:, :]).then_inc(h_etr, 1)

                def h_upd1(c, r):
                    pe.wait_ge(h_g, N_H * c + N_H)
                    mm(HF[:, 0:P], krow[r][:, :], gH[0][:, :], True, True).then_inc(h_U1, 1)

                def h_upd1b(c):
                    pe.wait_ge(h_g, N_H * c + N_H)
                    pe.wait_ge(h_e, N_H * c + N_H)
                    mm(HY[:, 0:1], gH[0][:, :], ones[:, 0:1], True, True).then_inc(h_U1b, 1)

                def h_upd2(c):
                    pe.wait_ge(h_arow, N_H * c + N_H)
                    pe.wait_ge(h_erow, N_H * c + N_H)
                    mm(HG[:, 0:P], arowH[0][:, 0:P], erowH[0][:, :], True, True)
                    mm(HG[:, P:2 * P + 1], erowH[0][:, :], arowH[0][:, :], True, True).then_inc(h_U2, 1)

                q_proj(0)
                pe.wait_ge(q_kvc, 1)
                q_gram(0)
                pe.wait_ge(q_G, 1)
                q_proj(1)
                pe.wait_ge(q_kvc, 2)
                q_gram(1)
                l_z0(0, 0, first=True)
                l_gram_(0, 0)
                l_y0(0, first=True)
                l_rows(0, 0)
                l_etr_a(0, 0)
                l_y_again(0, 0)
                pe.wait_ge(q_G, 2)
                l_fb(0, 0)
                l_etr_b(0, 0)
                l_ee(0, 0)
                l_z1(0, 0)
                l_gram_(0, 1)
                l_y1(0)
                l_rows(0, 1)
                l_etr_a(0, 1)
                l_fc(0)
                l_y_again(0, 1)
                l_fb(0, 1)
                l_etr_b(0, 1)
                l_ee(0, 1)

                with pe.Fori(0, CH // RING) as ring:
                    for r in range(RING):
                        c = ring * RING + r
                        m, s = c + 1, (r + 1) % RING
                        h_z0(c, r)
                        h_yc(c, 0)
                        l_upd1(m, s)
                        l_upd2(m)
                        h_Ta_(c, 0)
                        l_z0(m, s)
                        h_yb(c, 0)
                        h_Tt_(c, 0)
                        pe.wait_ge(l_b1, 2 * m + 2)
                        q_proj(c + 2)
                        l_gram_(m, 0)
                        l_y0(m)
                        h_fc(c, 0)
                        h_fb(c, 0)
                        h_etr_(c, 0)
                        h_grams(c, 0)
                        l_etr_a(m, 0)
                        h_zb(c, r, 1)
                        l_rows(m, 0)
                        h_zg(c, r, 1)
                        l_y_again(m, 0)
                        h_yc(c, 1)
                        h_fc(c, 1)
                        h_yb(c, 1)
                        h_Ta_(c, 1)
                        l_etr_b(m, 0)
                        l_fb(m, 0)
                        l_ee(m, 0)
                        h_Tt_(c, 1)
                        h_fb(c, 1)
                        l_z1(m, s)
                        h_grams(c, 1)
                        h_etr_(c, 1)
                        h_zb(c, r, 2)
                        l_gram_(m, 1)
                        h_zg(c, r, 2)
                        pe.wait_ge(l_g, 2 * m + 1)
                        pe.wait_ge(q_kvc, c + 3)
                        q_gram((r + 2) % RING)
                        l_y1(m)
                        l_rows(m, 1)
                        h_yc(c, 2)
                        h_Ta_(c, 2)
                        h_yb(c, 2)
                        l_etr_a(m, 1)
                        h_Tt_(c, 2)
                        h_fc(c, 2)
                        l_y_again(m, 1)
                        h_fb(c, 2)
                        h_etr_(c, 2)
                        l_fc(m)
                        l_etr_b(m, 1)
                        l_fb(m, 1)
                        l_ee(m, 1)
                        h_upd1(c, r)
                        h_upd1b(c)
                        h_upd2(c)

            @blk.scalar
            def _(act):
                def q_copy(q, r):
                    act.wait_ge(q_kv, q + 1)
                    nc.scalar.copy(kv[r][:, :], LD[:, 0:2 * P]).then_inc(q_kvc, 1)

                def q_rows(q, r):
                    act.wait_ge(q_kg, q + 1)
                    nc.scalar.copy(krow[r][:, :], LD[:, 2 * P:3 * P]).then_inc(q_krow, 1)

                def l_at(m, j):
                    if j == 0:
                        act.wait_ge(l_b1, 2 * m + 2)
                    act.wait_ge(l_z, 2 * m + j + 1)
                    nc.scalar.activation(aL[:, :], LA[:, 0:P], ACT.Silu, bias=b1L[:, 0:1]).then_inc(l_a, 1)
                    nc.scalar.activation(tL[:, :], LA[:, 0:P], ACT.Tanh, bias=b1hL[:, 0:1], scale=0.5).then_inc(l_t, 1)

                def l_arow_(m, j):
                    act.wait_ge(l_T, 2 * m + j + 1)
                    nc.scalar.copy(arowL[j][:, 0:P], LBb[:, 0:P]).then_inc(l_arow, 1)

                def l_erow_(m, n):
                    act.wait_ge(l_etr, 4 * m + n + 1)
                    nc.scalar.copy(erowL[2 if n == 3 else n % 2][:, :], LAb[:, 0:P]).then_inc(l_erow, 1)

                def h_at(c, i):
                    if i == 0:
                        act.wait_ge(h_b1, 2 * c + 2)
                    act.wait_ge(h_z, N_H * c + i + 1)
                    nc.scalar.activation(aH[:, :], HZ[:, 0:P], ACT.Silu, bias=b1c[:, 0:1]).then_inc(h_a, 1)
                    nc.scalar.activation(tH[:, :], HZ[:, 0:P], ACT.Tanh, bias=b1h[:, 0:1], scale=0.5).then_inc(h_t, 1)

                def h_arow_(c, i):
                    act.wait_ge(h_Ta, N_H * c + i + 1)
                    nc.scalar.copy(arowH[i % 2][:, 0:P], HG[:, 0:P]).then_inc(h_arow, 1)

                def h_erow_(c, i):
                    if i == 0:
                        act.wait_ge(chk_done, c + 1)
                    act.wait_ge(h_etr, N_H * c + i + 1)
                    nc.scalar.copy(erowH[i % 2][:, :], HG[:, 0:P]).then_inc(h_erow, 1)

                nc.scalar.preload_act_table_set("silu_and_others")
                q_copy(0, 0)
                q_rows(0, 0)
                q_copy(1, 1)
                q_rows(1, 1)
                l_at(0, 0)
                l_arow_(0, 0)
                l_erow_(0, 0)
                l_erow_(0, 1)
                l_at(0, 1)
                l_arow_(0, 1)
                l_erow_(0, 2)
                l_erow_(0, 3)
                with act.Fori(0, CH // RING) as ring:
                    for r in range(RING):
                        c = ring * RING + r
                        m, t = c + 1, (r + 2) % RING
                        h_at(c, 0)
                        h_arow_(c, 0)
                        l_at(m, 0)
                        q_copy(c + 2, t)
                        h_erow_(c, 0)
                        l_erow_(m, 0)
                        l_arow_(m, 0)
                        h_at(c, 1)
                        h_arow_(c, 1)
                        l_erow_(m, 1)
                        l_at(m, 1)
                        h_erow_(c, 1)
                        h_at(c, 2)
                        q_rows(c + 2, t)
                        h_arow_(c, 2)
                        l_arow_(m, 1)
                        l_erow_(m, 2)
                        h_erow_(c, 2)
                        l_erow_(m, 3)

            @blk.vector
            def _(dve):
                def stt(dst, a, s, b, o0, o1):
                    return dve.scalar_tensor_tensor(out=dst, in0=a, scalar=s, in1=b, op0=o0, op1=o1)

                def q_G_(q, r):
                    dve.wait_ge(q_krow, q + 1)
                    stt(G[r][:, :], LD[:, 3 * P:4 * P], 1.0, mkh[:, :], ALU.add, ALU.mult).then_inc(q_G, 1)

                def l_new1(m):
                    dve.wait_ge(l_U1, m)
                    dve.wait_ge(h_W1, m)
                    dve.wait_ge(h_b1, 2 * m)
                    stt(W1L[:, :], LD[:, 0:P], -KAPPA / 2, W1[:, :], ALU.mult, ALU.add).then_inc(l_W1, 1)
                    stt(b1L[:, :], LD[:, P:P + 1], -KAPPA / 2, b1c[:, :], ALU.mult, ALU.add).then_inc(l_b1, 1)
                    stt(b1hL[:, :], LD[:, P:P + 1], -KAPPA / 4, b1h[:, :], ALU.mult, ALU.add).then_inc(l_b1, 1)

                def l_new2(m):
                    dve.wait_ge(l_U2, m)
                    dve.wait_ge(h_W2, 3 * m)
                    stt(W2L[:, :], LB[:, 0:P], -KAPPA, W2[:, :], ALU.mult, ALU.add).then_inc(l_W2, 1)
                    stt(W2TL[:, :], LB[:, P:2 * P], -KAPPA, W2T[:, :], ALU.mult, ALU.add).then_inc(l_W2, 1)
                    stt(b2L[:, :], LB[:, 2 * P:2 * P + 1], -KAPPA, b2c[:, :], ALU.mult, ALU.add).then_inc(l_W2, 1)

                def l_Ga(m, j):
                    dve.wait_ge(l_gram, 2 * m + j + 1)
                    stt(GaL[j][:, :], LB[:, 0:P], 1.0, mk[:, :], ALU.add, ALU.mult).then_inc(l_GaM, 1)

                def l_e1(m, r, j):
                    if j == 0:
                        dve.wait_ge(l_W2, 3 * m + 3)
                    dve.wait_ge(l_ya, 2 * m + j + 1)
                    stt(eL[:, :], LC[:, 0:P], b2L[:, 0:1], kv[r][:, P:2 * P], ALU.add, ALU.subtract).then_inc(l_ea, 1)

                def l_e2(m, r, j):
                    dve.wait_ge(l_yb, 2 * m + j + 1)
                    stt(eL[:, :], LC[:, 0:P], b2L[:, 0:1], kv[r][:, P:2 * P], ALU.add, ALU.subtract).then_inc(l_eb, 1)

                def l_u_(m, j):
                    dve.wait_ge(l_arow, 2 * m + j + 1)
                    stt(uL[:, :], arowL[j][:, 0:P], -1.0, LBb[:, P:2 * P], ALU.add, ALU.mult).then_inc(l_u, 1)

                def l_sp_(m, j):
                    dve.wait_ge(l_u, 2 * m + j + 1)
                    stt(spL[:, :], arowL[j][:, 0:P], 1.0, uL[:, :], ALU.add, ALU.subtract).then_inc(l_sp, 1)

                def l_g_(m, j):
                    dve.wait_ge(l_sp, 2 * m + j + 1)
                    dve.wait_ge(l_f, 2 * m + j + 1)
                    dve.tensor_tensor(gL[j][:, :], LD[:, 0:P], spL[:, :], ALU.mult).then_inc(l_g, 1)

                def l_Ge(m, j):
                    dve.wait_ge(l_gE, 2 * m + j + 1)
                    dve.tensor_tensor(GeL[j][:, :], LC[:, 0:P], mk[:, :], ALU.mult).then_inc(l_GeM, 1)

                def h_Ga(c, i):
                    dve.wait_ge(h_gram, (N_H - 1) * c + i + 1)
                    stt(GaH[:, :], HY[:, 0:P], 1.0, mk[:, :], ALU.add, ALU.mult).then_inc(h_GaM, 1)

                def h_e_(c, r, i):
                    if i == 0:
                        dve.wait_ge(h_W2, 3 * c + 3)
                    dve.wait_ge(h_y, N_H * c + i + 1)
                    stt(eH[:, :], HY[:, 0:P], b2c[:, 0:1], kv[r][:, P:2 * P], ALU.add, ALU.subtract).then_inc(h_e, 1)

                def h_u_(c, i):
                    dve.wait_ge(h_arow, N_H * c + i + 1)
                    dve.wait_ge(h_Tt, N_H * c + i + 1)
                    stt(uH[:, :], arowH[i % 2][:, 0:P], -1.0, HZ[:, P:2 * P], ALU.add, ALU.mult).then_inc(h_u, 1)

                def h_sp_(c, i):
                    dve.wait_ge(h_u, N_H * c + i + 1)
                    stt(spH[:, :], arowH[i % 2][:, 0:P], 1.0, uH[:, :], ALU.add, ALU.subtract).then_inc(h_sp, 1)

                def h_Ge(c, i):
                    dve.wait_ge(h_gram, (N_H - 1) * c + i + 1)
                    dve.tensor_tensor(GeH[:, :], HY[:, P:2 * P], mk[:, :], ALU.mult).then_inc(h_GeM, 1)

                def h_g_(c, i):
                    if i == 0:
                        dve.wait_ge(chk_done, c + 1)
                    dve.wait_ge(h_sp, N_H * c + i + 1)
                    dve.wait_ge(h_f, N_H * c + i + 1)
                    dve.tensor_tensor(gH[i % 2][:, :], HF[:, 0:P], spH[:, :], ALU.mult).then_inc(h_g, 1)

                def h_new1(c):
                    dve.wait_ge(h_U1, c + 1)
                    stt(W1[:, :], HF[:, 0:P], -KAPPA / 2, W1[:, :], ALU.mult, ALU.add).then_inc(h_W1, 1)
                    dve.wait_ge(h_U1b, c + 1)
                    stt(b1c[:, :], HY[:, 0:1], -KAPPA / 2, b1c[:, :], ALU.mult, ALU.add).then_inc(h_b1, 1)
                    stt(b1h[:, :], HY[:, 0:1], -KAPPA / 4, b1h[:, :], ALU.mult, ALU.add).then_inc(h_b1, 1)

                def h_new2(c):
                    dve.wait_ge(h_U2, c + 1)
                    for w, u in ((W2[:, :], HG[:, 0:P]), (W2T[:, :], HG[:, P:2 * P]), (b2c[:, :], HG[:, 2 * P:2 * P + 1])):
                        stt(w, u, -KAPPA, w, ALU.mult, ALU.add).then_inc(h_W2, 1)

                dve.tensor_copy(W1L[:, :], W1[:, :]).then_inc(l_W1, 1)
                for dst, src in ((b1L, b1c), (b1hL, b1h)):
                    dve.tensor_copy(dst[:, :], src[:, :]).then_inc(l_b1, 1)
                for dst, src in ((W2L, W2), (W2TL, W2T), (b2L, b2c)):
                    dve.tensor_copy(dst[:, :], src[:, :]).then_inc(l_W2, 1)
                dve.sem_inc(h_W1, 1)
                dve.sem_inc(h_b1, 2)
                dve.sem_inc(h_W2, 3)
                q_G_(0, 0)
                q_G_(1, 1)
                for j in range(2):
                    l_Ga(0, j)
                    l_e1(0, 0, j)
                    l_u_(0, j)
                    l_sp_(0, j)
                    l_e2(0, 0, j)
                    l_g_(0, j)
                    l_Ge(0, j)
                with dve.Fori(0, CH // RING) as ring:
                    for r in range(RING):
                        c = ring * RING + r
                        m, s = c + 1, (r + 1) % RING
                        l_new1(m)
                        l_new2(m)
                        h_e_(c, r, 0)
                        h_u_(c, 0)
                        h_sp_(c, 0)
                        l_e1(m, s, 0)
                        l_Ga(m, 0)
                        h_g_(c, 0)
                        h_Ga(c, 0)
                        h_Ge(c, 0)
                        l_u_(m, 0)
                        l_e2(m, s, 0)
                        l_sp_(m, 0)
                        h_e_(c, r, 1)
                        l_g_(m, 0)
                        h_u_(c, 1)
                        h_sp_(c, 1)
                        l_Ge(m, 0)
                        h_g_(c, 1)
                        h_Ga(c, 1)
                        l_Ga(m, 1)
                        h_Ge(c, 1)
                        l_e1(m, s, 1)
                        q_G_(c + 2, (r + 2) % RING)
                        h_e_(c, r, 2)
                        h_u_(c, 2)
                        l_u_(m, 1)
                        h_sp_(c, 2)
                        l_e2(m, s, 1)
                        h_g_(c, 2)
                        l_sp_(m, 1)
                        l_g_(m, 1)
                        h_new1(c)
                        l_Ge(m, 1)
                        h_new2(c)

            @blk.gpsimd
            def _(pool):
                def q_cast_(q, r):
                    pool.wait_ge(q_G, q + 1)
                    pool.tensor_tensor(kTb[r][:, :], kv[r][:, 0:P], ones[:, :], ALU.mult)
                    pool.tensor_tensor(Gb[r][:, :], G[r][:, :], ones[:, :], ALU.mult)
                    pool.tensor_tensor(krowb[r][:, :], krow[r][:, :], ones[:, :], ALU.mult).then_inc(q_cast, 1)

                def check(c):
                    pool.wait_ge(chk_step, c * 6 + 1)
                    pool.wait_ge(h_g, N_H * c + N_H)
                    pool.tensor_tensor(chd[:, 0, :], gH[0][:, :], gH[1][:, :], ALU.subtract).then_inc(chk_step, 1)
                    pool.tensor_tensor(chd[:, 1, :], gH[0][:, :], gH[0][:, :], ALU.mult).then_inc(chk_step, 1)
                    pool.wait_ge(h_erow, N_H * c + N_H)
                    pool.tensor_tensor(chd[:, 2, :], erowH[0][:, :], erowH[1][:, :], ALU.subtract).then_inc(chk_step, 1)
                    pool.tensor_tensor(chd[:, 3, :], erowH[0][:, :], erowH[0][:, :], ALU.mult).then_inc(chk_done, 1)
                    pool.wait_ge(chk_step, c * 6 + 4)
                    pool.tensor_tensor(chd[:, 0, :], chd[:, 0, :], chd[:, 0, :], ALU.mult).then_inc(chk_step, 1)
                    pool.tensor_tensor(chd[:, 2, :], chd[:, 2, :], chd[:, 2, :], ALU.mult).then_inc(chk_step, 1)
                    pool.wait_ge(chk_step, c * 6 + 6)
                    pool.wait_ge(chk_done, c + 2)
                    flat = chk[:, :, :].rearrange("p a b -> p (a b)")
                    pool.tensor_tensor(flat, flat, chd[:, :, :].rearrange("p a b -> p (a b)"), ALU.add).then_inc(chk_step, 1)

                nc.gpsimd.memset(arowH[0][:, P:P + 1], 1.0)
                nc.gpsimd.memset(arowL[1][:, P:P + 1], 1.0)
                nc.gpsimd.memset(chk[:, :, :], 0.0).then_inc(chk_step, 1)
                pool.wait_ge(chk_step, 1)
                pool.sem_inc(chk_done, 1)
                q_cast_(0, 0)
                q_cast_(1, 1)
                with pool.Fori(0, CH // RING) as ring:
                    for r in range(RING):
                        c = ring * RING + r
                        q_cast_(c + 2, (r + 2) % RING)
                        check(c)

        sums = psb("sums", [P, 4])
        holds = psb("holds", [P, 4])
        count = psb("count", [1, 1], I32)
        with block() as blk:
            sums_ready, holds_step, total_ready, count_ready = sem("sums_ready"), sem("holds_step"), sem("total_ready"), sem("count_ready")

            @blk.vector
            def _(dve):
                dve.tensor_reduce(sums[:, :], chk[:, :, :], AX_X, ALU.add).then_inc(sums_ready, 1)
                dve.wait_ge(sums_ready, 1)
                for n in range(2):
                    dve.scalar_tensor_tensor(out=holds[:, 2 * n:2 * n + 1], in0=sums[:, 2 * n + 1:2 * n + 2], scalar=TOL * TOL,
                                             in1=sums[:, 2 * n:2 * n + 1], op0=ALU.mult, op1=ALU.is_ge).then_inc(holds_step, 1)
                    dve.tensor_scalar(holds[:, 2 * n + 1:2 * n + 2], sums[:, 2 * n + 1:2 * n + 2], 3e38, None,
                                      ALU.is_le).then_inc(holds_step, 1)
                dve.wait_ge(total_ready, 1)
                dve.tensor_reduce(holds[0:1, 0:1], bank[0][0:1, 0:4], AX_X, ALU.add).then_inc(holds_step, 1)
                dve.wait_ge(holds_step, 5)
                dve.tensor_copy(count[:, :], holds[0:1, 0:1]).then_inc(count_ready, 1)

            @blk.tensor
            def _(pe):
                pe.wait_ge(holds_step, 4)
                pe.matmul(bank[0][0:1, 0:4], ones[:, 0:1], holds[:, :], start=True, stop=True).then_inc(total_ready, 1)

        k4 = psb("k4", [P, 2 * B])
        a4, t4, u4, sp4, e4, g4 = (psb(n, [P, B]) for n in ("a4", "t4", "u4", "sp4", "e4", "g4"))
        gs, es = psb("gs", [P, 1]), psb("es", [P, 1])
        rows4 = psb("rows4", [B, 4, P])
        with block() as blk:
            s_again, w2t_again, w2t_copied = sem("s_again"), sem("w2t_again"), sem("w2t_copied")
            k_step, kc_step, z_step, a_step, t_step = (sem(f"{n}_step") for n in ("k", "kc", "z", "a", "t"))
            y_step, e_step, u_step, sp_step, f_step = (sem(f"{n}_step") for n in ("y", "e", "u", "sp", "f"))
            g_step, r_step, rc_step, U_step, s_step = (sem(f"{n}_step") for n in ("g", "r", "rc", "U", "s"))
            w_step = sem("w_step")

            def holding(eng):
                return eng.value_load(count[0:1, 0:1], min_val=0, max_val=4 * P)

            def steps(eng, body):
                with eng.Fori(0, CH) as c:
                    with eng.Fori(0, STEPS) as j:
                        body(c, j, c * STEPS + j)

            @blk.sync
            def _(sp):
                with sp.If(holding(sp) < 4 * P):
                    for dst, src in ((W1[:, :], w1), (W2[:, :], w2), (b1c[:, :], b1.rearrange("(d o) -> d o", o=1)),
                                     (b2c[:, :], b2.rearrange("(d o) -> d o", o=1))):
                        sp.dma_start(dst, src).then_inc(s_again, 16)

            @blk.tensor
            def _(pe):
                with pe.If(holding(pe) < 4 * P):
                    pe.wait_ge(s_again, 64)
                    pe.transpose(bank[0][:, 0:P], W2[:, :], ident[:, :]).then_inc(w2t_again, 1)

                    def step(c, j, n):
                        h4 = hT[:, c, :].rearrange("p (b t) -> p t b", t=STEPS)[:, j, :]
                        pe.wait_ge(w_step, n * 6 + 6)
                        pe.matmul(bank[0][:, 0:B], wkv[:, 0:D], h4, start=True, stop=True)
                        pe.matmul(bank[0][:, B:2 * B], wkv[:, D:2 * D], h4, start=True, stop=True).then_inc(k_step, 1)
                        pe.wait_ge(kc_step, n + 1)
                        pe.matmul(bank[1][:, 0:B], W1[:, :], k4[:, 0:B], start=True, stop=True).then_inc(z_step, 1)
                        pe.wait_ge(a_step, n + 1)
                        pe.matmul(bank[2][:, 0:B], W2[:, :], a4[:, :], start=True, stop=True).then_inc(y_step, 1)
                        pe.wait_ge(e_step, n + 1)
                        pe.matmul(bank[3][:, 0:B], W2T[:, :], e4[:, :], start=True, stop=True).then_inc(f_step, 1)
                        pe.wait_ge(g_step, n + 1)
                        for m, src in enumerate((k4[:, 0:B], a4[:, :], e4[:, :], g4[:, :])):
                            t = pe.transpose(bank[4][0:B, m * P:(m + 1) * P], src, ident[:, :])
                        t.then_inc(r_step, 1)
                        pe.wait_ge(rc_step, n + 1)
                        kr, ar, er, gr = (rows4[:, m, :] for m in range(4))
                        pe.matmul(bank[5][:, 0:P], kr, gr, start=True, stop=True)
                        pe.matmul(bank[5][:, P:2 * P], ar, er, start=True, stop=True)
                        pe.matmul(bank[5][:, 2 * P:3 * P], er, ar, start=True, stop=True).then_inc(U_step, 1)
                    steps(pe, step)

            @blk.scalar
            def _(act):
                with act.If(holding(act) < 4 * P):
                    def step(c, j, n):
                        act.wait_ge(k_step, n + 1)
                        nc.scalar.copy(k4[:, :], bank[0][:, 0:2 * B]).then_inc(kc_step, 1)
                        act.wait_ge(z_step, n + 1)
                        nc.scalar.activation(a4[:, :], bank[1][:, 0:B], ACT.Silu, bias=b1c[:, 0:1]).then_inc(a_step, 1)
                        nc.scalar.activation(t4[:, :], bank[1][:, 0:B], ACT.Tanh, bias=b1h[:, 0:1],
                                             scale=0.5).then_inc(t_step, 1)
                    steps(act, step)

            @blk.vector
            def _(dve):
                with dve.If(holding(dve) < 4 * P):
                    dve.wait_ge(w2t_again, 1)
                    dve.tensor_copy(W2T[:, :], bank[0][:, 0:P]).then_inc(w2t_copied, 1)
                    dve.tensor_scalar(b1h[:, :], b1c[:, :], 0.5, None, ALU.mult).then_inc(w2t_copied, 1)
                    dve.wait_ge(w2t_copied, 2)
                    dve.sem_inc(w_step, 6)

                    def step(c, j, n):
                        dve.wait_ge(y_step, n + 1)
                        dve.scalar_tensor_tensor(out=e4[:, :], in0=bank[2][:, 0:B], scalar=b2c[:, 0:1], in1=k4[:, B:2 * B],
                                                 op0=ALU.add, op1=ALU.subtract).then_inc(e_step, 1)
                        dve.wait_ge(t_step, n + 1)
                        dve.scalar_tensor_tensor(out=u4[:, :], in0=a4[:, :], scalar=-1.0, in1=t4[:, :],
                                                 op0=ALU.add, op1=ALU.mult).then_inc(u_step, 1)
                        dve.wait_ge(u_step, n + 1)
                        dve.scalar_tensor_tensor(out=sp4[:, :], in0=a4[:, :], scalar=1.0, in1=u4[:, :],
                                                 op0=ALU.add, op1=ALU.subtract).then_inc(sp_step, 1)
                        dve.wait_ge(sp_step, n + 1)
                        dve.wait_ge(f_step, n + 1)
                        dve.tensor_tensor(g4[:, :], bank[3][:, 0:B], sp4[:, :], ALU.mult).then_inc(g_step, 1)
                        dve.wait_ge(r_step, n + 1)
                        dve.tensor_copy(rows4[:, :, :].rearrange("b m d -> b (m d)"), bank[4][0:B, :]).then_inc(rc_step, 1)
                        dve.wait_ge(g_step, n + 1)
                        dve.tensor_reduce(gs[:, :], g4[:, :], AX_X, ALU.add).then_inc(s_step, 1)
                        dve.tensor_reduce(es[:, :], e4[:, :], AX_X, ALU.add).then_inc(s_step, 1)
                        dve.wait_ge(s_step, n * 2 + 2)
                        dve.wait_ge(U_step, n + 1)
                        for w, u, r in ((W1[:, :], bank[5][:, 0:P], -KAPPA / 2), (W2[:, :], bank[5][:, P:2 * P], -KAPPA),
                                        (W2T[:, :], bank[5][:, 2 * P:3 * P], -KAPPA), (b1c[:, :], gs[:, :], -KAPPA / 2),
                                        (b1h[:, :], gs[:, :], -KAPPA / 4), (b2c[:, :], es[:, :], -KAPPA)):
                            dve.scalar_tensor_tensor(out=w, in0=u, scalar=r, in1=w, op0=ALU.mult,
                                                     op1=ALU.add).then_inc(w_step, 1)
                        dve.wait_ge(w_step, n * 6 + 12)
                    steps(dve, step)
        scan_stack.close()

        with ExitStack() as stack, block() as blk:
            psb = phase(stack)
            wz = psb("wz", [P, D])
            diag = psb("diag", [P, D])
            qa = [psb(f"qa{i}", [P, TOK]) for i in range(2)]
            t1 = [psb(f"t1{i}", [P, GRP, D]) for i in range(2)]
            gab = psb("gab", [P, D])
            wz_ready, wz_copied = sem("wz_ready"), sem("wz_copied")
            d_ready, b_ready, gab_ready = sem("d_ready"), sem("b_ready"), sem("gab_ready")
            qz_ready, qa_ready = sem("qz_ready"), sem("qa_ready")
            o_ready, o_used, xg_ready, x1_ready = sem("o_ready"), sem("o_used"), sem("xg_ready"), sem("x1_ready")

            @blk.tensor
            def _(pe):
                pe.matmul(bank[7][:, 0:D], wqT[:, :], W1[:, :], start=True, stop=True).then_inc(wz_ready, 1)
                pe.wait_ge(d_ready, 1)
                pe.matmul(bank[6][:, 0:D], ones[:, :], diag[:, :], start=True, stop=True).then_inc(b_ready, 1)

                def hidden(g, k):
                    pe.wait_ge(qa_ready, g + 1)
                    pe.matmul(bank[2 + k][:, :], wz[:, :], hT[:, bass.ts(g, GRP), :].rearrange("p c t -> p (c t)"),
                              start=True, stop=True).then_inc(qz_ready, 1)

                def result(g, k):
                    pe.wait_ge(qa_ready, g + 3)
                    pe.wait_ge(o_used, g + 1)
                    for j in range(GRP):
                        mm = pe.matmul(bank[4 + k][:, j * P:(j + 1) * P], qa[k][:, j * P:(j + 1) * P], W2[:, :],
                                       start=True, stop=True)
                    mm.then_inc(o_ready, 1)

                pe.wait_ge(wz_copied, 1)
                hidden(0, 0)
                with pe.Fori(0, NG // 2 - 1) as pair:
                    g = pair * 2
                    hidden(g + 1, 1)
                    result(g, 0)
                    hidden(g + 2, 0)
                    result(g + 1, 1)
                hidden(NG - 1, 1)
                result(NG - 2, 0)
                result(NG - 1, 1)

            @blk.scalar
            def _(act):
                act.wait_ge(wz_ready, 1)
                nc.scalar.copy(wz[:, :], bank[7][:, 0:D]).then_inc(wz_copied, 1)
                nc.scalar.preload_act_table_set("silu_and_others")
                act.sem_inc(qa_ready, 2)
                act.sem_inc(o_ready, 2)
                with act.Fori(0, NG // 2) as pair:
                    g = pair * 2
                    for k in range(2):
                        act.wait_ge(qz_ready, g + k + 1)
                        act.wait_ge(o_ready, g + k + 1)
                        nc.scalar.activation(qa[k][:, :], bank[2 + k][:, :], ACT.Silu, bias=b1c[:, 0:1]).then_inc(qa_ready, 1)

            @blk.vector
            def _(dve):
                dve.tensor_scalar(diag[:, :], ident[:, :], b2c[:, 0:1], None, ALU.mult).then_inc(d_ready, 1)
                dve.sem_inc(o_used, 2)
                dve.wait_ge(b_ready, 1)
                dve.tensor_tensor(gab[:, :], bank[6][:, 0:D], gate[:, 0, :], ALU.mult).then_inc(gab_ready, 1)

                def times_gate(g, k):
                    dve.wait_ge(o_ready, g + 3)
                    dve.wait_ge(x1_ready, g + 1)
                    dve.tensor_tensor(t1[k][:, :, :], bank[4 + k][:, :].rearrange("p (c d) -> p c d", c=GRP),
                                      gate[:, 0, :].unsqueeze(1).broadcast_to([P, GRP, D]), ALU.mult).then_inc(o_used, 1)

                def statistics(g):
                    dve.wait_ge(x1_ready, g + 3)
                    for j in range(GRP):
                        c = g * GRP + j
                        dve.bn_stats(stats[:, c, :], xr[:, c, :])

                times_gate(0, 0)
                with dve.Fori(0, NG // 2 - 1) as pair:
                    g = pair * 2
                    times_gate(g + 1, 1)
                    statistics(g)
                    times_gate(g + 2, 0)
                    statistics(g + 1)
                times_gate(NG - 1, 1)
                statistics(NG - 2)
                statistics(NG - 1)

            @blk.gpsimd
            def _(pool):
                pool.sem_inc(x1_ready, 2)
                pool.wait_ge(gab_ready, 1)
                with pool.Fori(0, NG) as g:
                    xs = xr[:, bass.ts(g, GRP), :]
                    pool.tensor_tensor(xs, xs, gab[:, :].unsqueeze(1).broadcast_to([P, GRP, D]), ALU.add).then_inc(xg_ready, 1)
                pool.wait_ge(xg_ready, NG)
                with pool.Fori(0, NG // 2) as pair:
                    for k in range(2):
                        g = pair * 2 + k
                        pool.wait_ge(o_used, g + 3)
                        xs = xr[:, bass.ts(g, GRP), :]
                        pool.tensor_tensor(xs, t1[k][:, :, :], xs, ALU.add).then_inc(x1_ready, 1)

        with ExitStack() as stack, block() as blk:
            psb = phase(stack)
            gtmp = psb("gtmp", [P, CH, E])
            rank = psb("rank", [P, CH, E])
            cmp = psb("cmp", [P, CH, E, E])
            red = psb("red", [P, CH])
            ln2 = LayerNorm("ln2", 2)
            lg_ready, lg_copied = sem("lg_ready"), sem("lg_copied")
            step, ex_ready = sem("gate_step"), sem("ex_ready")

            @blk.tensor
            def _(pe):
                def route(g):
                    pe.wait_ge(ln2.copied, g + 3)
                    for j in range(GRP):
                        c = g * GRP + j
                        mm = pe.matmul(bank[2][:, c * E:(c + 1) * E], hT[:, c, :], wrT[:, :], start=True, stop=True)
                    return mm

                pe.sem_inc(ln2.tr, 2)
                for g in range(NG):
                    ln2.transpose(pe, g - g % 2, g % 2)
                    if g:
                        route(g - 1)
                route(NG - 1).then_inc(lg_ready, 1)

            @blk.scalar
            def _(act):
                ln2.scalar(act)
                act.wait_ge(lg_ready, 1)
                nc.scalar.copy(logits[:, :, :].rearrange("p c e -> p (c e)"), bank[2][:, 0:CH * E]).then_inc(lg_copied, 1)
                act.wait_ge(step, 2)
                nc.scalar.activation(gates[:, :, :], gtmp[:, :, :], ACT.Exp).then_inc(ex_ready, 1)

            @blk.vector
            def _(dve):
                ln2.vector_stats(dve)
                ln2.vector(dve)
                n = [0]

                def link(ins):
                    ins.then_inc(step, 1)
                    n[0] += 1
                    dve.wait_ge(step, n[0])

                bc = lambda t: t.unsqueeze(2).broadcast_to([P, CH, E])
                dve.wait_ge(lg_copied, 1)
                link(dve.tensor_reduce(red[:, :], logits[:, :, :], AX_X, ALU.max))
                link(dve.tensor_tensor(gtmp[:, :, :], logits[:, :, :], bc(red[:, :]), ALU.subtract))
                mine = logits[:, :, :].unsqueeze(3).broadcast_to([P, CH, E, E])
                other = logits[:, :, :].unsqueeze(2).broadcast_to([P, CH, E, E])
                link(dve.tensor_tensor(cmp[:, :, :, :], other, mine, ALU.is_gt))
                for e in range(1, E):
                    link(dve.tensor_tensor(cmp[:, :, e, 0:e], other[:, :, e, 0:e], mine[:, :, e, 0:e], ALU.is_ge))
                link(dve.tensor_reduce(rank[:, :, :], cmp[:, :, :, :], AX_X, ALU.add))
                dve.wait_ge(ex_ready, 1)
                link(dve.tensor_reduce(red[:, :], gates[:, :, :], AX_X, ALU.add))
                link(dve.reciprocal(red[:, :], red[:, :]))
                link(dve.tensor_tensor(gates[:, :, :], gates[:, :, :], bc(red[:, :]), ALU.mult))
                link(dve.scalar_tensor_tensor(out=gates[:, :, :], in0=rank[:, :, :], scalar=1.5, in1=gates[:, :, :],
                                              op0=ALU.is_lt, op1=ALU.mult))
                rest = gates
                for m in range(3):
                    link(dve.tensor_copy(gparts[:, :, m * E:(m + 1) * E], rest[:, :, :]))
                    if m < 2:
                        link(dve.tensor_tensor(gtmp[:, :, :], rest[:, :, :], gparts[:, :, m * E:(m + 1) * E], ALU.subtract))
                        rest = gtmp

        N_E = E + 1
        N_IT = 2 * N_E
        with ExitStack() as stack, block() as blk:
            psb = phase(stack)
            hx = [psb(f"hx{i}", [P, TOK]) for i in range(2)]
            hhH, hhL = ([psb(f"{n}{i}", [P, FT, TOK], F32R) for i in range(2)] for n in ("hhH", "hhL"))
            hgH, hgL = ([psb(f"{n}{i}", [P, TOK], F32R) for i in range(2)] for n in ("hgH", "hgL"))
            gst = psb("gst", [P, GRP, 3 * E], BF16)
            gT = [psb(f"gT{i}", [3 * E, TOK], BF16) for i in range(2)]
            gbs = [psb(f"gbs{i}", [P, TOK]) for i in range(2)]
            part = [psb(f"part{i}", [P, TOK]) for i in range(2)]
            acc = [psb(f"acc{i}", [P, TOK]) for i in range(2)]
            fo = [psb(f"fo{i}", [P, GRP, D]) for i in range(2)]
            gst_ready, gt_ready, gT_ready = sem("gst_ready"), sem("gt_ready"), sem("gT_ready")
            f_ready, fo_ready, fin_ready = sem("f_ready"), sem("fo_ready"), sem("fin_ready")
            hg_ready = sem("hg_ready")
            u_ready, x_ready, hi_ready, h_ready = sem("up_ready"), sem("gelu_ready"), sem("hi_ready"), sem("hid_ready")
            y_ready, p_ready = sem("down_ready"), sem("part_ready")
            gb_ready, gbs_ready, acc_ready = sem("gb_ready"), sem("gbs_ready"), sem("acc_ready")
            s_out = sem("s_out")
            X0, GBS0, H0, P0, Y0, FO0, ACC0 = 4, 1, 2, 2, 2, 1, 2
            HB, YB, GB, TB = (0, 1, 2, 3), (4, 5), 6, 7
            out_v = [out[b].rearrange("(c t) d -> t c d", t=STEPS) for b in range(B)]

            def where(p, i):
                k, e = i // N_E, i % N_E
                g = p * 2 + k
                return g, k, e, p * N_IT + i, g * E + e - 1

            def run(eng, start, step, end):
                start()
                for i in range(2):
                    step(0, i, True, False)
                with eng.Fori(0, NG // 2 - 1) as p:
                    for i in range(2, N_IT):
                        step(p, i, False, False)
                    for i in range(2):
                        step(p + 1, i, False, False)
                for i in range(2, N_IT):
                    step(NG // 2 - 1, i, False, True)
                end()

            @blk.tensor
            def _(pe):
                def up(p, i):
                    g, k, e, t, _ = where(p + i // N_IT, i % N_IT)
                    pe.wait_ge(hg_ready, 2 * g + 2)
                    for n in range(FT):
                        pe.wait_ge(x_ready, FT * (t - 1) + n + 1 + X0)
                        for m, (w, h) in enumerate(((w1H, hgH), (w1H, hgL), (w1L, hgH))):
                            mm = pe.matmul(bank[HB[n]][:, :], w[:, e - 1, n, :] if e else w[:, E, n, :], h[k][:, :],
                                           start=(m == 0), stop=(m == 2))
                        mm.then_inc(u_ready, 1)

                def gates_out(g, k, e, r):
                    pe.wait_ge(gT_ready, g + 1)
                    pe.wait_ge(gbs_ready, r + GBS0)
                    pe.matmul(bank[GB][:, :], sel[:, e - 1, :], gT[k][:, :], start=True, stop=True).then_inc(gb_ready, 1)

                def down(i, e, t):
                    pe.wait_ge(p_ready, t - 1 + P0)
                    for n in range(FT):
                        pe.wait_ge(h_ready, FT * t + n + 1 + H0)
                        for m, (w, h) in enumerate(((w2H, hhH), (w2H, hhL), (w2L, hhH))):
                            mm = pe.matmul(bank[YB[i % 2]][:, :], w[:, e - 1, n, :] if e else w[:, E, n, :], h[i % 2][:, n, :],
                                           start=(n == 0 and m == 0), stop=(n == FT - 1 and m == 2))
                    mm.then_inc(y_ready, 1)

                def gates_turn(g):
                    pe.wait_ge(gst_ready, g + 1)
                    for j in range(GRP):
                        tr = pe.transpose(bankb[TB][0:3 * E, j * P:(j + 1) * P], gst[:, j, :], identb[:, :])
                    tr.then_inc(gt_ready, 1)

                def result_turn(g, k):
                    pe.wait_ge(acc_ready, E * (g + 1) + ACC0)
                    for j in range(GRP):
                        tr = pe.transpose(bank[TB][:, j * P:(j + 1) * P], acc[k][:, j * P:(j + 1) * P], ident[:, :])
                    tr.then_inc(f_ready, 1)

                def start():
                    pe.sem_inc(y_ready, Y0)
                    gates_turn(0)
                    up(0, 0)

                def step(p, i, first, last):
                    g, k, e, t, r = where(p, i)
                    if not (last and i == N_IT - 1):
                        up(p, i + 1)
                    if e:
                        gates_out(g, k, e, r)
                    down(i, e, t)
                    if e == 1 and not first:
                        pe.wait_ge(gT_ready, g + 1)
                        result_turn(g - 1, 1 - k)
                    if e == 5 and not (last and k == 1):
                        pe.wait_ge(fo_ready, g + FO0)
                        gates_turn(g + 1)

                run(pe, start, step, lambda: result_turn(NG - 1, 1))

            @blk.scalar
            def _(act):
                def gelu(p, i):
                    _, k, e, t, _ = where(p + i // N_IT, i % N_IT)
                    for n in range(FT):
                        act.wait_ge(u_ready, FT * t + n + 1)
                        act.wait_ge(h_ready, FT * t + n - 1 + H0)
                        nc.scalar.activation(hx[n % 2][:, :], bank[HB[n]][:, :], ACT.Gelu_apprx_tanh,
                                             bias=eb1[:, (e - 1) % N_E, n:n + 1]).then_inc(x_ready, 1)

                def gates_turned(g, k):
                    act.wait_ge(gt_ready, g + 1)
                    nc.scalar.copy(gT[k][:, :], bankb[TB][0:3 * E, 0:TOK]).then_inc(gT_ready, 1)

                def start():
                    nc.scalar.preload_act_table_set("gelu_apprx_tanh_and_others")
                    act.sem_inc(x_ready, X0)
                    act.sem_inc(gbs_ready, GBS0)
                    gates_turned(0, 0)
                    gelu(0, 0)

                def step(p, i, first, last):
                    g, k, e, t, r = where(p, i)
                    if not (last and i == N_IT - 1):
                        gelu(p, i + 1)
                    if e:
                        act.wait_ge(gb_ready, r + 1)
                        act.wait_ge(p_ready, t - 1 + P0)
                        nc.scalar.copy(gbs[(e - 1) % 2][:, :], bank[GB][:, :]).then_inc(gbs_ready, 1)
                    if e == 5 and not (last and k == 1):
                        gates_turned(g + 1, 1 - k)

                run(act, start, step, lambda: None)

            @blk.vector
            def _(dve):
                def prepare(g, k):
                    if not (isinstance(g, int) and g == 0):
                        dve.wait_ge(gt_ready, g)
                    dve.tensor_copy(gst[:, :, :], gparts[:, bass.ts(g, GRP), :]).then_inc(gst_ready, 1)
                    hg = hT[:, bass.ts(g, GRP), :].rearrange("p c t -> p (c t)")
                    dve.tensor_copy(hgH[k][:, :], hg).then_inc(hg_ready, 1)
                    dve.wait_ge(hg_ready, 2 * g + 1)
                    dve.tensor_tensor(hgL[k][:, :], hg, hgH[k][:, :].bitcast(F32), ALU.subtract).then_inc(hg_ready, 1)

                def split(p, i):
                    _, _, _, t, _ = where(p + i // N_IT, i % N_IT)
                    dve.wait_ge(y_ready, t - 1 + Y0)
                    for n in range(FT):
                        dve.wait_ge(x_ready, FT * t + n + 1 + X0)
                        dve.tensor_copy(hhH[i % 2][:, n, :], hx[n % 2][:, :]).then_inc(hi_ready, 1)
                        dve.wait_ge(hi_ready, FT * t + n + 1)
                        dve.tensor_tensor(hhL[i % 2][:, n, :], hx[n % 2][:, :], hhH[i % 2][:, n, :].bitcast(F32),
                                          ALU.subtract).then_inc(h_ready, 1)

                def combine(i, k, e, t, r):
                    dve.wait_ge(y_ready, t + 1 + Y0)
                    y = bank[YB[i % 2]][:, :]
                    if e == 0:
                        dve.tensor_scalar(acc[k][:, :], y, bs2T[:, 0:1], None, ALU.add).then_inc(p_ready, 1)
                    else:
                        dve.wait_ge(gbs_ready, r + 1 + GBS0)
                        dve.wait_ge(acc_ready, r - 1 + ACC0)
                        dve.scalar_tensor_tensor(out=part[(e - 1) % 2][:, :], in0=y, scalar=b2T[:, e - 1:e],
                                                 in1=gbs[(e - 1) % 2][:, :], op0=ALU.add, op1=ALU.mult).then_inc(p_ready, 1)

                def finish(g, k):
                    dve.wait_ge(f_ready, g + 1)
                    dve.tensor_tensor(fo[k][:, :, :], bank[TB][:, :].rearrange("p (c d) -> p c d", c=GRP),
                                      gate[:, 1, :].unsqueeze(1).broadcast_to([P, GRP, D]), ALU.mult).then_inc(fo_ready, 1)

                def start():
                    dve.sem_inc(h_ready, H0)
                    dve.sem_inc(p_ready, P0)
                    dve.sem_inc(fo_ready, FO0)
                    prepare(0, 0)
                    dve.wait_ge(y_ready, 1)
                    split(0, 0)

                def step(p, i, first, last):
                    g, k, e, t, r = where(p, i)
                    if not (last and i == N_IT - 1):
                        split(p, i + 1)
                    combine(i, k, e, t, r)
                    if e == 1 and not first:
                        finish(g - 1, 1 - k)
                    if e == 3 and not (last and k == 1):
                        prepare(g + 1, 1 - k)

                run(dve, start, step, lambda: finish(NG - 1, 1))

            @blk.gpsimd
            def _(pool):
                def finish(g, k):
                    pool.wait_ge(fo_ready, g + 1 + FO0)
                    xs = xr[:, bass.ts(g, GRP), :]
                    pool.tensor_tensor(xs, fo[k][:, :, :], xs, ALU.add).then_inc(fin_ready, 1)

                def step(p, i, first, last):
                    g, k, e, t, r = where(p, i)
                    if e:
                        pool.wait_ge(p_ready, t + 1 + P0)
                        pool.wait_ge(acc_ready, r + ACC0)
                        pool.tensor_tensor(acc[k][:, :], acc[k][:, :], part[(e - 1) % 2][:, :], ALU.add).then_inc(acc_ready, 1)
                    if e == 1 and not first:
                        finish(g - 1, 1 - k)

                run(pool, lambda: pool.sem_inc(acc_ready, ACC0), step, lambda: finish(NG - 1, 1))

            @blk.sync
            def _(sp):
                with sp.Fori(0, NG) as g:
                    sp.wait_ge(fin_ready, g + 1)
                    for b in range(B):
                        sp.dma_start(out_v[b][:, bass.ts(g, GRP), :],
                                     xr[b * STEPS:(b + 1) * STEPS, bass.ts(g, GRP), :]).then_inc(s_out, 16)
                sp.wait_ge(s_out, 16 * B * NG)


_INS = ['L0_attn_x', 'L0_attn_W_Q', 'L0_attn_W_KV', 'L0_attn_W1', 'L0_attn_b1', 'L0_attn_W2', 'L0_attn_b2',
        'L0_ffn_w_router', 'L0_ffn_W1', 'L0_ffn_b1', 'L0_ffn_W2', 'L0_ffn_b2', 'L0_ffn_Ws1', 'L0_ffn_bs1',
        'L0_ffn_Ws2', 'L0_ffn_bs2', 'L0_c', 'L0_wmod']


def kernel(**inputs):
    import numpy as _np
    import concourse.bacc as _bacc
    from concourse import mybir as _mybir
    from concourse.bass_utils import run_bass_kernel_spmd as _run

    nc = _bacc.Bacc("TRN2", target_bir_lowering=False, num_devices=1)
    arrays, args = {}, []
    step = _np.arange(P) % STEPS
    given = {name: _np.ascontiguousarray(inputs[name]) for name in _INS}
    given["ident"] = _np.eye(P, dtype=_np.float32)
    given["before"] = (step[:, None] < step[None, :]).astype(_np.float32)
    for name, a in given.items():
        arrays[f"in_{name}_dram"] = a
        args.append(nc.dram_tensor(f"in_{name}_dram", a.shape, _mybir.dt.from_np(a.dtype), kind="ExternalInput").ap())
    out = nc.dram_tensor("out_0_dram", (B, S, D), F32, kind="ExternalOutput").ap()
    program(nc, *args, out)
    r = _run(nc, [arrays], core_ids=[0])
    return r.results[0]["out_0_dram"]
```
